# Optimizing a Trainium2 kernel written in Bass

```python
import numpy as np
import jax
import jax.numpy as jnp

def _softmax(x, axis=-1):
    return jax.nn.softmax(x, axis=axis)

def _gelu(x):
    return jax.nn.gelu(x, approximate=True)

def _silu(x):
    return jax.nn.silu(x)

def _sigmoid(x):
    return jax.nn.sigmoid(x)

def _layernorm(x, axis=-1, eps=1e-05):
    m = jnp.mean(x, axis=axis, keepdims=True)
    v = jnp.var(x, axis=axis, keepdims=True)
    return (x - m) / jnp.sqrt(v + eps)

def _scatter_add(tgt, idx, src, axis=0):
    return tgt.at[idx].add(src)

def _segment_sum(src, seg, n):
    return jax.ops.segment_sum(src, seg, n)
kernel_name = 'mk_gnn_ffn_d2_gnn_r8_f0274a'

def setup_inputs(seed: int=0):
    np.random.seed(seed)
    _w = jnp.asarray

    def _rec_inputs():
        import jax
        import jax.numpy as jnp
        _gk = jax.random.key(seed)
        x = -0.0002117 + 1 * jax.random.normal(jax.random.fold_in(_gk, 1), (6250, 256), jnp.float32)
        src = jax.random.randint(jax.random.fold_in(_gk, 2), (200000,), 0, 6250, jnp.int32)
        dst = jax.random.randint(jax.random.fold_in(_gk, 3), (200000,), 0, 6250, jnp.int32)
        _o = jnp.argsort(dst, stable=True)
        src = src[_o]
        dst = dst[_o]
        edge_attr_8 = -0.00019784 + 0.999804 * jax.random.normal(jax.random.fold_in(_gk, 12), (200000, 8), jnp.float32)
        edge_weight = jax.random.uniform(jax.random.fold_in(_gk, 14), (200000,), jnp.float32, 0.0, 0.999998)
        node_vec = jax.random.uniform(jax.random.fold_in(_gk, 15), (6250,), jnp.float32, 0.0, 0.999833)
        return (x, src, dst, edge_attr_8, edge_weight, node_vec)
    x, src, dst, edge_attr_8, edge_weight, node_vec = _rec_inputs()

    def _L0_gnn_setup():
        import jax, jax.numpy as jnp
        import numpy as np
        N = 12500
        E = 100000
        FEAT = 256
        HEADS = 8
        HEAD_DIM = FEAT // HEADS
        SCALING = HEAD_DIM ** (-0.5)
        key = jax.random.key(seed)
        ks = jax.random.split(key, 8)
        w_scale = (2.0 / (FEAT + FEAT)) ** 0.5
        return {'nfeat': jax.random.normal(ks[0], (N, FEAT), dtype=jnp.float32), 'attn_bias': jax.random.normal(ks[1], (E, HEADS), dtype=jnp.float32), 'Wq': jax.random.normal(ks[2], (FEAT, FEAT), dtype=jnp.float32) * w_scale, 'Wk': jax.random.normal(ks[3], (FEAT, FEAT), dtype=jnp.float32) * w_scale, 'Wv': jax.random.normal(ks[4], (FEAT, FEAT), dtype=jnp.float32) * w_scale, 'Wo': jax.random.normal(ks[5], (FEAT, FEAT), dtype=jnp.float32) * w_scale, 'src': jax.random.randint(ks[6], (E,), 0, N, dtype=jnp.int32), 'dst': jax.random.randint(ks[7], (E,), 0, N, dtype=jnp.int32)}
    _L0_gnn_all = _L0_gnn_setup()
    _L0_gnn_in = {k: v for k, v in _L0_gnn_all.items() if k in ('Wq', 'Wk', 'Wv', 'Wo')}
    del _L0_gnn_all

    def _L0_ffn_setup():
        import jax, jax.numpy as jnp
        import numpy as np
        B, N, D = (16, 512, 256)
        NUM_EXPERTS, TOP_K, HEADS = (4, 2, 4)
        N_EDGES = 131072
        LN_EPS = 1e-05

        def _layernorm(x, g, b):
            mu = x.mean(-1, keepdims=True)
            var = ((x - mu) ** 2).mean(-1, keepdims=True)
            return (x - mu) * jax.lax.rsqrt(var + LN_EPS) * g + b

        def _forward(x, edge_index, W_gat, att_src, att_dst, b_gat, ln_gamma, ln_beta, W1, b1, W2, b2):
            Bc, Nc, Dc = x.shape
            M = Bc * Nc
            x_flat = x.reshape(M, Dc)
            h = (x_flat @ W_gat).reshape(M, HEADS, NUM_EXPERTS)
            loops = jnp.arange(M, dtype=edge_index.dtype)
            src = jnp.concatenate([edge_index[0], loops])
            dst = jnp.concatenate([edge_index[1], loops])
            a_src = (h * att_src).sum(-1)
            a_dst = (h * att_dst).sum(-1)
            e = jax.nn.leaky_relu(a_src[src] + a_dst[dst], negative_slope=0.2)
            e_max = jax.ops.segment_max(e, dst, num_segments=M)
            ee = jnp.exp(e - e_max[dst])
            denom = jax.ops.segment_sum(ee, dst, num_segments=M)
            alpha = ee / (denom[dst] + 1e-16)
            msg = h[src] * alpha[:, :, None]
            agg = jax.ops.segment_sum(msg, dst, num_segments=M).reshape(M, HEADS * NUM_EXPERTS) + b_gat
            scores = _layernorm(agg, ln_gamma, ln_beta).reshape(M, HEADS, NUM_EXPERTS).mean(1)
            scores = scores.reshape(Bc, Nc, NUM_EXPERTS)
            topk_s, topk_i = jax.lax.top_k(scores, TOP_K)
            w = jax.nn.softmax(topk_s, axis=-1)
            out = jnp.zeros_like(x)
            for ei in range(NUM_EXPERTS):
                g = jnp.where(topk_i == ei, w, 0.0).sum(-1)
                hh = jax.nn.gelu(x @ W1[ei] + b1[ei], approximate=False)
                out = out + g[..., None] * (hh @ W2[ei] + b2[ei])
            return out
        key = jax.random.key(seed)
        ks = jax.random.split(key, 8)
        s = 0.05
        return {'x': jax.random.normal(ks[0], (B, N, D), jnp.float32), 'W_gat': jax.random.normal(ks[1], (D, HEADS * NUM_EXPERTS), jnp.float32) * s, 'att_src': jax.random.normal(ks[2], (HEADS, NUM_EXPERTS), jnp.float32) * s, 'att_dst': jax.random.normal(ks[3], (HEADS, NUM_EXPERTS), jnp.float32) * s, 'b_gat': jnp.zeros((HEADS * NUM_EXPERTS,), jnp.float32), 'ln_gamma': jnp.ones((HEADS * NUM_EXPERTS,), jnp.float32), 'ln_beta': jnp.zeros((HEADS * NUM_EXPERTS,), jnp.float32), 'W1': jax.random.normal(ks[4], (NUM_EXPERTS, D, 2 * D), jnp.float32) * s, 'b1': jnp.zeros((NUM_EXPERTS, 2 * D), jnp.float32), 'W2': jax.random.normal(ks[5], (NUM_EXPERTS, 2 * D, D), jnp.float32) * s, 'b2': jnp.zeros((NUM_EXPERTS, D), jnp.float32), 'edge_index': jax.random.randint(ks[6], (2, N_EDGES), 0, B * N, jnp.int32)}
    _L0_ffn_all = _L0_ffn_setup()
    _L0_ffn_in = {k: v for k, v in _L0_ffn_all.items() if k in ('W_gat', 'att_src', 'att_dst', 'b_gat', 'ln_gamma', 'ln_beta', 'W1', 'b1', 'W2', 'b2', 'edge_index')}
    del _L0_ffn_all

    def _L1_gnn_setup():
        import jax, jax.numpy as jnp
        import numpy as np
        from jax import lax
        N, E, D = (1024, 32768, 256)
        NH, FOUT = (4, 64)
        D_STATE, D_CONV, DT_RANK = (16, 4, 16)

        def _layer_norm(x, g, b, eps=1e-05):
            mu = jnp.mean(x, -1, keepdims=True)
            var = jnp.var(x, -1, keepdims=True)
            return (x - mu) * lax.rsqrt(var + eps) * g + b

        def _mamba(xs, in_proj_w, conv_w, conv_b, x_proj_w, dt_proj_w, dt_proj_b, A_log, D_param, out_proj_w):
            n = xs.shape[0]
            xz = xs @ in_proj_w.T
            xc, z = jnp.split(xz, 2, axis=-1)
            K = conv_w.shape[1]
            xp = jnp.pad(xc, ((K - 1, 0), (0, 0)))
            xc = sum((xp[k:k + n] * conv_w[:, k] for k in range(K))) + conv_b
            xc = jax.nn.silu(xc)
            dbc = xc @ x_proj_w.T
            dt = jax.nn.softplus(dbc[:, :DT_RANK] @ dt_proj_w.T + dt_proj_b)
            Bm = dbc[:, DT_RANK:DT_RANK + D_STATE]
            Cm = dbc[:, DT_RANK + D_STATE:]
            A = -jnp.exp(A_log)
            dA = jnp.exp(dt[:, :, None] * A)
            dBx = (dt * xc)[:, :, None] * Bm[:, None, :]

            def step(h, t):
                dA_t, dBx_t, C_t = t
                h = dA_t * h + dBx_t
                return (h, h @ C_t)
            _, y = lax.scan(step, jnp.zeros((xc.shape[1], D_STATE), xs.dtype), (dA, dBx, Cm))
            y = y + xc * D_param
            y = y * jax.nn.silu(z)
            return y @ out_proj_w.T

        def _forward(x, edge_index, deg_noise, gat_w, gat_a_src, gat_a_tgt, gat_b, ln_local_g, ln_local_b, ln_global_g, ln_global_b, ln2_g, ln2_b, in_proj_w, conv_w, conv_b, x_proj_w, dt_proj_w, dt_proj_b, A_log, D_param, out_proj_w, wl, wg, ff1_w, ff1_b, ff2_w, ff2_b):
            n = x.shape[0]
            src, tgt = (edge_index[0], edge_index[1])
            proj = (x @ gat_w.T).reshape(n, NH, FOUT)
            s_src = jnp.sum(proj * gat_a_src, -1)
            s_tgt = jnp.sum(proj * gat_a_tgt, -1)
            e = jax.nn.leaky_relu(s_src[src] + s_tgt[tgt], 0.2)
            exp_e = jnp.exp(e - jnp.max(e))
            denom = jax.ops.segment_sum(exp_e, tgt, num_segments=n)
            attn = exp_e / (denom[tgt] + 1e-16)
            agg = jax.ops.segment_sum(proj[src] * attn[:, :, None], tgt, num_segments=n)
            h_local = jax.nn.elu((agg + x.reshape(n, NH, FOUT)).reshape(n, NH * FOUT) + gat_b)
            h_local = _layer_norm(h_local, ln_local_g, ln_local_b)
            deg = jax.ops.segment_sum(jnp.ones((src.shape[0],), x.dtype), src, num_segments=n)
            perm = jnp.argsort(deg + deg_noise, stable=True)
            inv = jnp.argsort(perm)
            y = _mamba(x[perm], in_proj_w, conv_w, conv_b, x_proj_w, dt_proj_w, dt_proj_b, A_log, D_param, out_proj_w)
            h_attn = _layer_norm(x + y[inv], ln_global_g, ln_global_b)
            gate = jax.nn.sigmoid(h_local @ wl.T + h_attn @ wg.T)
            h = gate * h_local + (1.0 - gate) * h_attn
            ff = jax.nn.relu(h @ ff1_w.T + ff1_b) @ ff2_w.T + ff2_b
            return _layer_norm(h + ff, ln2_g, ln2_b)
        key = jax.random.key(seed)
        ks = jax.random.split(key, 24)
        w = lambda i, shape, s=0.05: jax.random.normal(ks[i], shape, dtype=jnp.float32) * s
        return {'x': jax.random.normal(ks[0], (N, D), dtype=jnp.float32), 'edge_index': jax.random.randint(ks[1], (2, E), 0, N, dtype=jnp.int32), 'edge_prob': jax.random.uniform(ks[2], (E,), dtype=jnp.float32), 'deg_noise': jax.random.uniform(ks[3], (N,), dtype=jnp.float32), 'gat_w': w(4, (NH * FOUT, D)), 'gat_a_src': w(5, (NH, FOUT)), 'gat_a_tgt': w(6, (NH, FOUT)), 'gat_b': jnp.zeros((NH * FOUT,), jnp.float32), 'ln_local_g': jnp.ones((D,), jnp.float32), 'ln_local_b': jnp.zeros((D,), jnp.float32), 'ln_global_g': jnp.ones((D,), jnp.float32), 'ln_global_b': jnp.zeros((D,), jnp.float32), 'ln2_g': jnp.ones((D,), jnp.float32), 'ln2_b': jnp.zeros((D,), jnp.float32), 'in_proj_w': w(7, (2 * D, D)), 'conv_w': w(8, (D, D_CONV), 0.2), 'conv_b': jnp.zeros((D,), jnp.float32), 'x_proj_w': w(9, (DT_RANK + 2 * D_STATE, D)), 'dt_proj_w': w(10, (D, DT_RANK)), 'dt_proj_b': w(11, (D,), 0.1) - 4.0, 'A_log': jnp.log(jnp.tile(jnp.arange(1, D_STATE + 1, dtype=jnp.float32), (D, 1))), 'D_param': jnp.ones((D,), jnp.float32), 'out_proj_w': w(12, (D, D)), 'wl': w(13, (D, D)), 'wg': w(14, (D, D)), 'ff1_w': w(15, (2 * D, D)), 'ff1_b': jnp.zeros((2 * D,), jnp.float32), 'ff2_w': w(16, (D, 2 * D)), 'ff2_b': jnp.zeros((D,), jnp.float32)}
    _L1_gnn_all = _L1_gnn_setup()
    _L1_gnn_in = {k: v for k, v in _L1_gnn_all.items() if k in ('gat_w', 'gat_a_src', 'gat_a_tgt', 'gat_b', 'ln_local_g', 'ln_local_b', 'ln_global_g', 'ln_global_b', 'ln2_g', 'ln2_b', 'in_proj_w', 'conv_w', 'conv_b', 'x_proj_w', 'dt_proj_w', 'dt_proj_b', 'A_log', 'D_param', 'out_proj_w', 'wl', 'wg', 'ff1_w', 'ff1_b', 'ff2_w', 'ff2_b')}
    del _L1_gnn_all

    def _L1_ffn_setup():
        import jax, jax.numpy as jnp
        import numpy as np
        C = 256
        HID = 1024
        E = 8
        TEMP = 1.0
        key = jax.random.key(seed)
        ks = jax.random.split(key, 7)
        x = jax.random.normal(ks[0], (8, 2048, C), dtype=jnp.float32)
        W1 = jax.random.normal(ks[1], (C, HID), dtype=jnp.float32) * 0.02
        b1 = jnp.zeros((HID,), dtype=jnp.float32)
        Wg = jax.random.normal(ks[2], (HID, E), dtype=jnp.float32) * 0.02
        bg = jnp.zeros((E,), dtype=jnp.float32)
        Wd = jax.random.normal(ks[3], (E, HID, C), dtype=jnp.float32) * 0.02
        bd = jnp.zeros((E, C), dtype=jnp.float32)
        return {'x': x, 'W1': W1, 'b1': b1, 'Wg': Wg, 'bg': bg, 'Wd': Wd, 'bd': bd}
    _L1_ffn_all = _L1_ffn_setup()
    _L1_ffn_in = {k: v for k, v in _L1_ffn_all.items() if k in ('W1', 'b1', 'Wg', 'bg', 'Wd', 'bd')}
    del _L1_ffn_all
    return {'x': x, 'src': src, 'dst': dst, 'edge_attr_8': edge_attr_8, 'edge_weight': edge_weight, 'node_vec': node_vec, 'L0_gnn_Wq': _L0_gnn_in['Wq'], 'L0_gnn_Wk': _L0_gnn_in['Wk'], 'L0_gnn_Wv': _L0_gnn_in['Wv'], 'L0_gnn_Wo': _L0_gnn_in['Wo'], 'L0_ffn_W_gat': _L0_ffn_in['W_gat'], 'L0_ffn_att_src': _L0_ffn_in['att_src'], 'L0_ffn_att_dst': _L0_ffn_in['att_dst'], 'L0_ffn_b_gat': _L0_ffn_in['b_gat'], 'L0_ffn_ln_gamma': _L0_ffn_in['ln_gamma'], 'L0_ffn_ln_beta': _L0_ffn_in['ln_beta'], 'L0_ffn_W1': _L0_ffn_in['W1'], 'L0_ffn_b1': _L0_ffn_in['b1'], 'L0_ffn_W2': _L0_ffn_in['W2'], 'L0_ffn_b2': _L0_ffn_in['b2'], 'L0_ffn_edge_index': _L0_ffn_in['edge_index'], 'L1_gnn_gat_w': _L1_gnn_in['gat_w'], 'L1_gnn_gat_a_src': _L1_gnn_in['gat_a_src'], 'L1_gnn_gat_a_tgt': _L1_gnn_in['gat_a_tgt'], 'L1_gnn_gat_b': _L1_gnn_in['gat_b'], 'L1_gnn_ln_local_g': _L1_gnn_in['ln_local_g'], 'L1_gnn_ln_local_b': _L1_gnn_in['ln_local_b'], 'L1_gnn_ln_global_g': _L1_gnn_in['ln_global_g'], 'L1_gnn_ln_global_b': _L1_gnn_in['ln_global_b'], 'L1_gnn_ln2_g': _L1_gnn_in['ln2_g'], 'L1_gnn_ln2_b': _L1_gnn_in['ln2_b'], 'L1_gnn_in_proj_w': _L1_gnn_in['in_proj_w'], 'L1_gnn_conv_w': _L1_gnn_in['conv_w'], 'L1_gnn_conv_b': _L1_gnn_in['conv_b'], 'L1_gnn_x_proj_w': _L1_gnn_in['x_proj_w'], 'L1_gnn_dt_proj_w': _L1_gnn_in['dt_proj_w'], 'L1_gnn_dt_proj_b': _L1_gnn_in['dt_proj_b'], 'L1_gnn_A_log': _L1_gnn_in['A_log'], 'L1_gnn_D_param': _L1_gnn_in['D_param'], 'L1_gnn_out_proj_w': _L1_gnn_in['out_proj_w'], 'L1_gnn_wl': _L1_gnn_in['wl'], 'L1_gnn_wg': _L1_gnn_in['wg'], 'L1_gnn_ff1_w': _L1_gnn_in['ff1_w'], 'L1_gnn_ff1_b': _L1_gnn_in['ff1_b'], 'L1_gnn_ff2_w': _L1_gnn_in['ff2_w'], 'L1_gnn_ff2_b': _L1_gnn_in['ff2_b'], 'L1_ffn_W1': _L1_ffn_in['W1'], 'L1_ffn_b1': _L1_ffn_in['b1'], 'L1_ffn_Wg': _L1_ffn_in['Wg'], 'L1_ffn_bg': _L1_ffn_in['bg'], 'L1_ffn_Wd': _L1_ffn_in['Wd'], 'L1_ffn_bd': _L1_ffn_in['bd']}

def reference(x, src, dst, edge_attr_8, edge_weight, node_vec, L0_gnn_Wq, L0_gnn_Wk, L0_gnn_Wv, L0_gnn_Wo, L0_ffn_W_gat, L0_ffn_att_src, L0_ffn_att_dst, L0_ffn_b_gat, L0_ffn_ln_gamma, L0_ffn_ln_beta, L0_ffn_W1, L0_ffn_b1, L0_ffn_W2, L0_ffn_b2, L0_ffn_edge_index, L1_gnn_gat_w, L1_gnn_gat_a_src, L1_gnn_gat_a_tgt, L1_gnn_gat_b, L1_gnn_ln_local_g, L1_gnn_ln_local_b, L1_gnn_ln_global_g, L1_gnn_ln_global_b, L1_gnn_ln2_g, L1_gnn_ln2_b, L1_gnn_in_proj_w, L1_gnn_conv_w, L1_gnn_conv_b, L1_gnn_x_proj_w, L1_gnn_dt_proj_w, L1_gnn_dt_proj_b, L1_gnn_A_log, L1_gnn_D_param, L1_gnn_out_proj_w, L1_gnn_wl, L1_gnn_wg, L1_gnn_ff1_w, L1_gnn_ff1_b, L1_gnn_ff2_w, L1_gnn_ff2_b, L1_ffn_W1, L1_ffn_b1, L1_ffn_Wg, L1_ffn_bg, L1_ffn_Wd, L1_ffn_bd):
    import jax
    import jax.numpy as jnp

    def _L0_gnn_ref(nfeat, attn_bias, Wq, Wk, Wv, Wo, src, dst):
        import jax, jax.numpy as jnp
        import numpy as np
        N = 12500
        E = 100000
        FEAT = 256
        HEADS = 8
        HEAD_DIM = FEAT // HEADS
        SCALING = HEAD_DIM ** (-0.5)
        n = nfeat.shape[0]
        q = (nfeat @ Wq.T).reshape(n, HEADS, HEAD_DIM) / SCALING
        k = (nfeat @ Wk.T).reshape(n, HEADS, HEAD_DIM)
        v = (nfeat @ Wv.T).reshape(n, HEADS, HEAD_DIM)
        attn = jnp.einsum('ehd,ehd->eh', k[src], q[dst])
        attn = attn + attn_bias
        m = jax.ops.segment_max(attn, dst, num_segments=n)
        a = jnp.exp(attn - m[dst])
        s = jax.ops.segment_sum(a, dst, num_segments=n)
        a = a / s[dst]
        out = jax.ops.segment_sum(v[src] * a[:, :, None], dst, num_segments=n)
        return out.reshape(n, FEAT) @ Wo.T

    def _L0_ffn_ref(x, W_gat, att_src, att_dst, b_gat, ln_gamma, ln_beta, W1, b1, W2, b2, edge_index):
        import jax, jax.numpy as jnp
        import numpy as np
        B, N, D = (16, 512, 256)
        NUM_EXPERTS, TOP_K, HEADS = (4, 2, 4)
        N_EDGES = 131072
        LN_EPS = 1e-05

        def _layernorm(x, g, b):
            mu = x.mean(-1, keepdims=True)
            var = ((x - mu) ** 2).mean(-1, keepdims=True)
            return (x - mu) * jax.lax.rsqrt(var + LN_EPS) * g + b

        def _forward(x, edge_index, W_gat, att_src, att_dst, b_gat, ln_gamma, ln_beta, W1, b1, W2, b2):
            Bc, Nc, Dc = x.shape
            M = Bc * Nc
            x_flat = x.reshape(M, Dc)
            h = (x_flat @ W_gat).reshape(M, HEADS, NUM_EXPERTS)
            loops = jnp.arange(M, dtype=edge_index.dtype)
            src = jnp.concatenate([edge_index[0], loops])
            dst = jnp.concatenate([edge_index[1], loops])
            a_src = (h * att_src).sum(-1)
            a_dst = (h * att_dst).sum(-1)
            e = jax.nn.leaky_relu(a_src[src] + a_dst[dst], negative_slope=0.2)
            e_max = jax.ops.segment_max(e, dst, num_segments=M)
            ee = jnp.exp(e - e_max[dst])
            denom = jax.ops.segment_sum(ee, dst, num_segments=M)
            alpha = ee / (denom[dst] + 1e-16)
            msg = h[src] * alpha[:, :, None]
            agg = jax.ops.segment_sum(msg, dst, num_segments=M).reshape(M, HEADS * NUM_EXPERTS) + b_gat
            scores = _layernorm(agg, ln_gamma, ln_beta).reshape(M, HEADS, NUM_EXPERTS).mean(1)
            scores = scores.reshape(Bc, Nc, NUM_EXPERTS)
            topk_s, topk_i = jax.lax.top_k(scores, TOP_K)
            w = jax.nn.softmax(topk_s, axis=-1)
            out = jnp.zeros_like(x)
            for ei in range(NUM_EXPERTS):
                g = jnp.where(topk_i == ei, w, 0.0).sum(-1)
                hh = jax.nn.gelu(x @ W1[ei] + b1[ei], approximate=False)
                out = out + g[..., None] * (hh @ W2[ei] + b2[ei])
            return out
        return _forward(x, edge_index, W_gat, att_src, att_dst, b_gat, ln_gamma, ln_beta, W1, b1, W2, b2)

    def _L1_gnn_ref(x, edge_index, edge_prob, deg_noise, gat_w, gat_a_src, gat_a_tgt, gat_b, ln_local_g, ln_local_b, ln_global_g, ln_global_b, ln2_g, ln2_b, in_proj_w, conv_w, conv_b, x_proj_w, dt_proj_w, dt_proj_b, A_log, D_param, out_proj_w, wl, wg, ff1_w, ff1_b, ff2_w, ff2_b):
        import jax, jax.numpy as jnp
        import numpy as np
        from jax import lax
        N, E, D = (1024, 32768, 256)
        NH, FOUT = (4, 64)
        D_STATE, D_CONV, DT_RANK = (16, 4, 16)

        def _layer_norm(x, g, b, eps=1e-05):
            mu = jnp.mean(x, -1, keepdims=True)
            var = jnp.var(x, -1, keepdims=True)
            return (x - mu) * lax.rsqrt(var + eps) * g + b

        def _mamba(xs, in_proj_w, conv_w, conv_b, x_proj_w, dt_proj_w, dt_proj_b, A_log, D_param, out_proj_w):
            n = xs.shape[0]
            xz = xs @ in_proj_w.T
            xc, z = jnp.split(xz, 2, axis=-1)
            K = conv_w.shape[1]
            xp = jnp.pad(xc, ((K - 1, 0), (0, 0)))
            xc = sum((xp[k:k + n] * conv_w[:, k] for k in range(K))) + conv_b
            xc = jax.nn.silu(xc)
            dbc = xc @ x_proj_w.T
            dt = jax.nn.softplus(dbc[:, :DT_RANK] @ dt_proj_w.T + dt_proj_b)
            Bm = dbc[:, DT_RANK:DT_RANK + D_STATE]
            Cm = dbc[:, DT_RANK + D_STATE:]
            A = -jnp.exp(A_log)
            dA = jnp.exp(dt[:, :, None] * A)
            dBx = (dt * xc)[:, :, None] * Bm[:, None, :]

            def step(h, t):
                dA_t, dBx_t, C_t = t
                h = dA_t * h + dBx_t
                return (h, h @ C_t)
            _, y = lax.scan(step, jnp.zeros((xc.shape[1], D_STATE), xs.dtype), (dA, dBx, Cm))
            y = y + xc * D_param
            y = y * jax.nn.silu(z)
            return y @ out_proj_w.T

        def _forward(x, edge_index, deg_noise, gat_w, gat_a_src, gat_a_tgt, gat_b, ln_local_g, ln_local_b, ln_global_g, ln_global_b, ln2_g, ln2_b, in_proj_w, conv_w, conv_b, x_proj_w, dt_proj_w, dt_proj_b, A_log, D_param, out_proj_w, wl, wg, ff1_w, ff1_b, ff2_w, ff2_b):
            n = x.shape[0]
            src, tgt = (edge_index[0], edge_index[1])
            proj = (x @ gat_w.T).reshape(n, NH, FOUT)
            s_src = jnp.sum(proj * gat_a_src, -1)
            s_tgt = jnp.sum(proj * gat_a_tgt, -1)
            e = jax.nn.leaky_relu(s_src[src] + s_tgt[tgt], 0.2)
            exp_e = jnp.exp(e - jnp.max(e))
            denom = jax.ops.segment_sum(exp_e, tgt, num_segments=n)
            attn = exp_e / (denom[tgt] + 1e-16)
            agg = jax.ops.segment_sum(proj[src] * attn[:, :, None], tgt, num_segments=n)
            h_local = jax.nn.elu((agg + x.reshape(n, NH, FOUT)).reshape(n, NH * FOUT) + gat_b)
            h_local = _layer_norm(h_local, ln_local_g, ln_local_b)
            deg = jax.ops.segment_sum(jnp.ones((src.shape[0],), x.dtype), src, num_segments=n)
            perm = jnp.argsort(deg + deg_noise, stable=True)
            inv = jnp.argsort(perm)
            y = _mamba(x[perm], in_proj_w, conv_w, conv_b, x_proj_w, dt_proj_w, dt_proj_b, A_log, D_param, out_proj_w)
            h_attn = _layer_norm(x + y[inv], ln_global_g, ln_global_b)
            gate = jax.nn.sigmoid(h_local @ wl.T + h_attn @ wg.T)
            h = gate * h_local + (1.0 - gate) * h_attn
            ff = jax.nn.relu(h @ ff1_w.T + ff1_b) @ ff2_w.T + ff2_b
            return _layer_norm(h + ff, ln2_g, ln2_b)
        return _forward(x, edge_index, deg_noise, gat_w, gat_a_src, gat_a_tgt, gat_b, ln_local_g, ln_local_b, ln_global_g, ln_global_b, ln2_g, ln2_b, in_proj_w, conv_w, conv_b, x_proj_w, dt_proj_w, dt_proj_b, A_log, D_param, out_proj_w, wl, wg, ff1_w, ff1_b, ff2_w, ff2_b)

    def _L1_ffn_ref(x, W1, b1, Wg, bg, Wd, bd):
        import jax, jax.numpy as jnp
        import numpy as np
        C = 256
        HID = 1024
        E = 8
        TEMP = 1.0
        orig_shape = x.shape
        xf = x.reshape(-1, orig_shape[-1])
        H = jax.nn.gelu(xf @ W1 + b1, approximate=False)
        probs = jax.nn.softmax((H @ Wg + bg) / TEMP, axis=-1)
        assign = jnp.argmax(probs, axis=-1)
        out = jnp.zeros_like(xf)
        for e in range(Wd.shape[0]):
            y = H @ Wd[e] + bd[e]
            sel = (assign == e)[:, None]
            out = out + jnp.where(sel, probs[:, e:e + 1] * y, 0.0)
        return out.reshape(orig_shape)
    edge_index = jnp.stack([src, dst])
    x = x + _L0_gnn_ref(_layernorm(x, axis=-1), edge_attr_8, L0_gnn_Wq, L0_gnn_Wk, L0_gnn_Wv, L0_gnn_Wo, src, dst)
    x = x + _L0_ffn_ref(_layernorm(x, axis=-1)[None], L0_ffn_W_gat, L0_ffn_att_src, L0_ffn_att_dst, L0_ffn_b_gat, L0_ffn_ln_gamma, L0_ffn_ln_beta, L0_ffn_W1, L0_ffn_b1, L0_ffn_W2, L0_ffn_b2, L0_ffn_edge_index)[0]
    x = x + _L1_gnn_ref(_layernorm(x, axis=-1), edge_index, edge_weight, node_vec, L1_gnn_gat_w, L1_gnn_gat_a_src, L1_gnn_gat_a_tgt, L1_gnn_gat_b, L1_gnn_ln_local_g, L1_gnn_ln_local_b, L1_gnn_ln_global_g, L1_gnn_ln_global_b, L1_gnn_ln2_g, L1_gnn_ln2_b, L1_gnn_in_proj_w, L1_gnn_conv_w, L1_gnn_conv_b, L1_gnn_x_proj_w, L1_gnn_dt_proj_w, L1_gnn_dt_proj_b, L1_gnn_A_log, L1_gnn_D_param, L1_gnn_out_proj_w, L1_gnn_wl, L1_gnn_wg, L1_gnn_ff1_w, L1_gnn_ff1_b, L1_gnn_ff2_w, L1_gnn_ff2_b)
    x = x + _L1_ffn_ref(_layernorm(x, axis=-1)[None], L1_ffn_W1, L1_ffn_b1, L1_ffn_Wg, L1_ffn_bg, L1_ffn_Wd, L1_ffn_bd)[0]
    return x

_drawn_inputs = setup_inputs


def setup_inputs(seed=0):
    import zlib

    import numpy as np

    out = dict(_drawn_inputs(seed))
    spreads = {'L0_ffn_b_gat': (0.0, 0.1),
     'L0_ffn_ln_gamma': (1.0, 0.2),
     'L0_ffn_ln_beta': (0.0, 0.1),
     'L0_ffn_b1': (0.0, 0.1),
     'L0_ffn_b2': (0.0, 0.1),
     'L1_gnn_gat_b': (0.0, 0.343),
     'L1_gnn_ln_local_g': (1.0, 0.2),
     'L1_gnn_ln_local_b': (0.0, 0.331),
     'L1_gnn_ln_global_g': (1.0, 0.2),
     'L1_gnn_ln_global_b': (0.0, 0.37),
     'L1_gnn_ln2_g': (1.0, 0.2),
     'L1_gnn_ln2_b': (0.0, 0.1),
     'L1_gnn_conv_b': (0.0, 0.8),
     'L1_gnn_D_param': (1.0, 0.6),
     'L1_gnn_ff1_b': (0.0, 0.291),
     'L1_gnn_ff2_b': (0.0, 0.1),
     'L1_ffn_b1': (0.0, 0.8),
     'L1_ffn_bg': (0.0, 0.8),
     'L1_ffn_bd': (0.0, 0.8)}
    factors = {'node_vec': 4.182,
     'L1_gnn_gat_a_src': 5.178,
     'L1_gnn_gat_a_tgt': 8.0,
     'L1_gnn_in_proj_w': 3.447,
     'L1_gnn_conv_w': 3.698,
     'L1_gnn_x_proj_w': 8.0,
     'L1_gnn_dt_proj_w': 8.0,
     'L1_gnn_dt_proj_b': 8.0,
     'L1_gnn_A_log': 8.0,
     'L1_gnn_out_proj_w': 3.423,
     'L1_ffn_W1': 6.202,
     'L1_ffn_Wg': 6.541,
     'L1_ffn_Wd': 7.698}
    for name, (base, spread) in spreads.items():
        noise = np.random.default_rng([zlib.crc32(name.encode()), seed]).standard_normal(out[name].shape)
        drawn = base * np.exp(spread * noise) if base else spread * noise
        out[name] = jnp.asarray(drawn.astype(out[name].dtype))
    for name, factor in factors.items():
        out[name] = (out[name] * factor).astype(out[name].dtype)
    return out
```

```python
import numpy as np
import concourse.bass as bass
from concourse import mybir
from contextlib import ExitStack

F32 = mybir.dt.float32
BF16 = mybir.dt.bfloat16
I32 = mybir.dt.int32
ALU = mybir.AluOpType
ACT = mybir.ActivationFunctionType
AX = mybir.AxisListType

P = 128
N = 6250
D = 256
KC = D // P
NT = -(-N // P)
NP = NT * P
TAIL = N - (NT - 1) * P
U = 7
GROUPS = NT // U
GN = U * P
EPS = 1e-5

E = 200000
H0 = 8
HD0 = D // H0
CH = P // H0
CT = -(-(-(-E // P)) // CH)
ET = CH * CT
STEPS = ET + NT - 1
ETX = ET + 24
SU = 8
PAD_DST = 8191
NEG = -1e30

E2 = 131072
ET2 = E2 // P
HR = 4
NX = 4
HR16 = HR * NX
RW = HR16 + HR
FH = 512
H1 = 4
HD1 = D // H1
PW = D + H1
TW = 2 * H1 + 1
DS = 16
DTR = 16
CONV = 4
HID = 1024
NE = 8


NAMES = {}


def fresh(name):
    NAMES[name] = NAMES.get(name, 0) + 1
    return name if NAMES[name] == 1 else f"{name}_{NAMES[name]}"


class Chain:

    def __init__(self, eng, sem):
        self.eng, self.sem, self.n = eng, sem, 0

    def __call__(self, ins):
        self.n += 1
        ins.then_inc(self.sem, 1)
        self.eng.wait_ge(self.sem, self.n)


class Steps:

    def __init__(self, eng, sem, turn, total):
        self.eng, self.sem, self.base, self.n = eng, sem, turn * total, 0

    def __call__(self, ins):
        self.n += 1
        ins.then_inc(self.sem, 1)
        self.eng.wait_ge(self.sem, self.base + self.n)


def bc(ap, shape):
    return ap.unsqueeze(len(ap.shape)).to_broadcast(shape)


def node_view(dram):
    full = dram[0:(NT - 1) * P, :].rearrange("(t p) d -> p t d", p=P)
    return full, dram[(NT - 1) * P:N, :]


def constants(nc, ident, iota):
    with nc.semaphore("c_zero") as zeroed, nc.semaphore("c_done") as made, nc.Block() as block:
        @block.gpsimd
        def _(pool):
            pool.memset(ident[:], 0.0).then_inc(zeroed, 1)
            pool.iota(iota[:], pattern=[[1, P]], base=0, channel_multiplier=0,
                      allow_small_or_imprecise_dtypes=True).then_inc(made, 1)
            pool.wait_ge(zeroed, 1)
            pool.affine_select(out=ident[:], in_=ident[:], compare_op=ALU.not_equal, fill=1.0, base=0,
                               pattern=[[-1, P]], channel_multiplier=1).then_inc(made, 1)
            pool.wait_ge(made, 2)


def load_nodes(nc, dst, dram):
    full, tail = node_view(dram)
    with nc.semaphore("ld") as loaded, nc.semaphore("ldz") as cleared, nc.Block() as block:
        @block.vector
        def _(dve):
            dve.memset(dst[:, NT - 1, :], 0.0).then_inc(cleared, 1)

        @block.sync
        def _(sp):
            sp.dma_start(dst[:, 0:NT - 1, :], full).then_inc(loaded, 16)
            sp.wait_ge(cleared, 1)
            sp.dma_start(dst[0:TAIL, NT - 1, :], tail).then_inc(loaded, 16)
            sp.wait_ge(loaded, 32)


def load_all(nc, pairs):
    with nc.semaphore("la") as loaded, nc.Block() as block:
        @block.sync
        def _(sp):
            for dst, src in pairs:
                sp.dma_start(dst, src).then_inc(loaded, 16)
            sp.wait_ge(loaded, 16 * len(pairs))


def rows_of(tab):
    return tab.rearrange("(t p) w -> p t w", p=P)


def store_nodes(nc, pairs):
    with nc.semaphore("st") as stored, nc.Block() as block:
        @block.sync
        def _(sp):
            for dst, src in pairs:
                sp.dma_start(rows_of(dst), src[:]).then_inc(stored, 16)
            sp.wait_ge(stored, 16 * len(pairs))


def layernorm(nc, src, out, scratch, gamma=None, beta=None):
    T, W = src.shape[1], src.shape[2]
    with ExitStack() as ctx:
        st = ctx.enter_context(nc.sbuf_tensor(fresh("ln_st"), [P, 4, T], F32))
        chain_sem = ctx.enter_context(nc.semaphore("ln_chain"))
        centred = ctx.enter_context(nc.semaphore("ln_centred"))
        squared = ctx.enter_context(nc.semaphore("ln_squared"))
        var_ready = ctx.enter_context(nc.semaphore("ln_var"))
        std_ready = ctx.enter_context(nc.semaphore("ln_std"))
        block = ctx.enter_context(nc.Block())
        full = [P, T, W]

        @block.vector
        def _(dve):
            link = Chain(dve, chain_sem)
            link(dve.tensor_reduce(st[:, 0, :], src, AX.X, ALU.add))
            link(dve.tensor_scalar(st[:, 1, :], st[:, 0, :], 1.0 / W, None, ALU.mult))
            dve.tensor_tensor(out, src, bc(st[:, 1, :], full), ALU.subtract).then_inc(centred, 1)
            dve.wait_ge(squared, 1)
            link(dve.tensor_reduce(st[:, 2, :], scratch, AX.X, ALU.add))
            dve.tensor_scalar(st[:, 3, :], st[:, 2, :], 1.0 / W, EPS, ALU.mult, ALU.add).then_inc(var_ready, 1)
            dve.wait_ge(std_ready, 1)
            link(dve.reciprocal(st[:, 1, :], st[:, 0, :]))
            link(dve.tensor_tensor(out, out, bc(st[:, 1, :], full), ALU.mult))
            if gamma is not None:
                link(dve.tensor_tensor(out, out, gamma.unsqueeze(1).to_broadcast(full), ALU.mult))
                link(dve.tensor_tensor(out, out, beta.unsqueeze(1).to_broadcast(full), ALU.add))

        @block.scalar
        def _(act):
            act.wait_ge(centred, 1)
            act.activation(scratch, out, ACT.Square).then_inc(squared, 1)
            act.wait_ge(var_ready, 1)
            act.activation(st[:, 0, :], st[:, 3, :], ACT.Sqrt).then_inc(std_ready, 1)


def apart(u, slots):
    return slots if u >= slots else u + U - max(v for v in range(U) if v % slots == u)


def tile(ap, t):
    return ap[:, bass.ds(t, 1), :].rearrange("p a w -> p (a w)")


XT_SLOTS = 2
OUT_SLOTS = 3


def project_tiles(nc, src, w, ident, evacuate, xT=None, turned_src=None):
    M = 0 if w is None else w.shape[2]
    parts = [(m, min(m + 512, M)) for m in range(0, M, 512)]
    with ExitStack() as ctx:
        xs = ctx.enter_context(nc.sbuf_tensor(fresh("pj_x"), [P, U, D], F32))
        xt = ctx.enter_context(nc.sbuf_tensor(fresh("pj_xt"), [P, U, D], F32))
        pT = ctx.enter_context(nc.psum_tensor(fresh("pj_pT"), [P, XT_SLOTS, 512], F32))
        po = ctx.enter_context(nc.psum_tensor(fresh("pj_po"), [P, OUT_SLOTS, 1024], F32))
        fetched = ctx.enter_context(nc.semaphore("pj_fetched"))
        turned = ctx.enter_context(nc.semaphore("pj_turned"))
        xt_ready = ctx.enter_context(nc.semaphore("pj_xt_ready"))
        made = ctx.enter_context(nc.semaphore("pj_made"))
        out_free = ctx.enter_context(nc.semaphore("pj_out_free"))
        block = ctx.enter_context(nc.Block())

        @block.gpsimd
        def _(pool):
            pool.sem_inc(turned, U)
            with pool.Fori(0, GROUPS) as g:
                for u in range(U):
                    pool.wait_ge(turned, g * U + u + 1)
                    if turned_src is None:
                        pool.tensor_copy(xs[:, u, :], tile(src, g * U + u)).then_inc(fetched, 1)
                    else:
                        pool.tensor_copy(xs[:, u, :].rearrange("p (k n) -> p k n", k=KC),
                                         turned_src[:, :, bass.ds((g * U + u) * P, P)]).then_inc(fetched, 1)

        @block.tensor
        def _(pe):
            def turn(g, u):
                pe.wait_ge(fetched, g * U + u + 1)
                pe.wait_ge(xt_ready, g * U + u + 1 + U - apart(u, XT_SLOTS))
                for k in range(KC):
                    ins = pe.matmul(pT[:, u % XT_SLOTS, k * P:(k + 1) * P], ident[:], xs[:, u, k * P:(k + 1) * P],
                                    start=True, stop=True) if turned_src is not None else \
                        pe.transpose(pT[:, u % XT_SLOTS, k * P:(k + 1) * P], xs[:, u, k * P:(k + 1) * P], ident[:])
                ins.then_inc(turned, 1)

            def multiply(g, u):
                pe.wait_ge(xt_ready, g * U + u + 1 + U)
                pe.wait_ge(out_free, g * U + u + 1 + U - apart(u, OUT_SLOTS))
                for a, b in parts:
                    for k in range(KC):
                        ins = pe.matmul(po[:, u % OUT_SLOTS, a:b], xt[:, u, k * P:(k + 1) * P], w[:, k, a:b],
                                        start=(k == 0), stop=(k == KC - 1))
                ins.then_inc(made, 1)

            with pe.Fori(0, GROUPS) as g:
                for u in range(U):
                    turn(g, u)
                    if M and u >= 1:
                        multiply(g, u - 1)
                if M:
                    multiply(g, U - 1)

        @block.scalar
        def _(act):
            act.sem_inc(xt_ready, U)
            if M:
                act.sem_inc(made, U)
            with act.Fori(0, GROUPS) as g:
                for u in range(U):
                    act.wait_ge(turned, g * U + u + 1 + U)
                    if M:
                        act.wait_ge(made, g * U + u + 1)
                    if xT is None:
                        act.copy(xt[:, u, :], pT[:, u % XT_SLOTS, 0:D]).then_inc(xt_ready, 1)
                    else:
                        if M:
                            act.copy(xt[:, u, :], pT[:, u % XT_SLOTS, 0:D])
                        act.copy(xT[:, :, bass.ds((g * U + u) * P, P)],
                                 pT[:, u % XT_SLOTS, 0:D].rearrange("p (k n) -> p k n", k=KC)).then_inc(xt_ready, 1)

        if M:
            @block.vector
            def _(dve):
                dve.sem_inc(out_free, U)
                with dve.Fori(0, GROUPS) as g:
                    for u in range(U):
                        dve.wait_ge(made, g * U + u + 1 + U)
                        evacuate(dve, po[:, u % OUT_SLOTS, :], g * U + u).then_inc(out_free, 1)


def phase_qkv(nc, env, d):
    with ExitStack() as ctx:
        q = ctx.enter_context(nc.sbuf_tensor(fresh("a_q"), [P, NT, D], F32))
        x = ctx.enter_context(nc.sbuf_tensor(fresh("a_x"), [P, NT, D], F32))
        xn = ctx.enter_context(nc.sbuf_tensor(fresh("a_xn"), [P, NT, D], F32))
        w = ctx.enter_context(nc.sbuf_tensor(fresh("a_w"), [P, KC, 3 * D], F32))
        load_all(nc, [(w[:], d["wqkvT"].rearrange("(k p) m -> p k m", p=P))])
        load_nodes(nc, x, d["x"])
        layernorm(nc, x[:], xn[:], q[:])

        def keep_qkv(dve, out, t):
            dve.tensor_scalar(tile(q, t), out[:, 0:D], float(1.0 / HD0 ** -0.5), None, ALU.mult)
            dve.tensor_copy(tile(x, t), out[:, D:2 * D])
            return dve.tensor_copy(tile(xn, t), out[:, 2 * D:3 * D])
        project_tiles(nc, xn, w, ident=env["ident"], evacuate=keep_qkv)
        with nc.semaphore("kv_out") as stored, nc.Block() as block:
            @block.sync
            def _(sp):
                sp.dma_start(d["k_tab"].rearrange("(t p) d -> p t d", p=P), x[:]).then_inc(stored, 16)
                sp.dma_start(d["v_tab"].rearrange("(t p) d -> p t d", p=P), xn[:]).then_inc(stored, 16)
                sp.dma_start(d["q_tab"].rearrange("(t p) d -> p t d", p=P), q[:]).then_inc(stored, 16)
                sp.wait_ge(stored, 48)


STEP_PAD = 24
SL = STEPS + STEP_PAD
SCOLS = 410
OH_LEAD = 2
OH_SLOTS = 4
ROW = CT * P
LW = ET * H0


def walk(nc, env, d):
    with ExitStack() as ctx:
        last = ctx.enter_context(nc.sbuf_tensor(fresh("w_last"), [P, ETX], I32))
        lastf = ctx.enter_context(nc.sbuf_tensor(fresh("w_lastf"), [P, ETX], F32))
        before = ctx.enter_context(nc.sbuf_tensor(fresh("w_before"), [P, ETX], F32))
        step = ctx.enter_context(nc.sbuf_tensor(fresh("w_step"), [P, SL], F32))
        entered = ctx.enter_context(nc.sbuf_tensor(fresh("w_entered"), [P, SL], F32))
        blk = ctx.enter_context(nc.sbuf_tensor(fresh("w_blk"), [P, SL], F32))
        col = ctx.enter_context(nc.sbuf_tensor(fresh("w_col"), [P, 4], F32))
        ones = ctx.enter_context(nc.sbuf_tensor(fresh("w_ones"), [P, P], F32))
        ps = ctx.enter_context(nc.psum_tensor(fresh("w_ps"), [P, 4, 512], F32))
        loaded = ctx.enter_context(nc.semaphore("w_loaded"))
        iotas = ctx.enter_context(nc.semaphore("w_iotas"))
        marked = ctx.enter_context(nc.semaphore("w_marked"))
        summed = ctx.enter_context(nc.semaphore("w_summed"))
        chain_sem = ctx.enter_context(nc.semaphore("w_chain"))
        block = ctx.enter_context(nc.Block())
        assert 4 * SCOLS == SL

        @block.sync
        def _(sp):
            sp.dma_start(last[:], d["tile_last"].partition_broadcast(P)).then_inc(loaded, 16)
            sp.dma_start(env["src"][:], d["src_cols"]).then_inc(loaded, 16)
            sp.dma_start(env["dst_i"][:], d["dst_cols"]).then_inc(loaded, 16)

        @block.gpsimd
        def _(pool):
            pool.iota(step[:], pattern=[[1, SL]], base=0, channel_multiplier=0,
                      allow_small_or_imprecise_dtypes=True).then_inc(iotas, 1)
            pool.iota(col[:, 0:1], pattern=[[0, 1]], base=0, channel_multiplier=1,
                      allow_small_or_imprecise_dtypes=True).then_inc(iotas, 1)

        @block.vector
        def _(dve):
            link = Chain(dve, chain_sem)
            link(dve.memset(ones[:], 1.0))
            dve.wait_ge(loaded, 48)
            dve.wait_ge(iotas, 2)
            link(dve.tensor_copy(env["dst"][:], env["dst_i"][:]))
            link(dve.tensor_copy(lastf[:], last[:]))
            link(dve.tensor_scalar(col[:, 1:2], col[:, 0:1], float(P), None, ALU.mult))
            link(dve.tensor_scalar(before[:], lastf[:], col[:, 1:2], None, ALU.is_lt, ALU.add, accum_out=col[:, 2:3]))
            link(dve.tensor_tensor(col[:, 3:4], col[:, 2:3], col[:, 0:1], ALU.add))
            dve.tensor_scalar(entered[:], step[:], col[:, 3:4], None, ALU.is_ge).then_inc(marked, 1)
            dve.wait_ge(summed, 1)
            link(dve.tensor_scalar(blk[:].rearrange("p (a c) -> p a c", a=4), ps[:, :, 0:SCOLS], -1.0, None, ALU.add))
            link(dve.tensor_scalar(env["base"][:], blk[:], float(P), None, ALU.mult))
            link(dve.tensor_copy(env["step_b"][:], blk[:]))

        @block.tensor
        def _(pe):
            pe.wait_ge(marked, 1)
            for a in range(4):
                ins = pe.matmul(ps[:, a, 0:SCOLS], ones[0:NT, :], entered[0:NT, a * SCOLS:(a + 1) * SCOLS],
                                start=True, stop=True)
            ins.then_inc(summed, 1)


def blocks_of(nc, eng, env, s, n):
    _, b = nc.values_load_multi_w_load_instructions(
        env["step_b"][0:1, bass.ds(s, n)], engines=(eng.engine,), min_val=0, max_val=NT - 1,
        skip_runtime_bounds_check_because='the walk has NT blocks')
    return b


def tile_of(nc, s, b, tiles=ETX):
    return nc.s_assert_within(s - b, 0, tiles - 1, 
                              skip_runtime_bounds_check_because="block b is entered at step T[b] + b or later")


def gather_rows(pool, table, rows, idx_slot, done):
    pool.indirect_dma_start(rows, None, table, bass.IndirectOffsetOnAxis(ap=idx_slot, axis=0)).then_inc(done, 16)


def one_hot(dve, env, out, s, t):
    return dve.tensor_scalar(out, env["iota"][:], env["base"][:, bass.ds(s, 1)], env["dst"][:, bass.ds(t, 1)],
                             ALU.add, ALU.is_equal)


def edge_logits(nc, env, d, logits, q):
    L = logits[:, 0:LW].rearrange("p (t h) -> p t h", h=H0)
    with ExitStack() as ctx:
        idx = ctx.enter_context(nc.sbuf_tensor(fresh("e_idx"), [P, SU], I32))
        rows = ctx.enter_context(nc.sbuf_tensor(fresh("e_rows"), [P, SU, D], F32))
        oh = ctx.enter_context(nc.sbuf_tensor(fresh("e_oh"), [P, OH_SLOTS, P], F32))
        ohT = ctx.enter_context(nc.sbuf_tensor(fresh("e_ohT"), [P, 2, P], F32))
        prod = ctx.enter_context(nc.sbuf_tensor(fresh("e_prod"), [P, 2, D], F32))
        dots = ctx.enter_context(nc.sbuf_tensor(fresh("e_dots"), [P, 2, H0], F32))
        pT = ctx.enter_context(nc.psum_tensor(fresh("e_pT"), [P, 2, 512], F32))
        pq = ctx.enter_context(nc.psum_tensor(fresh("e_pq"), [P, 2, 512], F32))
        idx_ready = ctx.enter_context(nc.semaphore("e_idx_ready"))
        landed = [ctx.enter_context(nc.semaphore(f"e_landed{u}")) for u in range(SU)]
        rows_used = ctx.enter_context(nc.semaphore("e_rows_used"))
        oh_ready = ctx.enter_context(nc.semaphore("e_oh_ready"))
        turned = ctx.enter_context(nc.semaphore("e_turned"))
        ohT_ready = ctx.enter_context(nc.semaphore("e_ohT_ready"))
        q_made = ctx.enter_context(nc.semaphore("e_q_made"))
        summed = ctx.enter_context(nc.semaphore("e_summed"))
        block = ctx.enter_context(nc.Block())

        @block.gpsimd
        def _(pool):
            with pool.Fori(0, STEPS // SU) as i:
                for u in range(SU):
                    pool.wait_ge(idx_ready, i * SU + u + 1)
                    pool.wait_ge(rows_used, i * SU + u + 1)
                    pool.nop(nofuse=True)
                    gather_rows(pool, d["k_tab"], rows[:, u, :], idx[:, u:u + 1], landed[u])

        @block.scalar
        def _(act):
            act.sem_inc(ohT_ready, 2)
            act.copy(idx[:], env["src"][:, 0:SU]).then_inc(idx_ready, SU)
            with act.Fori(0, STEPS // SU) as i:
                b = blocks_of(nc, act, env, i * SU + SU, SU)
                for u in range(SU):
                    act.wait_ge(turned, i * SU + u + 1 + OH_SLOTS)
                    act.wait_ge(q_made, i * SU + u + 1)
                    act.copy(ohT[:, u % 2, :], pT[:, u % 2, 0:P]).then_inc(ohT_ready, 1)
                    t = tile_of(nc, i * SU + (u + SU), b[u])
                    act.wait_ge(landed[u], i * 16 + 16)
                    act.copy(idx[:, u:u + 1], env["src"][:, bass.ds(t, 1)]).then_inc(idx_ready, 1)

        @block.tensor
        def _(pe):
            pe.sem_inc(turned, OH_SLOTS)
            pe.sem_inc(q_made, 2)

            def turn(s, u):
                pe.wait_ge(oh_ready, s + 1)
                pe.wait_ge(ohT_ready, s + 1)
                pe.transpose(pT[:, u % 2, 0:P], oh[:, u % OH_SLOTS, :], env["ident"][:]).then_inc(turned, 1)

            turn(0, 0)
            with pe.Fori(0, STEPS // SU) as i:
                b = blocks_of(nc, pe, env, i * SU, SU)
                for u in range(SU):
                    turn(i * SU + u + 1, u + 1)
                    pe.wait_ge(ohT_ready, i * SU + u + 1 + 2)
                    pe.wait_ge(rows_used, i * SU + u + 1 + SU - 2)
                    pe.matmul(pq[:, u % 2, 0:D], ohT[:, u % 2, :], tile(q, b[u]), start=True, stop=True).then_inc(q_made, 1)

        @block.vector
        def _(dve):
            dve.sem_inc(rows_used, SU)

            def mark(s, u, b):
                t = tile_of(nc, s, b)
                dve.wait_ge(turned, s + 1)
                one_hot(dve, env, oh[:, u % OH_SLOTS, :], s, t).then_inc(oh_ready, 1)

            for u in range(OH_LEAD):
                mark(u, u, 0)
            with dve.Fori(0, STEPS // SU) as i:
                b = blocks_of(nc, dve, env, i * SU, SU + 4)
                for u in range(SU):
                    s = i * SU + u
                    mark(s + OH_LEAD, u + OH_LEAD, b[u + OH_LEAD])
                    dve.wait_ge(landed[u], i * 16 + 16)
                    dve.wait_ge(q_made, s + 1 + 2)
                    dve.tensor_tensor(prod[:, u % 2, :], rows[:, u, :], pq[:, u % 2, 0:D], ALU.mult).then_inc(rows_used, 1)
                    t = tile_of(nc, s, b[u], ET)
                    dve.wait_ge(rows_used, s + 1 + SU)
                    dve.tensor_reduce(dots[:, u % 2, :], prod[:, u % 2, :].rearrange("p (h c) -> p h c", h=H0),
                                      AX.X, ALU.add).then_inc(summed, 1)
                    dve.wait_ge(summed, s + 1)
                    dve.tensor_tensor(tile(L, t), tile(L, t), dots[:, u % 2, :], ALU.add)


def edge_sums(nc, env, d, weights, acc):
    A = weights.rearrange("p (t h) -> p t h", h=H0)
    W = D + H0
    with ExitStack() as ctx:
        idx = ctx.enter_context(nc.sbuf_tensor(fresh("s_idx"), [P, SU], I32))
        rows = ctx.enter_context(nc.sbuf_tensor(fresh("s_rows"), [P, SU, D], F32))
        oh = ctx.enter_context(nc.sbuf_tensor(fresh("s_oh"), [P, OH_SLOTS, P], F32))
        msg = ctx.enter_context(nc.sbuf_tensor(fresh("s_msg"), [P, OH_SLOTS, W], F32))
        pa = ctx.enter_context(nc.psum_tensor(fresh("s_pa"), [P, 2, 512], F32))
        idx_ready = ctx.enter_context(nc.semaphore("s_idx_ready"))
        landed = [ctx.enter_context(nc.semaphore(f"s_landed{u}")) for u in range(SU)]
        msg_ready = ctx.enter_context(nc.semaphore("s_msg_ready"))
        a_ready = ctx.enter_context(nc.semaphore("s_a_ready"))
        oh_ready = ctx.enter_context(nc.semaphore("s_oh_ready"))
        made = ctx.enter_context(nc.semaphore("s_made"))
        added = ctx.enter_context(nc.semaphore("s_added"))
        cleared = ctx.enter_context(nc.semaphore("s_cleared"))
        block = ctx.enter_context(nc.Block())

        @block.gpsimd
        def _(pool):
            with pool.Fori(0, STEPS // SU) as i:
                for u in range(SU):
                    pool.wait_ge(idx_ready, i * SU + u + 1)
                    pool.wait_ge(msg_ready, i * SU + u + 1)
                    pool.nop(nofuse=True)
                    gather_rows(pool, d["v_tab"], rows[:, u, :], idx[:, u:u + 1], landed[u])
            pool.wait_ge(idx_ready, STEPS + 1)
            pool.wait_ge(msg_ready, STEPS + 1)
            pool.nop(nofuse=True)
            gather_rows(pool, d["v_tab"], rows[:, 0, :], idx[:, 0:1], landed[0])

        @block.scalar
        def _(act):
            act.copy(idx[:], env["src"][:, 0:SU]).then_inc(idx_ready, SU)
            with act.Fori(0, STEPS // SU) as i:
                b = blocks_of(nc, act, env, i * SU, 2 * SU)
                for u in range(SU):
                    t = tile_of(nc, i * SU + u, b[u], ET)
                    act.wait_ge(made, i * SU + u + 1)
                    act.copy(msg[:, u % OH_SLOTS, D:W], tile(A, t)).then_inc(a_ready, 1)
                    t = tile_of(nc, i * SU + (u + SU), b[u + SU])
                    act.wait_ge(landed[u], i * 16 + 16)
                    act.copy(idx[:, u:u + 1], env["src"][:, bass.ds(t, 1)]).then_inc(idx_ready, 1)

        @block.tensor
        def _(pe):
            pe.sem_inc(made, OH_SLOTS)
            with pe.Fori(0, STEPS // SU) as i:
                for u in range(SU):
                    s = i * SU + u
                    pe.wait_ge(oh_ready, s + 1)
                    pe.wait_ge(msg_ready, s + 1 + SU)
                    pe.wait_ge(a_ready, s + 1)
                    pe.wait_ge(added, s + 1)
                    pe.matmul(pa[:, u % 2, 0:W], oh[:, u % OH_SLOTS, :], msg[:, u % OH_SLOTS, :],
                              start=True, stop=True).then_inc(made, 1)

        @block.vector
        def _(dve):
            dve.sem_inc(msg_ready, SU)
            dve.sem_inc(added, 2)
            dve.memset(acc[:], 0.0).then_inc(cleared, 1)
            dve.memset(A[:, ET, :], 0.0).then_inc(cleared, 1)
            dve.wait_ge(cleared, 2)

            def mark(s, u, b):
                t = tile_of(nc, s, b)
                dve.wait_ge(made, s + 1)
                one_hot(dve, env, oh[:, u % OH_SLOTS, :], s, t).then_inc(oh_ready, 1)

            def weigh(s, u, turn, b):
                t = tile_of(nc, s, b, ET + 1)
                dve.wait_ge(landed[u % SU], turn * 16 + 16)
                dve.wait_ge(made, s + 1)
                a = tile(A, t).unsqueeze(2).to_broadcast([P, H0, HD0])
                dve.tensor_tensor(msg[:, u % OH_SLOTS, 0:D].rearrange("p (h c) -> p h c", h=H0),
                                  rows[:, u % SU, :].rearrange("p (h c) -> p h c", h=H0), a, ALU.mult).then_inc(msg_ready, 1)

            for u in range(OH_LEAD):
                mark(u, u, 0)
            weigh(0, 0, 0, 0)
            with dve.Fori(0, STEPS // SU) as i:
                b = blocks_of(nc, dve, env, i * SU, SU + 4)
                for u in range(SU):
                    s = i * SU + u
                    mark(s + OH_LEAD, u + OH_LEAD, b[u + OH_LEAD])
                    weigh(s + 1, u + 1, i + (u + 1) // SU, b[u + 1])
                    dve.wait_ge(made, s + 1 + OH_SLOTS)
                    dve.wait_ge(added, s + 2)
                    dve.tensor_tensor(tile(acc, b[u]), tile(acc, b[u]), pa[:, u % 2, 0:W], ALU.add).then_inc(added, 1)


def turn_groups(nc, ident, groups, source, dest):
    with ExitStack() as ctx:
        xs = ctx.enter_context(nc.sbuf_tensor(fresh("tg_x"), [P, U, P], F32))
        ps = ctx.enter_context(nc.psum_tensor(fresh("tg_ps"), [P, U, 512], F32))
        fetched = ctx.enter_context(nc.semaphore("tg_fetched"))
        turned = ctx.enter_context(nc.semaphore("tg_turned"))
        copied = ctx.enter_context(nc.semaphore("tg_copied"))
        block = ctx.enter_context(nc.Block())

        @block.gpsimd
        def _(pool):
            pool.sem_inc(turned, U)
            with pool.Fori(0, groups // U) as i:
                for u in range(U):
                    src = source(i * U + u)
                    out = xs[:, u, :]
                    if len(src.shape) == 3:
                        out = out.rearrange("p (a b) -> p a b", a=src.shape[1])
                    pool.wait_ge(turned, i * U + u + 1)
                    pool.tensor_copy(out, src).then_inc(fetched, 1)

        @block.tensor
        def _(pe):
            with pe.Fori(0, groups // U) as i:
                for u in range(U):
                    pe.wait_ge(fetched, i * U + u + 1)
                    pe.wait_ge(copied, i * U + u + 1)
                    pe.transpose(ps[:, u, 0:P], xs[:, u, :], ident[:]).then_inc(turned, 1)

        @block.vector
        def _(dve):
            dve.sem_inc(copied, U)
            with dve.Fori(0, groups // U) as i:
                for u in range(U):
                    dst = dest(i * U + u)
                    src = ps[:, u, 0:P]
                    if len(dst.shape) == 3:
                        src = src.rearrange("p (a b) -> p a b", a=dst.shape[1])
                    dve.wait_ge(turned, i * U + u + 1 + U)
                    dve.tensor_copy(dst, src).then_inc(copied, 1)


def segment_exp(nc, env, d, logits):
    L = logits[:, 0:LW].rearrange("p (j g h) -> p j g h", j=CH, h=H0)
    group = lambda g: L[:, :, bass.ds(g, 1), :].rearrange("p j a h -> p j (a h)")
    with ExitStack() as ctx:
        row = ctx.enter_context(nc.sbuf_tensor(fresh("x_row"), [P, ROW], F32))
        cut = [ctx.enter_context(nc.sbuf_tensor(fresh(n), [P, ROW], BF16)) for n in ("x_first", "x_last")]
        turn_groups(nc, env["ident"], CT, group, lambda g: row[:, bass.ds(g * P, P)])
        dsts = logits[:, 0:ROW + 2].bitcast(I32)
        run = logits[:, 0:ROW]

        with ExitStack() as ctx2:
            loaded = ctx2.enter_context(nc.semaphore("x_loaded"))
            chain_sem = ctx2.enter_context(nc.semaphore("x_chain"))
            block = ctx2.enter_context(nc.Block())

            @block.sync
            def _(sp):
                for j in range(CH):
                    sp.dma_start(dsts[j * H0:(j + 1) * H0, :],
                                 d["dst_line"][j * ROW:(j + 1) * ROW + 2].partition_broadcast(H0)).then_inc(loaded, 16)
                sp.wait_ge(loaded, 16 * CH)

            @block.vector
            def _(dve):
                link = Chain(dve, chain_sem)
                dve.wait_ge(loaded, 16 * CH)
                for c, other in zip(cut, (0, 2)):
                    link(dve.tensor_tensor(c[:], dsts[:, 1:ROW + 1], dsts[:, other:other + ROW], ALU.not_equal))
                    link(dve.tensor_scalar(c[:], c[:], NEG, None, ALU.mult))

        for c, data, way in ((cut[0], row, 1), (cut[1], None, -1)):
            segment_max(nc, env, c, data[:] if way == 1 else run, run, way)

        with ExitStack() as ctx2:
            shifted = ctx2.enter_context(nc.semaphore("x_shifted"))
            raised = ctx2.enter_context(nc.semaphore("x_raised"))
            block = ctx2.enter_context(nc.Block())

            @block.vector
            def _(dve):
                dve.tensor_tensor(row[:], row[:], run, ALU.subtract).then_inc(shifted, 1)

            @block.scalar
            def _(act):
                act.wait_ge(shifted, 1)
                act.activation(row[:], row[:], ACT.Exp).then_inc(raised, 1)
                act.wait_ge(raised, 1)
        turn_groups(nc, env["ident"], CT, lambda g: row[:, bass.ds(g * P, P)], group)


def segment_max(nc, env, cut, data, run, way):
    order = slice(None, None, way)
    PIECES = U
    PIECE = ROW // PIECES
    with ExitStack() as ctx:
        whole = ctx.enter_context(nc.sbuf_tensor(fresh("m_whole"), [P, 4], F32))
        part = ctx.enter_context(nc.sbuf_tensor(fresh("m_part"), [P, PIECE], F32))
        line = ctx.enter_context(nc.sbuf_tensor(fresh("m_line"), [1, 4, P + H0], F32))
        ps = ctx.enter_context(nc.psum_tensor(fresh("m_ps"), [P, 4, 512], F32))
        chain_sem = ctx.enter_context(nc.semaphore("m_chain"))
        ends_ready = ctx.enter_context(nc.semaphore("m_ends"))
        turned = ctx.enter_context(nc.semaphore("m_turned"))
        carries = ctx.enter_context(nc.semaphore("m_carries"))
        placed = ctx.enter_context(nc.semaphore("m_placed"))
        block = ctx.enter_context(nc.Block())
        end = PIECE - 1 if way == 1 else 0

        @block.vector
        def _(dve):
            link = Chain(dve, chain_sem)
            link(dve.tensor_reduce(whole[:, 1:2], cut[:], AX.X, ALU.min))
            link(dve.memset(line[:], NEG))
            link(dve.memset(whole[:, 0:1], NEG))
            for n in range(PIECES)[::way]:
                a, b = n * PIECE, (n + 1) * PIECE
                link(dve.tensor_tensor_scan(part[:, order], cut[:, a:b][:, order], data[:, a:b][:, order],
                                            whole[:, 0:1], ALU.add, ALU.max))
                link(dve.tensor_copy(whole[:, 0:1], part[:, end:end + 1]))
            dve.drain().then_inc(ends_ready, 1)
            dve.wait_ge(turned, 1)
            link(dve.tensor_copy(line[:, 0, 0:P], ps[0:1, 0, 0:P]))
            link(dve.tensor_copy(line[:, 1, 0:P], ps[0:1, 1, 0:P]))
            for h in range(H0):
                ends = line[:, 0, h:P:H0][:, order]
                cuts = line[:, 1, h:P:H0][:, order]
                out = (line[:, 2, h + H0:P + H0:H0] if way == 1 else line[:, 3, h:P:H0])[:, order]
                ins = dve.tensor_tensor_scan(out, cuts, ends, NEG, ALU.add, ALU.max)
                link(ins)
            dve.drain().then_inc(carries, 1)
            dve.wait_ge(placed, 1)
            link(dve.tensor_copy(whole[:, 2:3], ps[:, 2, 0:1]))
            link(dve.tensor_tensor_scan(run[:, order], cut[:, order], data[:, order], whole[:, 2:3], ALU.add, ALU.max))

        @block.tensor
        def _(pe):
            pe.wait_ge(ends_ready, 1)
            pe.transpose(ps[0:1, 0, 0:P], whole[:, 0:1], env["ident"][:])
            pe.transpose(ps[0:1, 1, 0:P], whole[:, 1:2], env["ident"][:]).then_inc(turned, 1)
            pe.wait_ge(carries, 1)
            src = line[:, 2, 0:P] if way == 1 else line[:, 3, H0:P + H0]
            pe.transpose(ps[:, 2, 0:1], src, env["ident"][0:1, 0:1]).then_inc(placed, 1)


BT = 8
NB2 = ET2 // BT
HALVES = 2
OHW = NT * RW
GC = GN // 2


def leaky(dve, out, z):
    return dve.scalar_tensor_tensor(out, z, 0.2, z, ALU.mult, ALU.max)


def finish_attention(nc, env, d, acc, x, x1n):
    with ExitStack() as ctx:
        den = ctx.enter_context(nc.sbuf_tensor(fresh("f_den"), [P, 2, NT, H0], F32))
        w = ctx.enter_context(nc.sbuf_tensor(fresh("f_wo"), [P, KC, D], F32))
        load_all(nc, [(w[:], d["woT"].rearrange("(k p) m -> p k m", p=P))])
        load_nodes(nc, x, d["x"])
        with nc.semaphore("f_chain") as chain_sem, nc.Block() as block:
            @block.vector
            def _(dve):
                link = Chain(dve, chain_sem)
                sums = acc[:, :, D:D + H0]
                link(dve.tensor_scalar(den[:, 0], sums, 0.0, None, ALU.is_equal))
                link(dve.tensor_tensor(den[:, 1], den[:, 0], sums, ALU.add))
                link(dve.reciprocal(den[:, 0], den[:, 1]))
                for h in range(H0):
                    part = acc[:, :, h * HD0:(h + 1) * HD0]
                    ins = dve.tensor_tensor(part, part, den[:, 0, :, h:h + 1].to_broadcast([P, NT, HD0]), ALU.mult)
                link(ins)
        project_tiles(nc, acc[:, :, 0:D], w, env["ident"],
                      lambda dve, out, t: dve.tensor_tensor(tile(x, t), tile(x, t), out[:, 0:D], ALU.add))


def routing_tables(nc, env, d, x1n, h20, dtab):
    with ExitStack() as ctx:
        w = ctx.enter_context(nc.sbuf_tensor(fresh("r_w"), [P, KC, HR16], F32))
        att = ctx.enter_context(nc.sbuf_tensor(fresh("r_att"), [P, 2, HR16], F32))
        prod = ctx.enter_context(nc.sbuf_tensor(fresh("r_prod"), [P, NT, HR16], F32))
        top = ctx.enter_context(nc.sbuf_tensor(fresh("r_top"), [P, 2, HR], F32))
        load_all(nc, [(w[:], d["w_gat"].rearrange("(k p) m -> p k m", p=P)),
                      (att[:, 0, :], d["att_src"].partition_broadcast(P)),
                      (att[:, 1, :], d["att_dst"].partition_broadcast(P))])
        project_tiles(nc, x1n, w, env["ident"],
                      lambda dve, out, t: dve.tensor_copy(tile(h20[:, :, 0:HR16], t), out[:, 0:HR16]))
        with ExitStack() as ctx2:
            chain_sem = ctx2.enter_context(nc.semaphore("r_chain"))
            topped = ctx2.enter_context(nc.semaphore("r_topped"))
            spread = ctx2.enter_context(nc.semaphore("r_spread"))
            tabled = ctx2.enter_context(nc.semaphore("r_tabled"))
            stored = ctx2.enter_context(nc.semaphore("r_stored"))
            block = ctx2.enter_context(nc.Block())

            @block.vector
            def _(dve):
                link = Chain(dve, chain_sem)
                for n, out in enumerate((h20[:, :, HR16:RW], dtab[:, :, 0:HR])):
                    link(dve.tensor_tensor(prod[:], h20[:, :, 0:HR16], att[:, n, :].unsqueeze(1).to_broadcast([P, NT, HR16]), ALU.mult))
                    link(dve.tensor_reduce(out, prod[:].rearrange("p t (h e) -> p t h e", h=HR), AX.X, ALU.add))
                dve.tensor_reduce(top[:, 0, :], h20[:, :, HR16:RW].rearrange("p t h -> p h t"), AX.X, ALU.max).then_inc(topped, 1)
                dve.wait_ge(spread, 1)
                link(dve.tensor_tensor(prod[:, :, 0:HR], dtab[:, :, 0:HR], top[:, 1, :].unsqueeze(1).to_broadcast([P, NT, HR]), ALU.add))
                leaky(dve, dtab[:, :, HR:2 * HR], prod[:, :, 0:HR]).then_inc(tabled, 1)

            @block.gpsimd
            def _(pool):
                pool.wait_ge(topped, 1)
                pool.partition_all_reduce(top[:, 1, :], top[:, 0, :], P, bass.bass_isa.ReduceOp.max).then_inc(spread, 1)

            @block.sync
            def _(sp):
                sp.wait_ge(tabled, 1)
                sp.dma_start(d["h_tab"].rearrange("(t p) w -> p t w", p=P), h20[:]).then_inc(stored, 16)
                sp.dma_start(d["d_tab"].rearrange("(t p) w -> p t w", p=P), dtab[:]).then_inc(stored, 16)
                sp.wait_ge(stored, 32)


def routing_sums(nc, env, d, sums):
    with ExitStack() as ctx:
        def sb(name, shape, dt=F32):
            return ctx.enter_context(nc.sbuf_tensor(fresh(name), shape, dt))

        def sem(name):
            return ctx.enter_context(nc.semaphore(name))
        ends = sb("g_ends", [P, ET2 + HALVES * BT, 2], I32)
        bits = sb("g_bits", [P, 2, ET2], I32)
        lowhigh = sb("g_lowhigh", [P, 2, ET2])
        idx = sb("g_idx", [P, HALVES, BT, 2], I32)
        hrow = sb("g_hrow", [P, HALVES, BT, RW])
        drow = sb("g_drow", [P, HALVES, BT, 2 * HR])
        score = sb("g_score", [P, HALVES, BT, HR])
        value = sb("g_value", [P, HALVES, BT, RW])
        low = sb("g_low", [P, HALVES, BT, P])
        high = sb("g_high", [P, HALVES, BT, NT])
        spread = sb("g_spread", [P, 4, NT, RW])
        zero = sb("g_zero", [P, OHW // 2])
        ps = ctx.enter_context(nc.psum_tensor(fresh("g_ps"), [P, 2, 512], F32))
        loaded, prepared, chain_sem, zeroed = sem("g_loaded"), sem("g_prepared"), sem("g_chain"), sem("g_zeroed")
        idx_ready, rows_used, shifted, exped = sem("g_idx"), sem("g_used"), sem("g_shifted"), sem("g_exped")
        landed = [sem(f"g_landed{n}") for n in range(HALVES)]
        spread_ready, multiplied, done = sem("g_spread"), sem("g_mult"), sem("g_done")
        block = ctx.enter_context(nc.Block())

        @block.sync
        def _(sp):
            sp.dma_start(ends[:], d["ends2"]).then_inc(loaded, 16)

        @block.gpsimd
        def _(pool):
            with pool.Fori(0, NB2 // HALVES) as i:
                for n in range(HALVES):
                    k = i * HALVES + n
                    pool.wait_ge(idx_ready, k + 1)
                    pool.wait_ge(rows_used, k + 1)
                    pool.nop(nofuse=True)
                    for u in range(BT):
                        gather_rows(pool, d["h_tab"], hrow[:, n, u, :], idx[:, n, u, 0:1], landed[n])
                        gather_rows(pool, d["d_tab"], drow[:, n, u, :], idx[:, n, u, 1:2], landed[n])

        @block.scalar
        def _(act):
            act.wait_ge(prepared, 1)
            for n in range(HALVES):
                act.copy(idx[:, n], ends[:, n * BT:(n + 1) * BT, :]).then_inc(idx_ready, 1)
            with act.Fori(0, NB2 // HALVES) as i:
                for n in range(HALVES):
                    k = i * HALVES + n
                    act.wait_ge(shifted, k + 1)
                    act.activation(value[:, n, :, HR16:RW], score[:, n], ACT.Exp).then_inc(exped, 1)
                    act.wait_ge(landed[n], (i + 1) * (16 * 2 * BT))
                    act.copy(idx[:, n], ends[:, bass.ds((k + HALVES) * BT, BT), :]).then_inc(idx_ready, 1)

        @block.tensor
        def _(pe):
            pe.wait_ge(zeroed, 1)
            for a in range(2):
                pe.matmul(ps[:, a, 0:OHW // 2], zero[:, 0:P], zero[:], start=True, stop=False)
            with pe.Fori(0, NB2 // HALVES) as i:
                for n in range(HALVES):
                    for u in range(BT):
                        m = (i * HALVES + n) * BT + u
                        pe.wait_ge(spread_ready, m + 1)
                        for a in range(2):
                            ins = pe.matmul(ps[:, a, 0:OHW // 2], low[:, n, u, :],
                                            spread[:, u % 4].rearrange("p b w -> p (b w)")[:, a * (OHW // 2):(a + 1) * (OHW // 2)],
                                            start=False, stop=False)
                        ins.then_inc(multiplied, 1)
            for a in range(2):
                ins = pe.matmul(ps[:, a, 0:OHW // 2], zero[:, 0:P], zero[:], start=False, stop=True)
            ins.then_inc(done, 1)

        @block.vector
        def _(dve):
            link = Chain(dve, chain_sem)
            dve.sem_inc(rows_used, HALVES)
            dve.sem_inc(multiplied, BT + 4)
            dve.memset(zero[:], 0.0).then_inc(zeroed, 1)
            dve.wait_ge(loaded, 16)
            link(dve.tensor_scalar(bits[:, 0, :], ends[:, 0:ET2, 1], P - 1, None, ALU.bitwise_and))
            link(dve.tensor_scalar(bits[:, 1, :], ends[:, 0:ET2, 1], 7, None, ALU.logical_shift_right))
            link(dve.tensor_copy(lowhigh[:], bits[:]))
            link(dve.tensor_scalar(ends[:], ends[:], float(N - 1), None, ALU.min))
            dve.drain().then_inc(prepared, 1)
            with dve.Fori(0, NB2 // HALVES) as i:
                for n in range(HALVES):
                    k = i * HALVES + n
                    t = k * BT
                    dve.wait_ge(landed[n], (i + 1) * (16 * 2 * BT))
                    dve.wait_ge(multiplied, t + 4)
                    dve.tensor_tensor(score[:, n], hrow[:, n, :, HR16:RW], drow[:, n, :, 0:HR], ALU.add).then_inc(chain_sem, 1)
                    dve.wait_ge(chain_sem, k * 2 + 5)
                    leaky(dve, score[:, n], score[:, n]).then_inc(chain_sem, 1)
                    dve.wait_ge(chain_sem, k * 2 + 6)
                    dve.tensor_tensor(score[:, n], score[:, n], drow[:, n, :, HR:2 * HR], ALU.subtract).then_inc(shifted, 1)
                    dve.tensor_tensor(low[:, n], env["iota"][:].unsqueeze(1).to_broadcast([P, BT, P]),
                                      bc(lowhigh[:, 0, bass.ds(t, BT)], [P, BT, P]), ALU.is_equal)
                    dve.tensor_tensor(high[:, n], env["iota"][:, 0:NT].unsqueeze(1).to_broadcast([P, BT, NT]),
                                      bc(lowhigh[:, 1, bass.ds(t, BT)], [P, BT, NT]), ALU.is_equal)
                    dve.wait_ge(exped, k + 1)
                    dve.tensor_tensor(value[:, n, :, 0:HR16].rearrange("p u (h e) -> p u h e", h=HR),
                                      hrow[:, n, :, 0:HR16].rearrange("p u (h e) -> p u h e", h=HR),
                                      bc(value[:, n, :, HR16:RW], [P, BT, HR, NX]), ALU.mult).then_inc(rows_used, 1)
                    dve.wait_ge(rows_used, k + 1 + HALVES)
                    for u in range(BT):
                        dve.wait_ge(multiplied, t + u + 1 + BT)
                        dve.tensor_tensor(spread[:, u % 4], high[:, n, u, :].unsqueeze(2).to_broadcast([P, NT, RW]),
                                          value[:, n, u, :].unsqueeze(1).to_broadcast([P, NT, RW]), ALU.mult).then_inc(spread_ready, 1)
            dve.wait_ge(done, 1)
            flat = sums[:].rearrange("p b w -> p (b w)")
            for a in range(2):
                dve.tensor_copy(flat[:, a * (OHW // 2):(a + 1) * (OHW // 2)], ps[:, a, 0:OHW // 2])


def routing_gates(nc, env, d, h20, dtab, sums, gates):
    T = [P, NT, HR]
    with ExitStack() as ctx:
        def sb(name, shape, dt=F32):
            return ctx.enter_context(nc.sbuf_tensor(fresh(name), shape, dt))
        z = sb("t_z", [P, NT, HR])
        p = sb("t_p", [P, NT, HR])
        loop = sb("t_loop", [P, NT, HR16])
        agg = sb("t_agg", [P, NT, HR16])
        score = sb("t_score", [P, NT, NX])
        rank = sb("t_rank", [P, NT, NX])
        cmp = sb("t_cmp", [P, NT])
        one = sb("t_one", [P, 2, NT])
        rows = sb("t_rows", [P, 3, HR16])
        load_all(nc, [(rows[:, 0, :], d["b_gat"].partition_broadcast(P)),
                      (rows[:, 1, :], d["ln_gamma"].partition_broadcast(P)),
                      (rows[:, 2, :], d["ln_beta"].partition_broadcast(P))])
        with ExitStack() as ctx2:
            chain_sem = ctx2.enter_context(nc.semaphore("t_chain"))
            ready = ctx2.enter_context(nc.semaphore("t_ready"))
            exped = ctx2.enter_context(nc.semaphore("t_exped"))
            block = ctx2.enter_context(nc.Block())

            @block.vector
            def _(dve):
                link = Chain(dve, chain_sem)
                link(dve.tensor_tensor(z[:], h20[:, :, HR16:RW], dtab[:, :, 0:HR], ALU.add))
                link(leaky(dve, z[:], z[:]))
                dve.tensor_tensor(z[:], z[:], dtab[:, :, HR:2 * HR], ALU.subtract).then_inc(ready, 1)
                dve.wait_ge(exped, 1)
                link(dve.tensor_tensor(loop[:].rearrange("p t (h e) -> p t h e", h=HR),
                                       h20[:, :, 0:HR16].rearrange("p t (h e) -> p t h e", h=HR),
                                       bc(p[:], [P, NT, HR, NX]), ALU.mult))
                link(dve.tensor_tensor(loop[:], loop[:], sums[:, :, 0:HR16], ALU.add))
                link(dve.tensor_tensor(p[:], p[:], sums[:, :, HR16:RW], ALU.add))
                link(dve.tensor_scalar(p[:], p[:], 1e-16, None, ALU.add))
                link(dve.reciprocal(z[:], p[:]))
                link(dve.tensor_tensor(agg[:].rearrange("p t (h e) -> p t h e", h=HR),
                                       loop[:].rearrange("p t (h e) -> p t h e", h=HR),
                                       bc(z[:], [P, NT, HR, NX]), ALU.mult))
                link(dve.tensor_tensor(agg[:], agg[:], rows[:, 0, :].unsqueeze(1).to_broadcast([P, NT, HR16]), ALU.add))

            @block.scalar
            def _(act):
                act.wait_ge(ready, 1)
                act.activation(p[:], z[:], ACT.Exp).then_inc(exped, 1)

        layernorm(nc, agg[:], agg[:], loop[:], rows[:, 1, :], rows[:, 2, :])
        with ExitStack() as ctx2:
            chain_sem = ctx2.enter_context(nc.semaphore("t_chain2"))
            ready = ctx2.enter_context(nc.semaphore("t_ready2"))
            exped = ctx2.enter_context(nc.semaphore("t_exped2"))
            block = ctx2.enter_context(nc.Block())

            @block.vector
            def _(dve):
                link = Chain(dve, chain_sem)
                link(dve.tensor_reduce(score[:], agg[:].rearrange("p t (h e) -> p t e h", h=HR), AX.X, ALU.add))
                link(dve.tensor_scalar(score[:], score[:], 1.0 / HR, None, ALU.mult))
                link(dve.memset(rank[:], 0.0))
                for e in range(NX):
                    for o in range(NX):
                        if o != e:
                            link(dve.tensor_tensor(cmp[:], score[:, :, o], score[:, :, e], ALU.is_ge if o < e else ALU.is_gt))
                            link(dve.tensor_tensor(rank[:, :, e], rank[:, :, e], cmp[:], ALU.add))
                link(dve.tensor_scalar(rank[:], rank[:], 2.0, None, ALU.is_lt))
                link(dve.tensor_reduce(one[:, 0, :], score[:], AX.X, ALU.max))
                dve.tensor_tensor(score[:], score[:], bc(one[:, 0, :], [P, NT, NX]), ALU.subtract).then_inc(ready, 1)
                dve.wait_ge(exped, 1)
                link(dve.tensor_tensor(z[:], z[:], rank[:], ALU.mult))
                link(dve.tensor_reduce(one[:, 0, :], z[:], AX.X, ALU.add))
                link(dve.reciprocal(one[:, 1, :], one[:, 0, :]))
                link(dve.tensor_tensor(gates[:], z[:], bc(one[:, 1, :], [P, NT, NX]), ALU.mult))

            @block.scalar
            def _(act):
                act.wait_ge(ready, 1)
                act.activation(z[:], score[:], ACT.Exp).then_inc(exped, 1)


def expert_ffn(nc, xT, gates, x, w1, b1, w2, b2, experts, shared, func=ACT.Gelu, route=None, stream=None):
    HC = w2.shape[1] // experts
    layers = 1 if shared else experts
    HS, OS = 2, 4
    with ExitStack() as ctx:
        hT = ctx.enter_context(nc.sbuf_tensor(fresh("ff_hT"), [P, HC, GN], F32))
        biased = ctx.enter_context(nc.sbuf_tensor(fresh("ff_out"), [P, 2, D], F32))
        ph = ctx.enter_context(nc.psum_tensor(fresh("ff_ph"), [P, HS, 512], F32))
        po = ctx.enter_context(nc.psum_tensor(fresh("ff_po"), [P, OS, 512], F32))
        h_made = ctx.enter_context(nc.semaphore("ff_h_made"))
        h_ready = ctx.enter_context(nc.semaphore("ff_h_ready"))
        o_made = ctx.enter_context(nc.semaphore("ff_o_made"))
        o_used = ctx.enter_context(nc.semaphore("ff_o_used"))
        added = ctx.enter_context(nc.semaphore("ff_added"))
        x_loaded = ctx.enter_context(nc.semaphore("ff_x_loaded"))
        x_stored = ctx.enter_context(nc.semaphore("ff_x_stored"))
        r_made = ctx.enter_context(nc.semaphore("ff_r_made"))
        r_shifted = ctx.enter_context(nc.semaphore("ff_r_shifted"))
        r_exped = ctx.enter_context(nc.semaphore("ff_r_exped"))
        r_chain = ctx.enter_context(nc.semaphore("ff_r_chain"))
        if route:
            wg, bg, countdown = route
            pr = ctx.enter_context(nc.psum_tensor(fresh("ff_pr"), [P, 512], F32))
            lg = ctx.enter_context(nc.sbuf_tensor(fresh("ff_lg"), [P, 4, U, NE], F32))
            one = ctx.enter_context(nc.sbuf_tensor(fresh("ff_one"), [P, 3, U], F32))
        block = ctx.enter_context(nc.Block())
        per = experts // layers
        NH = layers * HC * 2
        NO = experts * U
        assert NH % HS == 0
        before = [m - OS if m >= OS else max(b for b in range(NO) if b % OS == m) - NO for m in range(NO)]

        @block.tensor
        def _(pe):
            with pe.Fori(0, GROUPS) as g:
                for layer in range(layers):
                    for c in range(HC):
                        for half in range(2):
                            n = (layer * HC + c) * 2 + half
                            pe.wait_ge(h_ready, g * NH + n + 1)
                            for k in range(KC):
                                ins = pe.matmul(ph[:, n % HS, 0:GC], w1[:, k, (layer * HC + c) * P:(layer * HC + c + 1) * P],
                                                xT[:, k, bass.ds(g * GN + half * GC, GC)], start=(k == 0), stop=(k == KC - 1))
                            ins.then_inc(h_made, 1)
                    if route:
                        pe.wait_ge(h_ready, g * NH + (layer + 1) * HC * 2 + HS)
                        pe.wait_ge(r_shifted, g + 1)
                        for u in range(U):
                            for c in range(HC):
                                ins = pe.matmul(pr[:, u * NE:(u + 1) * NE], hT[:, c, u * P:(u + 1) * P], wg[:, c, :],
                                                start=(c == 0), stop=(c == HC - 1))
                        ins.then_inc(r_made, 1)
                    for e in range(layer * per, (layer + 1) * per):
                        for u in range(U):
                            m = e * U + u
                            pe.wait_ge(h_ready, g * NH + (layer + 1) * HC * 2 + HS)
                            pe.wait_ge(o_used, g * NO + before[m] + 1 + NO)
                            for c in range(HC):
                                ins = pe.matmul(po[:, m % OS, 0:D], hT[:, c, u * P:(u + 1) * P], w2[:, e * HC + c, :],
                                                start=(c == 0), stop=(c == HC - 1))
                            ins.then_inc(o_made, 1)

        @block.scalar
        def _(act):
            act.sem_inc(h_ready, HS)
            act.sem_inc(o_made, NO)
            with act.Fori(0, GROUPS) as g:
                for layer in range(layers):
                    act.wait_ge(o_made, g * NO + layer * per * U + NO)
                    for c in range(HC):
                        for half in range(2):
                            n = (layer * HC + c) * 2 + half
                            act.wait_ge(h_made, g * NH + n + 1)
                            act.activation(hT[:, c, half * GC:(half + 1) * GC], ph[:, n % HS, 0:GC], func,
                                           bias=b1[:, layer * HC + c:layer * HC + c + 1]).then_inc(h_ready, 1)
                    if route:
                        act.wait_ge(r_shifted, g + 2)
                        act.activation(lg[:, 2], lg[:, 1], ACT.Exp).then_inc(r_exped, 1)

        @block.vector
        def _(dve):
            dve.sem_inc(o_used, NO)
            dve.sem_inc(added, 2)
            dve.sem_inc(r_shifted, 1)
            with dve.Fori(0, GROUPS) as g:
                if route:
                    full = [P, U, NE]
                    steps = Steps(dve, r_chain, g, 7)
                    dve.wait_ge(r_made, g + 1)
                    steps(dve.tensor_tensor(lg[:, 0], pr[:, 0:U * NE].rearrange("p (u e) -> p u e", e=NE),
                                            bg.unsqueeze(1).to_broadcast(full), ALU.add))
                    steps(dve.tensor_reduce(one[:, 0, :], lg[:, 0], AX.X, ALU.max))
                    dve.tensor_tensor(lg[:, 1], lg[:, 0], bc(one[:, 0, :], full), ALU.subtract).then_inc(r_shifted, 1)
                    dve.wait_ge(r_exped, g * 2 + 1)
                    steps(dve.tensor_reduce(one[:, 1, :], lg[:, 2], AX.X, ALU.add))
                    steps(dve.scalar_tensor_tensor(lg[:, 0].rearrange("p u e -> p (u e)"), lg[:, 1].rearrange("p u e -> p (u e)"), 0.0,
                                                   countdown, ALU.is_equal, ALU.mult))
                    steps(dve.tensor_reduce(one[:, 0, :], lg[:, 0], AX.X, ALU.max))
                    steps(dve.reciprocal(one[:, 2, :], one[:, 1, :]))
                    steps(dve.tensor_tensor(lg[:, 3], lg[:, 0], bc(one[:, 0, :], full), ALU.is_equal))
                    dve.tensor_tensor(gates[:, bass.ds(g * U, U), :], lg[:, 3], bc(one[:, 2, :], full), ALU.mult).then_inc(r_exped, 1)
                    dve.wait_ge(r_exped, g * 2 + 2)
                if stream:
                    dve.wait_ge(x_loaded, g * 16 + 16)
                for e in range(experts):
                    for u in range(U):
                        m = e * U + u
                        t = g * U + u
                        xt = x[:, u, :] if stream else tile(x, t)
                        dve.wait_ge(o_made, g * NO + m + 1 + NO)
                        dve.wait_ge(added, g * NO + m + 1 + (NO % 2 if m == 0 else 0))
                        dve.tensor_tensor(biased[:, m % 2, :], po[:, m % OS, 0:D], b2[:, e, :], ALU.add).then_inc(o_used, 1)
                        dve.wait_ge(o_used, g * NO + m + 1 + NO)
                        dve.scalar_tensor_tensor(xt, biased[:, m % 2, :], tile(gates[:, :, e:e + 1], t), xt,
                                                 ALU.mult, ALU.add).then_inc(added, 1)

        if stream:
            @block.sync
            def _(sp):
                with sp.Fori(0, GROUPS) as g:
                    sp.dma_start(x[:], rows_of(stream[0])[:, bass.ds(g * U, U), :]).then_inc(x_loaded, 16)
                    sp.wait_ge(added, g * NO + NO + 2)
                    sp.nop(nofuse=True)
                    sp.dma_start(rows_of(stream[1])[:, bass.ds(g * U, U), :], x[:]).then_inc(x_stored, 16)
                    sp.wait_ge(x_stored, g * 16 + 16)
                    sp.nop(nofuse=True)


def degrees(nc, env, d, key):
    with ExitStack() as ctx:
        def sb(name, shape, dt=F32):
            return ctx.enter_context(nc.sbuf_tensor(fresh(name), shape, dt))

        def sem(name):
            return ctx.enter_context(nc.semaphore(name))
        bits = sb("n_bits", [P, 2, ETX], I32)
        parts = sb("n_parts", [P, 2, ETX + SU])
        noise = sb("n_noise", [P, NT])
        low = sb("n_low", [P, 2, SU, P], BF16)
        high = sb("n_high", [P, 2, SU, NT], BF16)
        zero = sb("n_zero", [P, P], BF16)
        ps = ctx.enter_context(nc.psum_tensor(fresh("n_ps"), [P, 512], F32))
        loaded, zeroed, chain_sem, marked, counted, done = (
            sem("n_loaded"), sem("n_zeroed"), sem("n_chain"), sem("n_marked"), sem("n_counted"), sem("n_done"))
        block = ctx.enter_context(nc.Block())
        turns = ETX // SU

        @block.sync
        def _(sp):
            sp.dma_start(noise[:], d["noise_cols"]).then_inc(loaded, 16)

        @block.vector
        def _(dve):
            link = Chain(dve, chain_sem)
            dve.sem_inc(counted, 2)
            dve.memset(zero[:], 0.0).then_inc(zeroed, 1)
            link(dve.tensor_scalar(bits[:, 0, :], env["src"][:], P - 1, None, ALU.bitwise_and))
            link(dve.tensor_scalar(bits[:, 1, :], env["src"][:], 7, None, ALU.logical_shift_right))
            link(dve.memset(parts[:, :, ETX:], float(PAD_DST)))
            link(dve.tensor_copy(parts[:, :, 0:ETX], bits[:]))
            with dve.Fori(0, turns // 2 + 1) as i:
                for n in range(2):
                    k = i * 2 + n
                    dve.wait_ge(counted, k + 1)
                    t = k * SU
                    dve.tensor_tensor(low[:, n], env["iota"][:].unsqueeze(1).to_broadcast([P, SU, P]),
                                      bc(parts[:, 0, bass.ds(t, SU)], [P, SU, P]), ALU.is_equal)
                    dve.tensor_tensor(high[:, n], env["iota"][:, 0:NT].unsqueeze(1).to_broadcast([P, SU, NT]),
                                      bc(parts[:, 1, bass.ds(t, SU)], [P, SU, NT]), ALU.is_equal).then_inc(marked, 1)
            dve.wait_ge(done, 1)
            dve.wait_ge(loaded, 16)
            link(dve.tensor_tensor(key[:], ps[:, 0:NT], noise[:], ALU.add))

        @block.tensor
        def _(pe):
            pe.wait_ge(zeroed, 1)
            pe.matmul(ps[:, 0:NT], zero[:], zero[:, 0:NT], start=True, stop=False)
            with pe.Fori(0, turns // 2 + 1) as i:
                for n in range(2):
                    k = i * 2 + n
                    pe.wait_ge(marked, k + 1)
                    for u in range(SU):
                        ins = pe.matmul(ps[:, 0:NT], low[:, n, u, :], high[:, n, u, :], start=False, stop=False)
                    ins.then_inc(counted, 1)
            pe.matmul(ps[:, 0:NT], zero[:], zero[:, 0:NT], start=False, stop=True).then_inc(done, 1)


def ranks(nc, env, d, key, rank):
    with ExitStack() as ctx:
        def sb(name, shape, dt=F32):
            return ctx.enter_context(nc.sbuf_tensor(fresh(name), shape, dt))

        def sem(name):
            return ctx.enter_context(nc.semaphore(name))
        keys = sb("k_keys", [P, NP])
        earlier = sb("k_earlier", [P, 2 * NP], BF16)
        trash = sb("k_trash", [P, 2, NP], BF16)
        col = sb("k_col", [P, 1])
        part = sb("k_part", [P, 2, NT])
        counted = sem("k_counted")
        stored, loaded, col_ready, chain_sem = sem("k_stored"), sem("k_loaded"), sem("k_col"), sem("k_chain")
        block = ctx.enter_context(nc.Block())

        @block.sync
        def _(sp):
            sp.dma_start(d["key_line"].rearrange("(t p) -> p t", p=P), key[:], allow_slow_non_contiguous=True).then_inc(stored, 16)
            sp.wait_ge(stored, 16)
            sp.dma_start(keys[:], d["key_line"].partition_broadcast(P)).then_inc(loaded, 16)

        @block.gpsimd
        def _(pool):
            pool.iota(col[:], pattern=[[0, 1]], base=0, channel_multiplier=1,
                      allow_small_or_imprecise_dtypes=True).then_inc(col_ready, 1)

        @block.vector
        def _(dve):
            link = Chain(dve, chain_sem)
            link(dve.memset(earlier[:, 0:NP], 1.0))
            link(dve.memset(earlier[:, NP:2 * NP], 0.0))
            dve.wait_ge(col_ready, 1)
            link(dve.tensor_scalar(earlier[:, NP:NP + P], env["iota"][:], col[:], None, ALU.is_lt))
            dve.wait_ge(loaded, 16)
            dve.sem_inc(counted, 2)
            with dve.Fori(0, NT) as t:
                k = key[:, bass.ds(t, 1)]
                dve.wait_ge(counted, t * 2 + 1)
                dve.scalar_tensor_tensor(trash[:, 0, :], keys[:], k, earlier[:, bass.ds(NP - t * P, NP)],
                                         ALU.is_equal, ALU.mult, accum_out=part[:, 0, bass.ds(t, 1)]).then_inc(counted, 1)
                dve.wait_ge(counted, t * 2 + 2)
                dve.tensor_scalar(trash[:, 1, :], keys[:], k, None, ALU.is_lt, ALU.add,
                                  accum_out=part[:, 1, bass.ds(t, 1)]).then_inc(counted, 1)
            dve.wait_ge(counted, 2 * NT + 2)
            link(dve.tensor_tensor(part[:, 0, :], part[:, 0, :], part[:, 1, :], ALU.add))
            link(dve.tensor_copy(rank[:], part[:, 0, :]))


def move_rows(nc, env, rank, table, buf, gather):
    with ExitStack() as ctx:
        slot = ctx.enter_context(nc.sbuf_tensor(fresh("v_slot"), [P, U, D], F32))
        idx = ctx.enter_context(nc.sbuf_tensor(fresh("v_idx"), [P, U], I32))
        idx_ready = ctx.enter_context(nc.semaphore("v_idx"))
        slot_ready = ctx.enter_context(nc.semaphore("v_slot"))
        group_moved = ctx.enter_context(nc.semaphore("v_group"))
        moved = [ctx.enter_context(nc.semaphore(f"v_moved{u}")) for u in range(U)]
        block = ctx.enter_context(nc.Block())

        @block.vector
        def _(dve):
            if gather:
                dve.sem_inc(slot_ready, U)
            else:
                dve.sem_inc(group_moved, 1)
            with dve.Fori(0, GROUPS) as g:
                if gather:
                    dve.wait_ge(slot_ready, g * U + U)
                    dve.tensor_copy(idx[:], rank[:, bass.ds(g * U, U)]).then_inc(idx_ready, 1)
                    for u in range(U):
                        dve.wait_ge(moved[u], g * 16 + 16)
                        dve.tensor_copy(tile(buf, g * U + u), slot[:, u, :]).then_inc(slot_ready, 1)
                else:
                    dve.wait_ge(group_moved, g + 1)
                    dve.tensor_copy(idx[:], rank[:, bass.ds(g * U, U)]).then_inc(idx_ready, 1)
                    for u in range(U):
                        dve.tensor_copy(slot[:, u, :], tile(buf, g * U + u)).then_inc(slot_ready, 1)

        @block.gpsimd
        def _(pool):
            with pool.Fori(0, GROUPS) as g:
                pool.wait_ge(idx_ready, g + 1)
                pool.nop(nofuse=True)
                for u in range(U):
                    if gather:
                        gather_rows(pool, table, slot[:, u, :], idx[:, u:u + 1], moved[u])
                    else:
                        pool.wait_ge(slot_ready, g * U + u + 1)
                        pool.nop(nofuse=True)
                        pool.indirect_dma_start(table, bass.IndirectOffsetOnAxis(ap=idx[:, u:u + 1], axis=0),
                                                slot[:, u, :], None).then_inc(moved[u], 16)
                if not gather:
                    for u in range(U):
                        pool.wait_ge(moved[u], g * 16 + 16)
                    pool.sem_inc(group_moved, 1)


def attention_tables(nc, env, d, x2n, rows, tgt):
    with ExitStack() as ctx:
        w = ctx.enter_context(nc.sbuf_tensor(fresh("o_w"), [P, KC, D], F32))
        att = ctx.enter_context(nc.sbuf_tensor(fresh("o_att"), [P, 2, D], F32))
        top = ctx.enter_context(nc.sbuf_tensor(fresh("o_top"), [P, 2, H1], F32))
        z = ctx.enter_context(nc.sbuf_tensor(fresh("o_z"), [P, NT, H1], F32))
        load_all(nc, [(w[:], d["gat_wT"].rearrange("(k p) m -> p k m", p=P)),
                      (att[:, 0, :], d["gat_a_src"].partition_broadcast(P)),
                      (att[:, 1, :], d["gat_a_tgt"].partition_broadcast(P))])
        project_tiles(nc, x2n, w, env["ident"],
                      lambda dve, out, t: dve.tensor_copy(tile(rows[:, :, 0:D], t), out[:, 0:D]))
        chain_sem = ctx.enter_context(nc.semaphore("o_chain"))
        topped = ctx.enter_context(nc.semaphore("o_topped"))
        spread = ctx.enter_context(nc.semaphore("o_spread"))
        stored = ctx.enter_context(nc.semaphore("o_stored"))
        block = ctx.enter_context(nc.Block())

        @block.vector
        def _(dve):
            link = Chain(dve, chain_sem)
            for n, out in enumerate((rows[:, :, D:PW], tgt[:, :, 0:H1])):
                link(dve.tensor_tensor(x2n[:], rows[:, :, 0:D], att[:, n, :].unsqueeze(1).to_broadcast([P, NT, D]), ALU.mult))
                link(dve.tensor_reduce(out, x2n[:].rearrange("p t (h c) -> p t h c", h=H1), AX.X, ALU.add))
            dve.tensor_reduce(top[:, 0, :], rows[:, :, D:PW].rearrange("p t h -> p h t"), AX.X, ALU.max).then_inc(topped, 1)
            link(dve.memset(tgt[:, :, 2 * H1:TW], 1.0))
            dve.wait_ge(spread, 1)
            link(dve.tensor_tensor(z[:], tgt[:, :, 0:H1], top[:, 1, :].unsqueeze(1).to_broadcast([P, NT, H1]), ALU.add))
            link(leaky(dve, tgt[:, :, H1:2 * H1], z[:]))

        @block.gpsimd
        def _(pool):
            pool.wait_ge(topped, 1)
            pool.partition_all_reduce(top[:, 1, :], top[:, 0, :], P, bass.bass_isa.ReduceOp.max).then_inc(spread, 1)

        @block.sync
        def _(sp):
            sp.wait_ge(topped, 1)
            sp.dma_start(rows_of(d["proj_tab"]), rows[:]).then_inc(stored, 16)
            sp.wait_ge(stored, 16)


def second_attention(nc, env, d, tgt, acc, top):
    HB = 4
    NB = STEPS // SU
    with ExitStack() as ctx:
        def sb(name, shape, dt=F32):
            return ctx.enter_context(nc.sbuf_tensor(fresh(name), shape, dt))

        def sem(name):
            return ctx.enter_context(nc.semaphore(name))

        def banks(name, n):
            return ctx.enter_context(nc.psum_tensor(fresh(name), [P, n, 512], F32))
        idx = sb("h_idx", [P, 2, SU], I32)
        rows = sb("h_rows", [P, 2, SU, PW])
        msg = sb("h_msg", [P, 2, SU, PW])
        oh = sb("h_oh", [P, 2, SU, P])
        ohT = sb("h_ohT", [P, SU, P])
        z = sb("h_z", [P, SU, H1])
        e = sb("h_e", [P, 2, SU, H1])
        valid = sb("h_valid", [P, SU])
        best = sb("h_best", [P, SU, H1])
        pT, pS, pa = banks("h_pT", 2), banks("h_pS", 1), banks("h_pa", 4)
        idx_ready, oh_ready, turned, ohT_ready = sem("h_idx"), sem("h_oh"), sem("h_turned"), sem("h_ohT")
        sides, used, shifted, exped = sem("h_sides"), sem("h_used"), sem("h_shifted"), sem("h_exped")
        msg_ready, made, added, chain_sem, best_sem = (
            sem("h_msg"), sem("h_made"), sem("h_added"), sem("h_chain"), sem("h_best"))
        landed = [sem(f"h_landed{n}") for n in range(2)]
        block = ctx.enter_context(nc.Block())

        @block.gpsimd
        def _(pool):
            def fetch(n):
                for u in range(SU):
                    gather_rows(pool, d["proj_tab"], rows[:, n, u, :], idx[:, n, u:u + 1], landed[n])

            pool.wait_ge(idx_ready, 1)
            fetch(0)
            with pool.Fori(0, NB // 2) as i:
                for n in (1, 0):
                    k = i * 2 + (1 if n else 2)
                    pool.wait_ge(idx_ready, k + 1)
                    pool.wait_ge(msg_ready, k)
                    pool.nop(nofuse=True)
                    fetch(n)

        @block.scalar
        def _(act):
            def turn_copies(k):
                for a in range(2):
                    act.wait_ge(turned, k * 2 + a + 1)
                    if a == 0:
                        act.wait_ge(sides, k + 1)
                    act.copy(ohT[:, a * HB:(a + 1) * HB, :], pT[:, a, :].rearrange("p (u n) -> p u n", u=HB)).then_inc(ohT_ready, 1)

            def exps(k, n):
                act.wait_ge(shifted, k + 1)
                act.wait_ge(made, k * SU + 1)
                act.activation(msg[:, n, :, D:PW], e[:, 1], ACT.Exp).then_inc(exped, 1)

            def indices(k, n, b):
                for u in range(SU):
                    t = tile_of(nc, k * SU + u, b[u])
                    ins = act.copy(idx[:, n, u:u + 1], env["src"][:, bass.ds(t, 1)])
                ins.then_inc(idx_ready, 1)

            act.copy(idx[:, 0, :], env["src"][:, 0:SU]).then_inc(idx_ready, 1)
            b = blocks_of(nc, act, env, SU, SU)
            indices(1, 1, b)
            turn_copies(0)
            exps(0, 0)
            with act.Fori(0, NB // 2) as i:
                for n in (1, 0):
                    k = i * 2 + (1 if n else 2)
                    b = blocks_of(nc, act, env, (k + 1) * SU, SU)
                    act.wait_ge(landed[1 - n], (i + 1) * 16 * SU)
                    indices(k + 1, 1 - n, b)
                    turn_copies(k)
                    exps(k, n)

        @block.tensor
        def _(pe):
            def turns(k, n):
                pe.wait_ge(oh_ready, k + 1)
                for a in range(2):
                    pe.wait_ge(ohT_ready, k * 2 + a + 1)
                    for u in range(HB):
                        ins = pe.transpose(pT[:, a, u * P:(u + 1) * P], oh[:, n, a * HB + u, :], env["ident"][:])
                    ins.then_inc(turned, 1)

            def dst_sides(k, b):
                pe.wait_ge(ohT_ready, k * 2 + 4)
                pe.wait_ge(used, k + 1)
                for u in range(SU):
                    ins = pe.matmul(pS[:, 0, u * TW:(u + 1) * TW], ohT[:, u, :], tile(tgt, b[u]), start=True, stop=True)
                ins.then_inc(sides, 1)

            b = blocks_of(nc, pe, env, 0, SU)
            turns(0, 0)
            dst_sides(0, b)
            with pe.Fori(0, NB // 2) as i:
                for n in (1, 0):
                    k = i * 2 + (1 if n else 2)
                    b = blocks_of(nc, pe, env, k * SU, SU)
                    pe.wait_ge(msg_ready, k + 1)
                    for u in range(SU):
                        pe.wait_ge(added, (k - 1) * SU + u + 1)
                        pe.matmul(pa[:, u % 4, 0:PW], oh[:, 1 - n, u, :], msg[:, 1 - n, u, :],
                                  start=True, stop=True).then_inc(made, 1)
                    turns(k, n)
                    dst_sides(k, b)

        @block.vector
        def _(dve):
            def one_hots(k, n, b):
                for u in range(SU):
                    s = k * SU + u
                    ins = one_hot(dve, env, oh[:, n, u, :], s, s if b is None else tile_of(nc, s, b[u]))
                ins.then_inc(oh_ready, 1)

            def messages(k, n, rounds):
                steps = Steps(dve, chain_sem, k, 3)
                dve.wait_ge(landed[n], rounds * 16 * SU)
                dve.wait_ge(sides, k + 2)
                side = pS[:, 0, 0:SU * TW].rearrange("p (u w) -> p u w", w=TW)
                dve.tensor_scalar(valid[:], side[:, :, 2 * H1], -1.0, -NEG, ALU.add, ALU.mult)
                steps(dve.tensor_tensor(z[:], rows[:, n, :, D:PW], side[:, :, 0:H1], ALU.add))
                steps(leaky(dve, e[:, 0], z[:]))
                dve.tensor_tensor(e[:, 1], e[:, 0], side[:, :, H1:2 * H1], ALU.subtract).then_inc(shifted, 1)
                steps(dve.tensor_tensor(z[:], e[:, 0], bc(valid[:], [P, SU, H1]), ALU.add))
                dve.tensor_tensor(best[:], best[:], z[:], ALU.max).then_inc(used, 1)
                dve.wait_ge(exped, k + 1)
                dve.tensor_tensor(msg[:, n, :, 0:D].rearrange("p u (h c) -> p u h c", h=H1),
                                  rows[:, n, :, 0:D].rearrange("p u (h c) -> p u h c", h=H1),
                                  bc(msg[:, n, :, D:PW], [P, SU, H1, HD1]), ALU.mult).then_inc(msg_ready, 1)

            dve.sem_inc(msg_ready, 1)
            dve.sem_inc(ohT_ready, 2)
            dve.sem_inc(sides, 1)
            dve.sem_inc(used, 1)
            dve.sem_inc(added, 4)
            dve.sem_inc(made, SU + 1)
            dve.memset(acc[:], 0.0).then_inc(best_sem, 1)
            dve.memset(best[:], NEG).then_inc(best_sem, 1)
            dve.wait_ge(best_sem, 2)
            one_hots(0, 0, None)
            messages(0, 0, 1)
            with dve.Fori(0, NB // 2) as i:
                for n in (1, 0):
                    k = i * 2 + (1 if n else 2)
                    b = blocks_of(nc, dve, env, (k - 1) * SU, 2 * SU)
                    dve.wait_ge(made, (k - 1) * SU + SU + 1)
                    one_hots(k, n, b[SU:])
                    for u in range(SU):
                        s = (k - 1) * SU + u
                        dve.wait_ge(made, s + 1 + SU + 1)
                        dve.wait_ge(added, s + 4)
                        dve.tensor_tensor(tile(acc, b[u]), tile(acc, b[u]), pa[:, u % 4, 0:PW], ALU.add).then_inc(added, 1)
                    messages(k, n, i + 1 if n else i + 2)
            dve.drain().then_inc(best_sem, 1)
            dve.wait_ge(best_sem, 3)
            dve.tensor_reduce(top[:, 0:1], best[:].rearrange("p u h -> p (u h)"), AX.X, ALU.max).then_inc(best_sem, 1)


TC = GN // 2
CHUNKS = NP // TC
LOG_SMALL = 2.0 ** -6


def mamba(nc, env, d, xT):
    with ExitStack() as ctx:
        def sb(name, shape, dt=F32):
            return ctx.enter_context(nc.sbuf_tensor(fresh(name), shape, dt))

        def sem(name):
            return ctx.enter_context(nc.semaphore(name))
        w_in = sb("b_win", [P, KC, 2 * D])
        w_x = sb("b_wx", [P, KC, DTR + 2 * DS])
        w_dt = sb("b_wdt", [DTR, D])
        col = sb("b_col", [P, 3, KC])
        conv = sb("b_conv", [P, KC, CONV])
        A = sb("b_A", [P, KC, DS])
        xc = sb("b_xc", [P, KC, TC + CONV - 1])
        cv = sb("b_cv", [P, KC, TC])
        z = sb("b_z", [P, KC, TC])
        dbc = sb("b_dbc", [DTR + 2 * DS, TC])
        mag = sb("b_mag", [P, KC, TC])
        u = sb("b_u", [P, KC, TC])
        lg = sb("b_lg", [P, KC, TC])
        small = sb("b_small", [P, KC, TC])
        ser = sb("b_ser", [P, KC, TC])
        dt = sb("b_dt", [P, KC, TC])
        du = sb("b_du", [P, KC, TC])
        dA = sb("b_dA", [P, 2, KC, TC])
        dB = sb("b_dB", [P, 2, KC, TC])
        hs = sb("b_hs", [P, 2, KC, TC])
        Cs = sb("b_Cs", [P, 2, TC])
        hC = sb("b_hC", [P, 2, KC, TC])
        state = sb("b_state", [P, DS, KC])
        y = sb("b_y", [P, KC, TC])
        ps = ctx.enter_context(nc.psum_tensor(fresh("b_ps"), [P, 8, 512], F32))
        loaded, ready, chain_sem = sem("b_loaded"), sem("b_ready"), sem("b_chain")
        in_made, in_read, conved, siluc, dbc_made, dbc_copied, dt_made = (
            sem("b_in_made"), sem("b_in_read"), sem("b_conved"), sem("b_siluc"), sem("b_dbcm"), sem("b_dbcc"), sem("b_dtm"))
        act_dt, du_ready, y_done = sem("b_act_dt"), sem("b_du"), sem("b_ydone")
        bc_made, c_copied, dA_ready, dB_ready, scanned, hC_ready, y_added = (
            sem("b_bcm"), sem("b_cc"), sem("b_dA"), sem("b_dB"), sem("b_scan"), sem("b_hC"), sem("b_yadd"))
        block = ctx.enter_context(nc.Block())
        NDBC = DTR + 2 * DS
        LOADS = 8
        DVE_STEPS = 22

        @block.sync
        def _(sp):
            for dst, src in [(w_in[:], d["in_wT"].rearrange("(k p) m -> p k m", p=P)),
                             (w_x[:], d["x_wT"].rearrange("(k p) m -> p k m", p=P)),
                             (w_dt[:], d["dt_wT"]), (conv[:], d["conv_w"].rearrange("(k p) m -> p k m", p=P)),
                             (A[:], d["A_log"].rearrange("(k p) m -> p k m", p=P)),
                             (col[:, 0, :], d["conv_b"]),
                             (col[:, 1, :], d["dt_b"]),
                             (col[:, 2, :], d["D_param"])]:
                sp.dma_start(dst, src).then_inc(loaded, 16)

        @block.tensor
        def _(pe):
            pe.wait_ge(loaded, 16 * LOADS)
            with pe.Fori(0, CHUNKS) as g:
                pe.wait_ge(y_done, g + 1)
                for m in range(4):
                    for k in range(KC):
                        ins = pe.matmul(ps[:, m, 0:TC], w_in[:, k, m * P:(m + 1) * P], xT[:, k, bass.ds(g * TC, TC)],
                                        start=(k == 0), stop=(k == KC - 1))
                ins.then_inc(in_made, 1)
                pe.wait_ge(siluc, g * 2 + 1)
                for k in range(KC):
                    ins = pe.matmul(ps[0:NDBC, 4, 0:TC], w_x[:, k, :], cv[:, k, :], start=(k == 0), stop=(k == KC - 1))
                ins.then_inc(dbc_made, 1)
                pe.wait_ge(dbc_copied, g + 1)
                for k in range(KC):
                    ins = pe.matmul(ps[:, 5 + k, 0:TC], w_dt[:, k * P:(k + 1) * P], dbc[0:DTR, :], start=True, stop=True)
                ins.then_inc(dt_made, 1)

                def add_y(n):
                    pe.wait_ge(hC_ready, g * DS + n + 1 + 2)
                    for k in range(KC):
                        ins = pe.matmul(ps[:, k, 0:TC], env["ident"][:], hC[:, n % 2, k, :],
                                        start=(n == 0), stop=(n == DS - 1))
                    ins.then_inc(y_added, 1)

                for n in range(DS):
                    if n < 2:
                        pe.wait_ge(act_dt, g * 2 + 1)
                        pe.wait_ge(siluc, g * 2 + 2)
                    pe.wait_ge(dB_ready, g * DS + n + 1)
                    pe.wait_ge(c_copied, g * DS + n + 1)
                    for bank, row in ((2 + n % 2, DTR + n), (4 + n % 2, DTR + DS + n)):
                        ins = pe.matmul(ps[:, bank, 0:TC], env["ident"][0:NDBC, row:row + 1].to_broadcast([NDBC, P]), dbc[:],
                                        start=True, stop=True)
                    ins.then_inc(bc_made, 1)
                    if n:
                        add_y(n - 1)
                add_y(DS - 1)

        @block.scalar
        def _(act):
            act.sem_inc(dA_ready, 1)
            act.sem_inc(c_copied, 2)
            act.wait_ge(loaded, 16 * LOADS)
            act.activation(A[:], A[:], ACT.Exp).then_inc(ready, 1)
            act.wait_ge(ready, 1)
            act.mul(A[:], A[:], -1.0).then_inc(ready, 1)
            act.wait_ge(ready, 2)
            with act.Fori(0, CHUNKS) as g:
                act.wait_ge(in_made, g + 1)
                act.copy(xc[:, :, CONV - 1:], ps[:, 0:2, 0:TC]).then_inc(in_read, 1)
                act.wait_ge(conved, g + 1)
                act.activation(cv[:], cv[:], ACT.Silu).then_inc(siluc, 1)
                act.activation(z[:], ps[:, 2:4, 0:TC], ACT.Silu).then_inc(siluc, 1)
                act.wait_ge(dbc_made, g + 1)
                act.copy(dbc[:], ps[0:NDBC, 4, 0:TC]).then_inc(dbc_copied, 1)
                act.wait_ge(dt_made, g + 1)
                for k in range(KC):
                    act.activation(mag[:, k, :], ps[:, 5 + k, 0:TC], ACT.Abs, bias=col[:, 1, k:k + 1])
                for k in range(KC):
                    ins = act.activation(dt[:, k, :], ps[:, 5 + k, 0:TC], ACT.Relu, bias=col[:, 1, k:k + 1])
                ins.then_inc(act_dt, 1)
                act.wait_ge(act_dt, g * 2 + 1)
                act.activation(u[:], mag[:], ACT.Exp, scale=-1.0).then_inc(ready, 1)
                act.wait_ge(ready, g + 3)
                act.activation(lg[:], u[:], ACT.Ln, bias=1.0).then_inc(act_dt, 1)
                act.wait_ge(du_ready, g + 1)
                for n in range(DS):
                    act.wait_ge(scanned, g * DS + n + 1)
                    for k in range(KC):
                        ins = act.activation(dA[:, n % 2, k, :], dt[:, k, :], ACT.Exp, scale=A[:, k, n:n + 1])
                    ins.then_inc(dA_ready, 1)
                    act.wait_ge(bc_made, g * DS + n + 1)
                    act.wait_ge(hC_ready, g * DS + n + 1)
                    act.copy(Cs[:, n % 2, :], ps[:, 4 + n % 2, 0:TC]).then_inc(c_copied, 1)

        @block.gpsimd
        def _(pool):
            pool.sem_inc(y_added, 2)
            pool.sem_inc(hC_ready, 2)
            with pool.Fori(0, CHUNKS) as g:
                for n in range(DS):
                    m = g * DS + n
                    pool.wait_ge(scanned, m + 1 + 2)
                    pool.wait_ge(c_copied, m + 1 + 2)
                    pool.wait_ge(y_added, m + 1)
                    for k in range(KC):
                        ins = pool.tensor_tensor(hC[:, n % 2, k, :], hs[:, n % 2, k, :], Cs[:, n % 2, :], ALU.mult)
                    ins.then_inc(hC_ready, 1)

        @block.vector
        def _(dve):
            dve.sem_inc(y_done, 1)
            dve.sem_inc(dB_ready, 2)
            dve.sem_inc(scanned, 2)
            link = Chain(dve, chain_sem)
            link(dve.memset(state[:], 0.0))
            link(dve.memset(xc[:, :, 0:CONV - 1], 0.0))
            dve.wait_ge(loaded, 16 * LOADS)
            with dve.Fori(0, CHUNKS) as g:
                steps = Steps(dve, chain_sem, g, DVE_STEPS)
                steps.n = link.n
                dve.wait_ge(in_read, g + 1)
                for k in range(KC):
                    steps(dve.tensor_scalar(cv[:, k, :], xc[:, k, 0:TC], conv[:, k, 0:1], col[:, 0, k:k + 1], ALU.mult, ALU.add))
                    for j in range(1, CONV):
                        steps(dve.scalar_tensor_tensor(cv[:, k, :], xc[:, k, j:j + TC], conv[:, k, j:j + 1], cv[:, k, :], ALU.mult, ALU.add))
                dve.tensor_copy(small[:, :, 0:CONV - 1], xc[:, :, TC:TC + CONV - 1]).then_inc(conved, 1)
                dve.wait_ge(conved, g + 1)
                steps(dve.tensor_copy(xc[:, :, 0:CONV - 1], small[:, :, 0:CONV - 1]))
                dve.wait_ge(act_dt, g * 2 + 2)
                steps(dve.tensor_scalar(small[:], u[:], LOG_SMALL, None, ALU.is_lt))
                steps(dve.tensor_scalar(ser[:], u[:], -0.25, 1.0 / 3.0, ALU.mult, ALU.add))
                steps(dve.tensor_tensor(ser[:], ser[:], u[:], ALU.mult))
                steps(dve.scalar_tensor_tensor(ser[:], ser[:], -0.5, u[:], ALU.add, ALU.mult))
                steps(dve.scalar_tensor_tensor(ser[:], ser[:], 1.0, u[:], ALU.add, ALU.mult))
                steps(dve.tensor_tensor(ser[:], ser[:], lg[:], ALU.subtract))
                steps(dve.tensor_tensor(ser[:], ser[:], small[:], ALU.mult))
                steps(dve.tensor_tensor(ser[:], ser[:], lg[:], ALU.add))
                steps(dve.tensor_tensor(dt[:], dt[:], ser[:], ALU.add))
                steps(dve.tensor_tensor(du[:], dt[:], cv[:], ALU.mult))
                dve.sem_inc(du_ready, 1)

                for n in range(DS):
                    m = g * DS + n
                    dve.wait_ge(bc_made, m + 1)
                    dve.tensor_tensor(dB[:, n % 2], du[:], ps[:, 2 + n % 2, 0:TC].unsqueeze(1).to_broadcast([P, KC, TC]),
                                      ALU.mult).then_inc(dB_ready, 1)
                    dve.wait_ge(dB_ready, m + 1 + 2)
                    dve.wait_ge(dA_ready, m + 2)
                    dve.wait_ge(hC_ready, m + 1)
                    for k in range(KC):
                        ins = dve.tensor_tensor_scan(hs[:, n % 2, k, :], dA[:, n % 2, k, :], dB[:, n % 2, k, :],
                                                     state[:, n, k:k + 1], ALU.mult, ALU.add)
                    ins.then_inc(scanned, 1)
                    dve.wait_ge(scanned, m + 1 + 2)
                    dve.tensor_copy(state[:, n, :], hs[:, n % 2, :, TC - 1])
                dve.wait_ge(y_added, g * DS + DS + 2)
                for k in range(KC):
                    steps(dve.scalar_tensor_tensor(y[:, k, :], cv[:, k, :], col[:, 2, k:k + 1], ps[:, k, 0:TC], ALU.mult, ALU.add))
                steps(dve.tensor_tensor(xT[:, :, bass.ds(g * TC, TC)], y[:], z[:], ALU.mult))
                assert steps.n == link.n + DVE_STEPS, steps.n - link.n
                dve.sem_inc(y_done, 1)


def local_and_global(nc, env, d, acc, x, other, top):
    with ExitStack() as ctx:
        rows = ctx.enter_context(nc.sbuf_tensor(fresh("l_rows"), [P, 5, D], F32))
        eps = ctx.enter_context(nc.sbuf_tensor(fresh("l_eps"), [P, NT, H1], F32))
        bound = ctx.enter_context(nc.sbuf_tensor(fresh("l_bound"), [P, NT, H1], F32))
        best = ctx.enter_context(nc.sbuf_tensor(fresh("l_best"), [P, 1], F32))
        load_all(nc, [(rows[:, n, :], d[name].partition_broadcast(P)) for n, name in
                      enumerate(["gat_b", "ln_local_g", "ln_local_b", "ln_global_g", "ln_global_b"])] +
                 [(bound[:], d["bound_tab"].rearrange("(t p) w -> p t w", p=P))])
        with ExitStack() as ctx2:
            chain_sem = ctx2.enter_context(nc.semaphore("l_chain"))
            spread = ctx2.enter_context(nc.semaphore("l_spread"))
            shifted = ctx2.enter_context(nc.semaphore("l_shifted"))
            exped = ctx2.enter_context(nc.semaphore("l_exped"))
            block = ctx2.enter_context(nc.Block())

            @block.gpsimd
            def _(pool):
                pool.partition_all_reduce(best[:], top[:, 0:1], P, bass.bass_isa.ReduceOp.max).then_inc(spread, 1)

            @block.vector
            def _(dve):
                link = Chain(dve, chain_sem)
                dve.wait_ge(spread, 1)
                dve.tensor_scalar(eps[:], bound[:], best[:], -1.0, ALU.subtract, ALU.mult).then_inc(shifted, 1)
                dve.wait_ge(exped, 1)
                link(dve.scalar_tensor_tensor(eps[:], eps[:], 1e-16, acc[:, :, D:PW], ALU.mult, ALU.add))
                link(dve.reciprocal(bound[:], eps[:]))
                for h in range(H1):
                    part = acc[:, :, h * HD1:(h + 1) * HD1]
                    ins = dve.tensor_tensor(part, part, bound[:, :, h:h + 1].to_broadcast([P, NT, HD1]), ALU.mult)
                link(ins)
                hl = acc[:, :, 0:D]
                link(dve.tensor_tensor(hl, hl, x[:], ALU.add))
                link(dve.tensor_tensor(hl, hl, rows[:, 0, :].unsqueeze(1).to_broadcast([P, NT, D]), ALU.add))
                dve.tensor_scalar(other[:], hl, 0.0, None, ALU.min).then_inc(shifted, 1)
                dve.wait_ge(exped, 2)
                link(dve.scalar_tensor_tensor(hl, hl, 0.0, other[:], ALU.max, ALU.add))
                link(dve.tensor_scalar(hl, hl, -1.0, None, ALU.add))

            @block.scalar
            def _(act):
                act.wait_ge(shifted, 1)
                act.activation(eps[:], eps[:], ACT.Exp).then_inc(exped, 1)
                act.wait_ge(shifted, 2)
                act.activation(other[:], other[:], ACT.Exp).then_inc(exped, 1)
        layernorm(nc, acc[:, :, 0:D], acc[:, :, 0:D], other[:], rows[:, 1, :], rows[:, 2, :])
        move_rows(nc, env, env["rank"], d["y_tab"], other, True)
        with nc.semaphore("l_add") as added, nc.Block() as block:
            @block.vector
            def _(dve):
                dve.tensor_tensor(other[:], other[:], x[:], ALU.add).then_inc(added, 1)
                dve.wait_ge(added, 1)
        layernorm(nc, other[:], other[:], x[:], rows[:, 3, :], rows[:, 4, :])


def gate_and_mix(nc, env, d, acc, gate, other):
    with ExitStack() as ctx:
        w = ctx.enter_context(nc.sbuf_tensor(fresh("i_w"), [P, 2, KC, D], F32))
        load_all(nc, [(w[:, n], d[name].rearrange("(k p) m -> p k m", p=P)) for n, name in enumerate(("wlT", "wgT"))])
        project_tiles(nc, acc[:, :, 0:D], w[:, 0], env["ident"],
                      lambda dve, out, t: dve.tensor_copy(tile(gate, t), out[:, 0:D]))
        project_tiles(nc, other, w[:, 1], env["ident"],
                      lambda dve, out, t: dve.tensor_tensor(tile(gate, t), tile(gate, t), out[:, 0:D], ALU.add))
        with ExitStack() as ctx2:
            chain_sem = ctx2.enter_context(nc.semaphore("i_chain"))
            opened = ctx2.enter_context(nc.semaphore("i_opened"))
            block = ctx2.enter_context(nc.Block())

            @block.scalar
            def _(act):
                act.activation(gate[:], gate[:], ACT.Sigmoid).then_inc(opened, 1)

            @block.vector
            def _(dve):
                link = Chain(dve, chain_sem)
                hl = acc[:, :, 0:D]
                link(dve.tensor_tensor(hl, hl, other[:], ALU.subtract))
                dve.wait_ge(opened, 1)
                link(dve.tensor_tensor(hl, hl, gate[:], ALU.mult))
                link(dve.tensor_tensor(other[:], other[:], hl, ALU.add))




INTERNAL = [("q_tab", [NP, D], F32), ("k_tab", [NP, D], F32), ("v_tab", [NP, D], F32),
            ("h_tab", [NP, RW], F32), ("d_tab", [NP, 2 * HR], F32), ("x1_tab", [NP, D], F32), ("x1n_tab", [NP, D], F32), ("x2_tab", [NP, D], F32),
            ("x2n_tab", [NP, D], F32), ("proj_tab", [NP, PW], F32), ("bound_tab", [NP, H1], F32), ("key_line", [NP], F32),
            ("xs_tab", [NP, D], F32), ("y_tab", [NP, D], F32), ("agg_tab", [NP, PW], F32), ("x3_tab", [NP, D], F32)]


def flat_nodes(acc):
    return acc[:].rearrange("p t w -> p (t w)")[:, 0:NT * D].rearrange("p (t w) -> p t w", w=D)


def fill(nc, buf, value):
    with nc.semaphore("fill") as filled, nc.Block() as block:
        @block.vector
        def _(dve):
            dve.memset(buf[:], value).then_inc(filled, 1)
            dve.wait_ge(filled, 1)


def reset_semaphores(nc):
    free = sorted(nc.free_semaphores)
    with nc.Block() as block:
        @block.gpsimd
        def _(pool):
            start = free[0]
            for n, sem in enumerate(free):
                if n + 1 == len(free) or free[n + 1] != sem + 1:
                    pool.dma_reset(range(start, sem + 1))
                    pool.sem_clear(range(start, sem + 1))
                    start = free[n + 1] if n + 1 < len(free) else sem


def program(nc, d):
    NAMES.clear()
    for name, shape, dt in INTERNAL:
        d[name] = nc.dram_tensor(name, shape, dt, kind="Internal").ap()
    with ExitStack() as ctx:
        def keep(name, shape, dt=F32, stack=ctx):
            return stack.enter_context(nc.sbuf_tensor(name, shape, dt))
        ident = keep("ident", [P, P])
        iota = keep("iota", [P, P])
        env = {"ident": ident, "iota": iota}
        constants(nc, ident, iota)
        phase_qkv(nc, env, d)
        reset_semaphores(nc)
        gates = keep("gates", [P, NT, NE])
        ones = keep("ones", [P, NT, 1])
        top = keep("top", [P, 1])
        env["rank"] = keep("rank", [P, NT], I32)
        edges = ExitStack()
        for name, shape, dt in [("src", [P, ETX], I32), ("dst", [P, ETX], F32), ("dst_i", [P, ETX], I32),
                                ("base", [P, SL], F32), ("step_b", [P, SL], I32)]:
            env[name] = keep(name, shape, dt, edges)
        walk(nc, env, d)
        reset_semaphores(nc)
        with ExitStack() as first:
            h20 = keep("h20", [P, NT, RW], stack=first)
            dtab = keep("dtab", [P, NT, 2 * HR], stack=first)
            routing = ExitStack()
            with nc.sbuf_tensor("logits", [P, LW + H0], F32) as logits:
                load_all(nc, [(logits[:, 0:LW], d["bias_cols"].rearrange("p t h -> p (t h)"))])
                with nc.sbuf_tensor("q", [P, NT, D], F32) as q:
                    load_all(nc, [(q[:], rows_of(d["q_tab"]))])
                    edge_logits(nc, env, d, logits, q)
                segment_exp(nc, env, d, logits)
                acc = first.enter_context(nc.sbuf_tensor("acc", [P, NT, D + H0], F32, side="right"))
                edge_sums(nc, env, d, logits, acc)
            x = keep("x1", [P, NT, D], stack=routing)
            x1n = keep("x1n", [P, NT, D], stack=routing)
            reset_semaphores(nc)
            finish_attention(nc, env, d, acc, x, x1n)
            layernorm(nc, x[:], x1n[:], flat_nodes(acc))
            store_nodes(nc, [(d["x1_tab"], x), (d["x1n_tab"], x1n)])
            routing_tables(nc, env, d, x1n, h20, dtab)
            routing.close()
            sums = keep("sums", [P, NT, RW], stack=first)
            routing_sums(nc, env, d, sums)
            routing_gates(nc, env, d, h20, dtab, sums, gates[:, :, 0:NX])
        reset_semaphores(nc)
        with ExitStack() as ffn:
            x = keep("x1_again", [P, NT, D], stack=ffn)
            xT = keep("x1nT", [P, KC, NP], stack=ffn)
            with nc.sbuf_tensor("x1n_again", [P, NT, D], F32, side="right") as x1n:
                load_all(nc, [(x[:], rows_of(d["x1_tab"])), (x1n[:], rows_of(d["x1n_tab"]))])
                project_tiles(nc, x1n, None, ident, None, xT=xT)
            w1 = keep("f0_w1", [P, KC, NX * FH], stack=ffn)
            b1 = keep("f0_b1", [P, NX * FH // P], stack=ffn)
            w2 = keep("f0_w2", [P, NX * FH // P, D], stack=ffn)
            b2 = keep("f0_b2", [P, NX, D], stack=ffn)
            load_all(nc, [(w1[:], d["w1_0"].rearrange("(k p) m -> p k m", p=P)), (b1[:], d["b1_0"]),
                          (w2[:], d["w2_0"].rearrange("(c p) m -> p c m", p=P)),
                          (b2[:].rearrange("p e m -> p (e m)"), d["b2_0"].partition_broadcast(P))])
            expert_ffn(nc, xT, gates, x, w1, b1, w2, b2, NX, False)
            store_nodes(nc, [(d["x2_tab"], x)])
        reset_semaphores(nc)
        with ExitStack() as second:
            key = keep("key", [P, NT], stack=second)
            degrees(nc, env, d, key)
            ranks(nc, env, d, key, env["rank"])
            reset_semaphores(nc)
            tgt = keep("tgt", [P, NT, TW], stack=second)
            with nc.sbuf_tensor("x2", [P, NT, D], F32) as x, nc.sbuf_tensor("x2n", [P, NT, D], F32) as x2n:
                load_all(nc, [(x[:], rows_of(d["x2_tab"]))])
                with nc.sbuf_tensor("x2sq", [P, NT, D], F32) as squares:
                    layernorm(nc, x[:], x2n[:], squares[:])
                store_nodes(nc, [(d["x2n_tab"], x2n)])
                move_rows(nc, env, env["rank"], d["xs_tab"], x2n, False)
                with nc.sbuf_tensor("proj", [P, NT, PW], F32) as proj:
                    attention_tables(nc, env, d, x2n, proj, tgt)
            reset_semaphores(nc)
            store_nodes(nc, [(d["bound_tab"], tgt[:, :, H1:2 * H1])])
            acc = keep("acc1", [P, NT, PW], stack=second)
            second_attention(nc, env, d, tgt, acc, top)
            store_nodes(nc, [(d["agg_tab"], acc)])
        edges.close()
        reset_semaphores(nc)
        with ExitStack() as scan:
            xT = keep("xsT", [P, KC, NP], stack=scan)
            with nc.sbuf_tensor("xs", [P, NT, D], F32) as xs:
                load_all(nc, [(xs[:], rows_of(d["xs_tab"]))])
                project_tiles(nc, xs, None, ident, None, xT=xT)
            reset_semaphores(nc)
            mamba(nc, env, d, xT)
            w = keep("out_w", [P, KC, D], stack=scan)
            y = keep("y", [P, NT, D], stack=scan)
            load_all(nc, [(w[:], d["out_wT"].rearrange("(k p) m -> p k m", p=P))])
            project_tiles(nc, None, w, ident, lambda dve, out, t: dve.tensor_copy(tile(y, t), out[:, 0:D]), turned_src=xT)
            store_nodes(nc, [(d["y_tab"], y)])
        reset_semaphores(nc)
        with ExitStack() as last:
            a = keep("buf_a", [P, NT, PW], stack=last)
            b = keep("buf_b", [P, NT, D], stack=last)
            c = keep("buf_c", [P, NT, D], stack=last)
            b_turned = b[:].rearrange("p t d -> p (t d)").rearrange("p (k n) -> p k n", k=KC)
            load_all(nc, [(a[:], rows_of(d["agg_tab"])), (b[:], rows_of(d["x2n_tab"]))])
            local_and_global(nc, env, d, a, b, c, top)
            reset_semaphores(nc)
            gate_and_mix(nc, env, d, a, b, c)
            with ExitStack() as ffn:
                w1 = keep("f1_w1", [P, KC, 2 * D], stack=ffn)
                b1 = keep("f1_b1", [P, 2 * D // P], stack=ffn)
                w2 = keep("f1_w2", [P, 2 * D // P, D], stack=ffn)
                b2 = keep("f1_b2", [P, 1, D], stack=ffn)
                load_all(nc, [(w1[:], d["ff1_T"].rearrange("(k p) m -> p k m", p=P)), (b1[:], d["ff1_b"]),
                              (w2[:], d["ff2_T"].rearrange("(c p) m -> p c m", p=P)),
                              (b2[:, 0, :], d["ff2_b"].partition_broadcast(P))])
                fill(nc, ones, 1.0)
                project_tiles(nc, c, None, ident, None, xT=b_turned)
                expert_ffn(nc, b_turned, ones, c, w1, b1, w2, b2, 1, True, func=ACT.Relu)
            reset_semaphores(nc)
            rows = keep("ln2_rows", [P, 2, D], stack=last)
            load_all(nc, [(rows[:, n, :], d[name].partition_broadcast(P)) for n, name in enumerate(("ln2_g", "ln2_b"))])
            layernorm(nc, c[:], c[:], b[:], rows[:, 0, :], rows[:, 1, :])
            load_all(nc, [(b[:], rows_of(d["x2_tab"]))])
            with nc.semaphore("x3_add") as added, nc.Block() as block:
                @block.vector
                def _(dve):
                    dve.tensor_tensor(c[:], c[:], b[:], ALU.add).then_inc(added, 1)
                    dve.wait_ge(added, 1)
            store_nodes(nc, [(d["x3_tab"], c)])
        with ExitStack() as last:
            xT = keep("x3T", [P, KC, NP], stack=last)
            with nc.sbuf_tensor("x3", [P, NT, D], F32) as x, nc.sbuf_tensor("x3n", [P, NT, D], F32) as x3n:
                load_all(nc, [(x[:], rows_of(d["x3_tab"]))])
                layernorm(nc, x[:], x3n[:], xT[:].rearrange("p k n -> p (k n)").rearrange("p (t w) -> p t w", w=D))
                project_tiles(nc, x3n, None, ident, None, xT=xT)
            reset_semaphores(nc)
            w1 = keep("f2_w1", [P, KC, HID], stack=last)
            b1 = keep("f2_b1", [P, HID // P], stack=last)
            wg = keep("f2_wg", [P, HID // P, NE], stack=last)
            bg = keep("f2_bg", [P, NE], stack=last)
            b2 = keep("f2_b2", [P, NE, D], stack=last)
            countdown = keep("f2_count", [P, U * NE], stack=last)
            load_all(nc, [(w1[:], d["w1_1"].rearrange("(k p) m -> p k m", p=P)), (b1[:], d["b1_1"]),
                          (wg[:], d["wg_1"].rearrange("(c p) m -> p c m", p=P)), (bg[:], d["bg_1"].partition_broadcast(P)),
                          (b2[:].rearrange("p e m -> p (e m)"), d["bd_1"].partition_broadcast(P))])
            with nc.semaphore("countdown") as made, nc.Block() as block:
                @block.gpsimd
                def _(pool):
                    pool.iota(countdown[:], pattern=[[0, U], [-1, NE]], base=NE, channel_multiplier=0,
                              allow_small_or_imprecise_dtypes=True).then_inc(made, 1)
                    pool.wait_ge(made, 1)
            w2 = keep("f2_wd", [P, NE * HID // P, D], stack=last)
            load_all(nc, [(w2[:], d["wd_1"].rearrange("(c p) m -> p c m", p=P))])
            x = keep("x3_group", [P, U, D], stack=last)
            expert_ffn(nc, xT, gates, x, w1, b1, w2, b2, NE, True, route=(wg[:], bg[:], countdown[:]),
                       stream=(d["x3_tab"], d["out"]))


def edge_columns(a, pad, tiles=ETX):
    full = np.full((tiles * P,) + a.shape[1:], pad, a.dtype)
    full[:E] = a
    return np.ascontiguousarray(np.swapaxes(full.reshape((tiles, P) + a.shape[1:]), 0, 1))


def routing_columns(e):
    full = np.zeros((2, ET2 + HALVES * BT, P), e.dtype)
    full[:, :ET2] = e.reshape(2, ET2, P)
    return np.ascontiguousarray(full.transpose(2, 1, 0))


def node_columns(a, pad):
    full = np.full(NP, pad, a.dtype)
    full[:N] = a
    return np.ascontiguousarray(full.reshape(NT, P).T)


def T(a):
    return np.ascontiguousarray(a.T)


def layout(i):
    i = {k: np.asarray(v) for k, v in i.items()}
    dst = i["dst"]
    linear = np.full(ET * P + 2, PAD_DST, dst.dtype)
    linear[0] = PAD_DST
    linear[1:E + 1] = dst
    return {
        "x": i["x"],
        "wqkvT": np.ascontiguousarray(np.concatenate([i["L0_gnn_Wq"].T, i["L0_gnn_Wk"].T, i["L0_gnn_Wv"].T], 1)),
        "woT": np.ascontiguousarray(i["L0_gnn_Wo"].T),
        "tile_last": edge_columns(dst, PAD_DST)[P - 1].copy(),
        "src_cols": edge_columns(i["src"], NP - 1),
        "dst_cols": edge_columns(dst, PAD_DST),
        "bias_cols": edge_columns(i["edge_attr_8"], 0, ET),
        "dst_line": linear,
        "ends2": routing_columns(i["L0_ffn_edge_index"]),
        "w_gat": i["L0_ffn_W_gat"],
        "att_src": i["L0_ffn_att_src"].reshape(-1),
        "att_dst": i["L0_ffn_att_dst"].reshape(-1),
        "b_gat": i["L0_ffn_b_gat"],
        "ln_gamma": i["L0_ffn_ln_gamma"],
        "ln_beta": i["L0_ffn_ln_beta"],
        "w1_0": np.ascontiguousarray(i["L0_ffn_W1"].transpose(1, 0, 2).reshape(D, NX * FH)),
        "b1_0": np.ascontiguousarray(i["L0_ffn_b1"].reshape(NX * FH // P, P).T),
        "w2_0": i["L0_ffn_W2"].reshape(NX * FH, D),
        "b2_0": i["L0_ffn_b2"].reshape(-1),
        "noise_cols": node_columns(i["node_vec"], 3e38),
        "gat_wT": T(i["L1_gnn_gat_w"]),
        "gat_a_src": i["L1_gnn_gat_a_src"].reshape(-1),
        "gat_a_tgt": i["L1_gnn_gat_a_tgt"].reshape(-1),
        "gat_b": i["L1_gnn_gat_b"],
        "ln_local_g": i["L1_gnn_ln_local_g"],
        "ln_local_b": i["L1_gnn_ln_local_b"],
        "ln_global_g": i["L1_gnn_ln_global_g"],
        "ln_global_b": i["L1_gnn_ln_global_b"],
        "ln2_g": i["L1_gnn_ln2_g"],
        "ln2_b": i["L1_gnn_ln2_b"],
        "in_wT": T(i["L1_gnn_in_proj_w"]),
        "x_wT": T(i["L1_gnn_x_proj_w"]),
        "dt_wT": T(i["L1_gnn_dt_proj_w"]),
        "out_wT": T(i["L1_gnn_out_proj_w"]),
        "conv_w": i["L1_gnn_conv_w"],
        "conv_b": T(i["L1_gnn_conv_b"].reshape(KC, P)),
        "dt_b": T(i["L1_gnn_dt_proj_b"].reshape(KC, P)),
        "A_log": i["L1_gnn_A_log"],
        "D_param": T(i["L1_gnn_D_param"].reshape(KC, P)),
        "wlT": T(i["L1_gnn_wl"]),
        "wgT": T(i["L1_gnn_wg"]),
        "ff1_T": T(i["L1_gnn_ff1_w"]),
        "ff1_b": T(i["L1_gnn_ff1_b"].reshape(-1, P)),
        "ff2_T": T(i["L1_gnn_ff2_w"]),
        "ff2_b": i["L1_gnn_ff2_b"],
        "w1_1": i["L1_ffn_W1"],
        "b1_1": T(i["L1_ffn_b1"].reshape(-1, P)),
        "wg_1": i["L1_ffn_Wg"],
        "bg_1": i["L1_ffn_bg"],
        "wd_1": i["L1_ffn_Wd"].reshape(NE * HID, D),
        "bd_1": i["L1_ffn_bd"].reshape(-1),
    }


OUT_SHAPE = (NP, D)


def kernel(**inputs):
    import concourse.bacc as _bacc
    from concourse.bass_utils import run_bass_kernel_spmd as _run

    nc = _bacc.Bacc("TRN2", target_bir_lowering=False, num_devices=1)
    arrays = layout(inputs)
    d = {n: nc.dram_tensor(n, a.shape, mybir.dt.from_np(a.dtype), kind="ExternalInput").ap()
         for n, a in arrays.items()}
    d["out"] = nc.dram_tensor("out", OUT_SHAPE, F32, kind="ExternalOutput").ap()
    program(nc, d)
    r = _run(nc, [arrays], core_ids=[0])
    return r.results[0]["out"][:N]
```

```python
import numpy as np
import concourse.bass as bass
from concourse import mybir
from contextlib import ExitStack

F32 = mybir.dt.float32
BF16 = mybir.dt.bfloat16
I32 = mybir.dt.int32
ALU = mybir.AluOpType
ACT = mybir.ActivationFunctionType
AX = mybir.AxisListType

P = 128
N = 6250
D = 256
KC = D // P
NT = -(-N // P)
NP = NT * P
TAIL = N - (NT - 1) * P
U = 7
GROUPS = NT // U
GN = U * P
EPS = 1e-5

E = 200000
H0 = 8
HD0 = D // H0
CH = P // H0
CT = -(-(-(-E // P)) // CH)
ET = CH * CT
STEPS = ET + NT - 1
ETX = ET + 24
SU = 8
PAD_DST = 8191
NEG = -1e30

E2 = 131072
ET2 = E2 // P
HR = 4
NX = 4
HR16 = HR * NX
RW = HR16 + HR
FH = 512
H1 = 4
HD1 = D // H1
PW = D + H1
TW = 2 * H1 + 1
DS = 16
DTR = 16
CONV = 4
HID = 1024
NE = 8


NAMES = {}


def fresh(name):
    NAMES[name] = NAMES.get(name, 0) + 1
    return name if NAMES[name] == 1 else f"{name}_{NAMES[name]}"


class Chain:

    def __init__(self, eng, sem):
        self.eng, self.sem, self.n = eng, sem, 0

    def __call__(self, ins):
        self.n += 1
        ins.then_inc(self.sem, 1)
        self.eng.wait_ge(self.sem, self.n)


class Steps:

    def __init__(self, eng, sem, turn, total):
        self.eng, self.sem, self.base, self.n = eng, sem, turn * total, 0

    def __call__(self, ins):
        self.n += 1
        ins.then_inc(self.sem, 1)
        self.eng.wait_ge(self.sem, self.base + self.n)


def bc(ap, shape):
    return ap.unsqueeze(len(ap.shape)).to_broadcast(shape)


def node_view(dram):
    full = dram[0:(NT - 1) * P, :].rearrange("(t p) d -> p t d", p=P)
    return full, dram[(NT - 1) * P:N, :]


def constants(nc, ident, iota):
    with nc.semaphore("c_zero") as zeroed, nc.semaphore("c_done") as made, nc.Block() as block:
        @block.gpsimd
        def _(pool):
            pool.memset(ident[:], 0.0).then_inc(zeroed, 1)
            pool.iota(iota[:], pattern=[[1, P]], base=0, channel_multiplier=0,
                      allow_small_or_imprecise_dtypes=True).then_inc(made, 1)
            pool.wait_ge(zeroed, 1)
            pool.affine_select(out=ident[:], in_=ident[:], compare_op=ALU.not_equal, fill=1.0, base=0,
                               pattern=[[-1, P]], channel_multiplier=1).then_inc(made, 1)
            pool.wait_ge(made, 2)


def load_nodes(nc, dst, dram):
    full, tail = node_view(dram)
    with nc.semaphore("ld") as loaded, nc.semaphore("ldz") as cleared, nc.Block() as block:
        @block.vector
        def _(dve):
            dve.memset(dst[:, NT - 1, :], 0.0).then_inc(cleared, 1)

        @block.sync
        def _(sp):
            sp.dma_start(dst[:, 0:NT - 1, :], full).then_inc(loaded, 16)
            sp.wait_ge(cleared, 1)
            sp.dma_start(dst[0:TAIL, NT - 1, :], tail).then_inc(loaded, 16)
            sp.wait_ge(loaded, 32)


def load_all(nc, pairs):
    with nc.semaphore("la") as loaded, nc.Block() as block:
        @block.sync
        def _(sp):
            for dst, src in pairs:
                sp.dma_start(dst, src).then_inc(loaded, 16)
            sp.wait_ge(loaded, 16 * len(pairs))


def rows_of(tab):
    return tab.rearrange("(t p) w -> p t w", p=P)


def store_nodes(nc, pairs):
    with nc.semaphore("st") as stored, nc.Block() as block:
        @block.sync
        def _(sp):
            for dst, src in pairs:
                sp.dma_start(rows_of(dst), src[:]).then_inc(stored, 16)
            sp.wait_ge(stored, 16 * len(pairs))


def layernorm(nc, src, out, scratch, gamma=None, beta=None):
    T, W = src.shape[1], src.shape[2]
    with ExitStack() as ctx:
        st = ctx.enter_context(nc.sbuf_tensor(fresh("ln_st"), [P, 4, T], F32))
        chain_sem = ctx.enter_context(nc.semaphore("ln_chain"))
        centred = ctx.enter_context(nc.semaphore("ln_centred"))
        squared = ctx.enter_context(nc.semaphore("ln_squared"))
        var_ready = ctx.enter_context(nc.semaphore("ln_var"))
        std_ready = ctx.enter_context(nc.semaphore("ln_std"))
        block = ctx.enter_context(nc.Block())
        full = [P, T, W]

        @block.vector
        def _(dve):
            link = Chain(dve, chain_sem)
            link(dve.tensor_reduce(st[:, 0, :], src, AX.X, ALU.add))
            link(dve.tensor_scalar(st[:, 1, :], st[:, 0, :], 1.0 / W, None, ALU.mult))
            dve.tensor_tensor(out, src, bc(st[:, 1, :], full), ALU.subtract).then_inc(centred, 1)
            dve.wait_ge(squared, 1)
            link(dve.tensor_reduce(st[:, 2, :], scratch, AX.X, ALU.add))
            dve.tensor_scalar(st[:, 3, :], st[:, 2, :], 1.0 / W, EPS, ALU.mult, ALU.add).then_inc(var_ready, 1)
            dve.wait_ge(std_ready, 1)
            link(dve.reciprocal(st[:, 1, :], st[:, 0, :]))
            link(dve.tensor_tensor(out, out, bc(st[:, 1, :], full), ALU.mult))
            if gamma is not None:
                link(dve.tensor_tensor(out, out, gamma.unsqueeze(1).to_broadcast(full), ALU.mult))
                link(dve.tensor_tensor(out, out, beta.unsqueeze(1).to_broadcast(full), ALU.add))

        @block.scalar
        def _(act):
            act.wait_ge(centred, 1)
            act.activation(scratch, out, ACT.Square).then_inc(squared, 1)
            act.wait_ge(var_ready, 1)
            act.activation(st[:, 0, :], st[:, 3, :], ACT.Sqrt).then_inc(std_ready, 1)


def apart(u, slots):
    return slots if u >= slots else u + U - max(v for v in range(U) if v % slots == u)


def tile(ap, t):
    return ap[:, bass.ds(t, 1), :].rearrange("p a w -> p (a w)")


XT_SLOTS = 2
OUT_SLOTS = 3


def project_tiles(nc, src, w, ident, evacuate, xT=None, turned_src=None):
    M = 0 if w is None else w.shape[2]
    parts = [(m, min(m + 512, M)) for m in range(0, M, 512)]
    with ExitStack() as ctx:
        xs = ctx.enter_context(nc.sbuf_tensor(fresh("pj_x"), [P, U, D], F32))
        xt = ctx.enter_context(nc.sbuf_tensor(fresh("pj_xt"), [P, U, D], F32))
        pT = ctx.enter_context(nc.psum_tensor(fresh("pj_pT"), [P, XT_SLOTS, 512], F32))
        po = ctx.enter_context(nc.psum_tensor(fresh("pj_po"), [P, OUT_SLOTS, 1024], F32))
        fetched = ctx.enter_context(nc.semaphore("pj_fetched"))
        turned = ctx.enter_context(nc.semaphore("pj_turned"))
        xt_ready = ctx.enter_context(nc.semaphore("pj_xt_ready"))
        made = ctx.enter_context(nc.semaphore("pj_made"))
        out_free = ctx.enter_context(nc.semaphore("pj_out_free"))
        block = ctx.enter_context(nc.Block())

        @block.gpsimd
        def _(pool):
            pool.sem_inc(turned, U)
            with pool.Fori(0, GROUPS) as g:
                for u in range(U):
                    pool.wait_ge(turned, g * U + u + 1)
                    if turned_src is None:
                        pool.tensor_copy(xs[:, u, :], tile(src, g * U + u)).then_inc(fetched, 1)
                    else:
                        pool.tensor_copy(xs[:, u, :].rearrange("p (k n) -> p k n", k=KC),
                                         turned_src[:, :, bass.ds((g * U + u) * P, P)]).then_inc(fetched, 1)

        @block.tensor
        def _(pe):
            def turn(g, u):
                pe.wait_ge(fetched, g * U + u + 1)
                pe.wait_ge(xt_ready, g * U + u + 1 + U - apart(u, XT_SLOTS))
                for k in range(KC):
                    ins = pe.matmul(pT[:, u % XT_SLOTS, k * P:(k + 1) * P], ident[:], xs[:, u, k * P:(k + 1) * P],
                                    start=True, stop=True) if turned_src is not None else \
                        pe.transpose(pT[:, u % XT_SLOTS, k * P:(k + 1) * P], xs[:, u, k * P:(k + 1) * P], ident[:])
                ins.then_inc(turned, 1)

            def multiply(g, u):
                pe.wait_ge(xt_ready, g * U + u + 1 + U)
                pe.wait_ge(out_free, g * U + u + 1 + U - apart(u, OUT_SLOTS))
                for a, b in parts:
                    for k in range(KC):
                        ins = pe.matmul(po[:, u % OUT_SLOTS, a:b], xt[:, u, k * P:(k + 1) * P], w[:, k, a:b],
                                        start=(k == 0), stop=(k == KC - 1))
                ins.then_inc(made, 1)

            with pe.Fori(0, GROUPS) as g:
                for u in range(U):
                    turn(g, u)
                    if M and u >= 1:
                        multiply(g, u - 1)
                if M:
                    multiply(g, U - 1)

        @block.scalar
        def _(act):
            act.sem_inc(xt_ready, U)
            if M:
                act.sem_inc(made, U)
            with act.Fori(0, GROUPS) as g:
                for u in range(U):
                    act.wait_ge(turned, g * U + u + 1 + U)
                    if M:
                        act.wait_ge(made, g * U + u + 1)
                    if xT is None:
                        act.copy(xt[:, u, :], pT[:, u % XT_SLOTS, 0:D]).then_inc(xt_ready, 1)
                    else:
                        if M:
                            act.copy(xt[:, u, :], pT[:, u % XT_SLOTS, 0:D])
                        act.copy(xT[:, :, bass.ds((g * U + u) * P, P)],
                                 pT[:, u % XT_SLOTS, 0:D].rearrange("p (k n) -> p k n", k=KC)).then_inc(xt_ready, 1)

        if M:
            @block.vector
            def _(dve):
                dve.sem_inc(out_free, U)
                with dve.Fori(0, GROUPS) as g:
                    for u in range(U):
                        dve.wait_ge(made, g * U + u + 1 + U)
                        evacuate(dve, po[:, u % OUT_SLOTS, :], g * U + u).then_inc(out_free, 1)


def phase_qkv(nc, env, d):
    with ExitStack() as ctx:
        q = ctx.enter_context(nc.sbuf_tensor(fresh("a_q"), [P, NT, D], F32))
        x = ctx.enter_context(nc.sbuf_tensor(fresh("a_x"), [P, NT, D], F32))
        xn = ctx.enter_context(nc.sbuf_tensor(fresh("a_xn"), [P, NT, D], F32))
        w = ctx.enter_context(nc.sbuf_tensor(fresh("a_w"), [P, KC, 3 * D], F32))
        load_all(nc, [(w[:], d["wqkvT"].rearrange("(k p) m -> p k m", p=P))])
        load_nodes(nc, x, d["x"])
        layernorm(nc, x[:], xn[:], q[:])

        def keep_qkv(dve, out, t):
            dve.tensor_scalar(tile(q, t), out[:, 0:D], float(1.0 / HD0 ** -0.5), None, ALU.mult)
            dve.tensor_copy(tile(x, t), out[:, D:2 * D])
            return dve.tensor_copy(tile(xn, t), out[:, 2 * D:3 * D])
        project_tiles(nc, xn, w, ident=env["ident"], evacuate=keep_qkv)
        with nc.semaphore("kv_out") as stored, nc.Block() as block:
            @block.sync
            def _(sp):
                sp.dma_start(d["k_tab"].rearrange("(t p) d -> p t d", p=P), x[:]).then_inc(stored, 16)
                sp.dma_start(d["v_tab"].rearrange("(t p) d -> p t d", p=P), xn[:]).then_inc(stored, 16)
                sp.dma_start(d["q_tab"].rearrange("(t p) d -> p t d", p=P), q[:]).then_inc(stored, 16)
                sp.wait_ge(stored, 48)


STEP_PAD = 24
SL = STEPS + STEP_PAD
SCOLS = 410
LEAD = 3
BLEAD = 4
ROW = CT * P
LW = ET * H0


def walk(nc, env, d):
    with ExitStack() as ctx:
        dst_i = ctx.enter_context(nc.sbuf_tensor(fresh("w_dst"), [P, ETX], I32))
        last = ctx.enter_context(nc.sbuf_tensor(fresh("w_last"), [P, ETX], I32))
        lastf = ctx.enter_context(nc.sbuf_tensor(fresh("w_lastf"), [P, ETX], F32))
        before = ctx.enter_context(nc.sbuf_tensor(fresh("w_before"), [P, ETX], F32))
        step = ctx.enter_context(nc.sbuf_tensor(fresh("w_step"), [P, SL], F32))
        entered = ctx.enter_context(nc.sbuf_tensor(fresh("w_entered"), [P, SL], F32))
        til = ctx.enter_context(nc.sbuf_tensor(fresh("w_til"), [P, SL], F32))
        blk = ctx.enter_context(nc.sbuf_tensor(fresh("w_blk"), [P, SL], F32))
        col = ctx.enter_context(nc.sbuf_tensor(fresh("w_col"), [P, 4], F32))
        ones = ctx.enter_context(nc.sbuf_tensor(fresh("w_ones"), [P, P], F32))
        ps = ctx.enter_context(nc.psum_tensor(fresh("w_ps"), [P, 4, 512], F32))
        loaded = ctx.enter_context(nc.semaphore("w_loaded"))
        iotas = ctx.enter_context(nc.semaphore("w_iotas"))
        marked = ctx.enter_context(nc.semaphore("w_marked"))
        summed = ctx.enter_context(nc.semaphore("w_summed"))
        chain_sem = ctx.enter_context(nc.semaphore("w_chain"))
        block = ctx.enter_context(nc.Block())
        assert 4 * SCOLS == SL

        @block.sync
        def _(sp):
            sp.dma_start(last[:], d["tile_last"].partition_broadcast(P)).then_inc(loaded, 16)
            sp.dma_start(env["src"][:], d["src_cols"]).then_inc(loaded, 16)
            sp.dma_start(dst_i[:], d["dst_cols"]).then_inc(loaded, 16)

        @block.gpsimd
        def _(pool):
            pool.iota(step[:], pattern=[[1, SL]], base=0, channel_multiplier=0,
                      allow_small_or_imprecise_dtypes=True).then_inc(iotas, 1)
            pool.iota(col[:, 0:1], pattern=[[0, 1]], base=0, channel_multiplier=1,
                      allow_small_or_imprecise_dtypes=True).then_inc(iotas, 1)

        @block.vector
        def _(dve):
            link = Chain(dve, chain_sem)
            link(dve.memset(ones[:], 1.0))
            dve.wait_ge(loaded, 48)
            dve.wait_ge(iotas, 2)
            link(dve.tensor_copy(env["dst"][:], dst_i[:]))
            link(dve.tensor_copy(lastf[:], last[:]))
            link(dve.tensor_scalar(col[:, 1:2], col[:, 0:1], float(P), None, ALU.mult))
            link(dve.tensor_scalar(before[:], lastf[:], col[:, 1:2], None, ALU.is_lt, ALU.add, accum_out=col[:, 2:3]))
            link(dve.tensor_tensor(col[:, 3:4], col[:, 2:3], col[:, 0:1], ALU.add))
            dve.tensor_scalar(entered[:], step[:], col[:, 3:4], None, ALU.is_ge).then_inc(marked, 1)
            dve.wait_ge(summed, 1)
            link(dve.tensor_scalar(blk[:].rearrange("p (a c) -> p a c", a=4), ps[:, :, 0:SCOLS], -1.0, None, ALU.add))
            link(dve.tensor_scalar(env["base"][:], blk[:], float(P), None, ALU.mult))
            link(dve.tensor_copy(env["step_b"], blk[0:1, :]))
            link(dve.tensor_tensor(til[:], step[:], blk[:], ALU.subtract))
            for table, first, p, lead, w in ((env["tile_pairs"], til, 32, LEAD, 2), (env["block_pairs"], blk, 64, BLEAD, 2),
                                             (env["block_fours"], blk, 96, BLEAD, 4)):
                n = SL // w - lead
                groups = table.rearrange("p (k c) -> p k c", c=2 * w)
                link(dve.tensor_copy(groups[:, 0:n, 0:w], first[p:p + 1, 0:w * n].rearrange("p (k c) -> p k c", c=w)))
                link(dve.tensor_copy(groups[:, 0:n, w:2 * w], til[p:p + 1, w * lead:w * lead + w * n].rearrange("p (k c) -> p k c", c=w)))

        @block.tensor
        def _(pe):
            pe.wait_ge(marked, 1)
            for a in range(4):
                ins = pe.matmul(ps[:, a, 0:SCOLS], ones[0:NT, :], entered[0:NT, a * SCOLS:(a + 1) * SCOLS],
                                start=True, stop=True)
            ins.then_inc(summed, 1)


def blocks_of(nc, eng, env, s, n):
    _, b = nc.values_load_multi_w_load_instructions(
        env["step_b"][0:1, bass.ds(s, n)], engines=(eng.engine,), min_val=0, max_val=NT - 1,
        skip_runtime_bounds_check_because='the walk has NT blocks')
    return b


def group_of(nc, eng, table, k, most, n=4):
    _, v = nc.values_load_multi_w_load_instructions(
        table[0:1, bass.ds(k * n, n)], engines=(eng.engine,), min_val=0, max_val=most,
        skip_runtime_bounds_check_because='the walk has ET + NT - 1 steps')
    return v


def tile_of(nc, s, b, tiles=ETX):
    return nc.s_assert_within(s - b, 0, tiles - 1, 
                              skip_runtime_bounds_check_because="block b is entered at step T[b] + b or later")


def gather_rows(pool, table, rows, idx_slot, done):
    pool.indirect_dma_start(rows, None, table, bass.IndirectOffsetOnAxis(ap=idx_slot, axis=0)).then_inc(done, 16)


def one_hot(dve, env, out, s, t):
    return dve.tensor_scalar(out, env["iota"][:], env["base"][:, bass.ds(s, 1)], env["dst"][:, bass.ds(t, 1)],
                             ALU.add, ALU.is_equal)


def edge_logits(nc, env, d, logits, q):
    L = logits[:, 0:LW].rearrange("p (t h) -> p t h", h=H0)
    G, SLOTS = 2, 4
    with ExitStack() as ctx:
        def sb(name, shape, dt=F32):
            return ctx.enter_context(nc.sbuf_tensor(fresh(name), shape, dt))

        def sem(name):
            return ctx.enter_context(nc.semaphore(name))
        idx = sb("e_idx", [P, SU], I32)
        rows = sb("e_rows", [P, SLOTS, G * D])
        oh = sb("e_oh", [P, SLOTS, G, P])
        ohT = sb("e_ohT", [P, SLOTS, G, P])
        prod = sb("e_prod", [P, 2, G * D])
        dots = sb("e_dots", [P, 2, G, H0])
        pT = ctx.enter_context(nc.psum_tensor(fresh("e_pT"), [P, 2, 512], F32))
        pq = ctx.enter_context(nc.psum_tensor(fresh("e_pq"), [P, SLOTS, G * D], F32))
        idx_ready, rows_used, oh_ready, turned = sem("e_idx_ready"), sem("e_rows_used"), sem("e_oh_ready"), sem("e_turned")
        ohT_ready, q_made, summed, added = sem("e_ohT_ready"), sem("e_q_made"), sem("e_summed"), sem("e_added")
        landed = [sem(f"e_landed{n}") for n in range(SLOTS)]
        block = ctx.enter_context(nc.Block())
        assert SLOTS * G == SU

        @block.gpsimd
        def _(pool):
            with pool.Fori(0, STEPS // SU) as i:
                for n in range(SLOTS):
                    k = i * SLOTS + n
                    pool.wait_ge(idx_ready, k + 1)
                    pool.wait_ge(rows_used, k + 1)
                    pool.nop(nofuse=True)
                    for u in range(G):
                        gather_rows(pool, d["k_tab"], rows[:, n, u * D:(u + 1) * D], idx[:, n * G + u:n * G + u + 1], landed[n])

        @block.scalar
        def _(act):
            act.sem_inc(ohT_ready, 2)
            act.copy(idx[:], env["src"][:, 0:SU]).then_inc(idx_ready, SLOTS)
            with act.Fori(0, STEPS // SU) as i:
                b = blocks_of(nc, act, env, i * SU + SU, SU)
                for n in range(SLOTS):
                    k = i * SLOTS + n
                    act.wait_ge(turned, k + 1 + SLOTS)
                    act.wait_ge(q_made, k + 1)
                    act.copy(ohT[:, n], pT[:, n % 2, 0:G * P].rearrange("p (u e) -> p u e", u=G)).then_inc(ohT_ready, 1)
                    act.wait_ge(landed[n], (i + 1) * (16 * G))
                    for u in range(n * G, n * G + G):
                        t = tile_of(nc, i * SU + (u + SU), b[u])
                        ins = act.copy(idx[:, u:u + 1], env["src"][:, bass.ds(t, 1)])
                    ins.then_inc(idx_ready, 1)

        @block.tensor
        def _(pe):
            pe.sem_inc(turned, SLOTS)
            pe.sem_inc(q_made, SLOTS)

            def turn(k, n):
                pe.wait_ge(oh_ready, k + 1)
                pe.wait_ge(ohT_ready, k + 1)
                for u in range(G):
                    ins = pe.transpose(pT[:, n % 2, u * P:(u + 1) * P], oh[:, n % SLOTS, u, :], env["ident"][:])
                ins.then_inc(turned, 1)

            turn(0, 0)
            with pe.Fori(0, STEPS // SU) as i:
                for n in range(SLOTS):
                    k = i * SLOTS + n
                    turn(k + 1, n + 1)
                    if n == 0:
                        b = blocks_of(nc, pe, env, i * SU, SU)
                    pe.wait_ge(ohT_ready, k + 1 + 2)
                    pe.wait_ge(rows_used, k + 1)
                    for u in range(G):
                        ins = pe.matmul(pq[:, n, u * D:(u + 1) * D], ohT[:, n, u, :], tile(q, b[n * G + u]), start=True, stop=True)
                    ins.then_inc(q_made, 1)

        @block.vector
        def _(dve):
            dve.sem_inc(rows_used, SLOTS)
            dve.sem_inc(summed, 2)
            dve.sem_inc(added, 1)

            def mark(k, n, t):
                dve.wait_ge(turned, k + 1)
                for u in range(G):
                    ins = one_hot(dve, env, oh[:, n % SLOTS, u, :], k * G + u, t[u])
                ins.then_inc(oh_ready, 1)

            def add(k, n, u, t):
                t = nc.s_assert_within(t[u], 0, ET - 1, skip_runtime_bounds_check_because="a tile of edges")
                dve.wait_ge(summed, k + 1 + 2)
                dve.wait_ge(added, k * G + u + 1)
                dve.tensor_tensor(tile(L, t), tile(L, t), dots[:, n % 2, u, :], ALU.add).then_inc(added, 1)

            for k in range(LEAD):
                mark(k, k, [k * G, k * G + 1])
            with dve.Fori(0, STEPS // SU) as i:
                last = None
                for n in range(SLOTS):
                    k = i * SLOTS + n
                    dve.wait_ge(landed[n], (i + 1) * (16 * G))
                    dve.wait_ge(q_made, k + 1 + SLOTS)
                    dve.wait_ge(summed, k + 1)
                    dve.tensor_tensor(prod[:, n % 2, :], rows[:, n, :], pq[:, n, :], ALU.mult).then_inc(rows_used, 1)
                    t = group_of(nc, dve, env["tile_pairs"], k, ETX - 1)
                    if n:
                        add(k - 1, n - 1, 0, last)
                    dve.wait_ge(rows_used, k + 1 + SLOTS)
                    dve.tensor_reduce(dots[:, n % 2].rearrange("p u h -> p (u h)"),
                                      prod[:, n % 2, :].rearrange("p (h c) -> p h c", c=HD0), AX.X, ALU.add).then_inc(summed, 1)
                    if n:
                        add(k - 1, n - 1, 1, last)
                    mark(k + LEAD, n + LEAD, t[G:])
                    last = t
                for u in range(G):
                    add(i * SLOTS + SLOTS - 1, SLOTS - 1, u, last)


def edge_sums(nc, env, d, weights, acc):
    A = weights.rearrange("p (t h) -> p t h", h=H0)
    W = D + H0
    G, SLOTS = 2, 4
    GROUPS_OF_STEPS = STEPS // G
    with ExitStack() as ctx:
        def sb(name, shape, dt=F32):
            return ctx.enter_context(nc.sbuf_tensor(fresh(name), shape, dt))

        def sem(name):
            return ctx.enter_context(nc.semaphore(name))
        idx = sb("s_idx", [P, SU], I32)
        rows = sb("s_rows", [P, SLOTS, G, D])
        oh = sb("s_oh", [P, SLOTS, G, P])
        msg = sb("s_msg", [P, SLOTS, G, W])
        pa = ctx.enter_context(nc.psum_tensor(fresh("s_pa"), [P, 2, G, 512], F32))
        idx_ready, msg_ready, a_ready, oh_ready = sem("s_idx_ready"), sem("s_msg_ready"), sem("s_a_ready"), sem("s_oh_ready")
        made, added, cleared = sem("s_made"), sem("s_added"), sem("s_cleared")
        landed = [sem(f"s_landed{n}") for n in range(SLOTS)]
        block = ctx.enter_context(nc.Block())

        @block.gpsimd
        def _(pool):
            def fetch(k, n):
                pool.wait_ge(idx_ready, k + 1)
                pool.wait_ge(msg_ready, k + 1)
                pool.nop(nofuse=True)
                for u in range(G):
                    gather_rows(pool, d["v_tab"], rows[:, n, u, :], idx[:, n * G + u:n * G + u + 1], landed[n])

            with pool.Fori(0, STEPS // SU) as i:
                for n in range(SLOTS):
                    fetch(i * SLOTS + n, n)
            fetch(GROUPS_OF_STEPS, 0)

        @block.scalar
        def _(act):
            def take(k, n, b):
                act.wait_ge(made, k * G + G)
                for u in range(G):
                    t = tile_of(nc, k * G + u, b[u], ET + G)
                    ins = act.copy(msg[:, n % SLOTS, u, D:W], tile(A, t))
                ins.then_inc(a_ready, 1)

            act.copy(idx[:], env["src"][:, 0:SU]).then_inc(idx_ready, SLOTS)
            act.wait_ge(cleared, 2)
            take(0, 0, [0] * G)
            with act.Fori(0, STEPS // SU) as i:
                b = blocks_of(nc, act, env, i * SU, 2 * SU)
                for n in range(SLOTS):
                    k = i * SLOTS + n
                    take(k + 1, n + 1, b[(n + 1) * G:])
                    act.wait_ge(landed[n], (i + 1) * (16 * G))
                    for u in range(n * G, n * G + G):
                        t = tile_of(nc, i * SU + (u + SU), b[u + SU])
                        ins = act.copy(idx[:, u:u + 1], env["src"][:, bass.ds(t, 1)])
                    ins.then_inc(idx_ready, 1)

        @block.tensor
        def _(pe):
            pe.sem_inc(made, SLOTS * G)
            with pe.Fori(0, STEPS // SU) as i:
                for n in range(SLOTS):
                    k = i * SLOTS + n
                    pe.wait_ge(oh_ready, k + 1)
                    pe.wait_ge(msg_ready, k + 1 + SLOTS)
                    for u in range(G):
                        pe.wait_ge(added, k * G + u + 1)
                        pe.matmul(pa[:, n % 2, u, 0:W], oh[:, n, u, :], msg[:, n, u, :],
                                  start=True, stop=True).then_inc(made, 1)

        @block.vector
        def _(dve):
            dve.sem_inc(msg_ready, SLOTS)
            dve.sem_inc(added, 2 * G)
            dve.memset(acc[:], 0.0).then_inc(cleared, 1)
            dve.memset(A[:, ET:ET + G, :], 0.0).then_inc(cleared, 1)
            dve.wait_ge(cleared, 2)

            def mark(k, n, t):
                dve.wait_ge(made, k * G + G)
                for u in range(G):
                    ins = one_hot(dve, env, oh[:, n % SLOTS, u, :], k * G + u, t[u])
                ins.then_inc(oh_ready, 1)

            def weigh(k, n, turn):
                n = n % SLOTS
                dve.wait_ge(landed[n], (turn + 1) * (16 * G))
                dve.wait_ge(a_ready, k + 1)
                dve.tensor_tensor(msg[:, n, :, 0:D].rearrange("p u (h c) -> p u h c", h=H0),
                                  rows[:, n].rearrange("p u (h c) -> p u h c", h=H0),
                                  bc(msg[:, n, :, D:W], [P, G, H0, HD0]), ALU.mult).then_inc(msg_ready, 1)

            def add(k, n, u, b):
                b = nc.s_assert_within(b[u], 0, NT - 1, skip_runtime_bounds_check_because="a block of nodes")
                s = k * G + u
                dve.wait_ge(made, s + 1 + SLOTS * G)
                dve.wait_ge(added, s + 2 * G)
                dve.tensor_tensor(tile(acc, b), tile(acc, b), pa[:, n % 2, u, 0:W], ALU.add).then_inc(added, 1)

            for k in range(BLEAD):
                mark(k, k, [k * G, k * G + 1])
            weigh(0, 0, 0)
            with dve.Fori(0, STEPS // SU) as i:
                for n in range(SLOTS):
                    k = i * SLOTS + n
                    weigh(k + 1, n + 1, i + (n + 1) // SLOTS)
                    v = group_of(nc, dve, env["block_pairs"], k, ETX - 1)
                    add(k, n, 0, v)
                    add(k, n, 1, v)
                    mark(k + BLEAD, n + BLEAD, v[G:])


def turn_groups(nc, ident, groups, source, dest):
    with ExitStack() as ctx:
        xs = ctx.enter_context(nc.sbuf_tensor(fresh("tg_x"), [P, U, P], F32))
        ps = ctx.enter_context(nc.psum_tensor(fresh("tg_ps"), [P, U, 512], F32))
        fetched = ctx.enter_context(nc.semaphore("tg_fetched"))
        turned = ctx.enter_context(nc.semaphore("tg_turned"))
        copied = ctx.enter_context(nc.semaphore("tg_copied"))
        block = ctx.enter_context(nc.Block())

        @block.gpsimd
        def _(pool):
            pool.sem_inc(turned, U)
            with pool.Fori(0, groups // U) as i:
                for u in range(U):
                    src = source(i * U + u)
                    out = xs[:, u, :]
                    if len(src.shape) == 3:
                        out = out.rearrange("p (a b) -> p a b", a=src.shape[1])
                    pool.wait_ge(turned, i * U + u + 1)
                    pool.tensor_copy(out, src).then_inc(fetched, 1)

        @block.tensor
        def _(pe):
            with pe.Fori(0, groups // U) as i:
                for u in range(U):
                    pe.wait_ge(fetched, i * U + u + 1)
                    pe.wait_ge(copied, i * U + u + 1)
                    pe.transpose(ps[:, u, 0:P], xs[:, u, :], ident[:]).then_inc(turned, 1)

        @block.vector
        def _(dve):
            dve.sem_inc(copied, U)
            with dve.Fori(0, groups // U) as i:
                for u in range(U):
                    dst = dest(i * U + u)
                    src = ps[:, u, 0:P]
                    if len(dst.shape) == 3:
                        src = src.rearrange("p (a b) -> p a b", a=dst.shape[1])
                    dve.wait_ge(turned, i * U + u + 1 + U)
                    dve.tensor_copy(dst, src).then_inc(copied, 1)


def segment_exp(nc, env, d, logits):
    L = logits[:, 0:LW].rearrange("p (j g h) -> p j g h", j=CH, h=H0)
    group = lambda g: L[:, :, bass.ds(g, 1), :].rearrange("p j a h -> p j (a h)")
    with ExitStack() as ctx:
        row = ctx.enter_context(nc.sbuf_tensor(fresh("x_row"), [P, ROW], F32))
        cut = [ctx.enter_context(nc.sbuf_tensor(fresh(n), [P, ROW], BF16)) for n in ("x_first", "x_last")]
        turn_groups(nc, env["ident"], CT, group, lambda g: row[:, bass.ds(g * P, P)])
        dsts = logits[:, 0:ROW + 2].bitcast(I32)
        run = logits[:, 0:ROW]

        with ExitStack() as ctx2:
            loaded = ctx2.enter_context(nc.semaphore("x_loaded"))
            chain_sem = ctx2.enter_context(nc.semaphore("x_chain"))
            block = ctx2.enter_context(nc.Block())

            @block.sync
            def _(sp):
                for j in range(CH):
                    sp.dma_start(dsts[j * H0:(j + 1) * H0, :],
                                 d["dst_line"][j * ROW:(j + 1) * ROW + 2].partition_broadcast(H0)).then_inc(loaded, 16)
                sp.wait_ge(loaded, 16 * CH)

            @block.vector
            def _(dve):
                link = Chain(dve, chain_sem)
                dve.wait_ge(loaded, 16 * CH)
                for c, other in zip(cut, (0, 2)):
                    link(dve.tensor_tensor(c[:], dsts[:, 1:ROW + 1], dsts[:, other:other + ROW], ALU.not_equal))
                    link(dve.tensor_scalar(c[:], c[:], NEG, None, ALU.mult))

        for c, data, way in ((cut[0], row, 1), (cut[1], None, -1)):
            segment_max(nc, env, c, data[:] if way == 1 else run, run, way)

        with ExitStack() as ctx2:
            shifted = ctx2.enter_context(nc.semaphore("x_shifted"))
            raised = ctx2.enter_context(nc.semaphore("x_raised"))
            block = ctx2.enter_context(nc.Block())

            @block.vector
            def _(dve):
                dve.tensor_tensor(row[:], row[:], run, ALU.subtract).then_inc(shifted, 1)

            @block.scalar
            def _(act):
                act.wait_ge(shifted, 1)
                act.activation(row[:], row[:], ACT.Exp).then_inc(raised, 1)
                act.wait_ge(raised, 1)
        turn_groups(nc, env["ident"], CT, lambda g: row[:, bass.ds(g * P, P)], group)


def segment_max(nc, env, cut, data, run, way):
    order = slice(None, None, way)
    PIECES = U
    PIECE = ROW // PIECES
    with ExitStack() as ctx:
        whole = ctx.enter_context(nc.sbuf_tensor(fresh("m_whole"), [P, 4], F32))
        part = ctx.enter_context(nc.sbuf_tensor(fresh("m_part"), [P, PIECE], F32))
        line = ctx.enter_context(nc.sbuf_tensor(fresh("m_line"), [1, 4, P + H0], F32))
        ps = ctx.enter_context(nc.psum_tensor(fresh("m_ps"), [P, 4, 512], F32))
        chain_sem = ctx.enter_context(nc.semaphore("m_chain"))
        ends_ready = ctx.enter_context(nc.semaphore("m_ends"))
        turned = ctx.enter_context(nc.semaphore("m_turned"))
        carries = ctx.enter_context(nc.semaphore("m_carries"))
        placed = ctx.enter_context(nc.semaphore("m_placed"))
        block = ctx.enter_context(nc.Block())
        end = PIECE - 1 if way == 1 else 0

        @block.vector
        def _(dve):
            link = Chain(dve, chain_sem)
            link(dve.tensor_reduce(whole[:, 1:2], cut[:], AX.X, ALU.min))
            link(dve.memset(line[:], NEG))
            link(dve.memset(whole[:, 0:1], NEG))
            for n in range(PIECES)[::way]:
                a, b = n * PIECE, (n + 1) * PIECE
                link(dve.tensor_tensor_scan(part[:, order], cut[:, a:b][:, order], data[:, a:b][:, order],
                                            whole[:, 0:1], ALU.add, ALU.max))
                link(dve.tensor_copy(whole[:, 0:1], part[:, end:end + 1]))
            dve.drain().then_inc(ends_ready, 1)
            dve.wait_ge(turned, 1)
            link(dve.tensor_copy(line[:, 0, 0:P], ps[0:1, 0, 0:P]))
            link(dve.tensor_copy(line[:, 1, 0:P], ps[0:1, 1, 0:P]))
            for h in range(H0):
                ends = line[:, 0, h:P:H0][:, order]
                cuts = line[:, 1, h:P:H0][:, order]
                out = (line[:, 2, h + H0:P + H0:H0] if way == 1 else line[:, 3, h:P:H0])[:, order]
                ins = dve.tensor_tensor_scan(out, cuts, ends, NEG, ALU.add, ALU.max)
                link(ins)
            dve.drain().then_inc(carries, 1)
            dve.wait_ge(placed, 1)
            link(dve.tensor_copy(whole[:, 2:3], ps[:, 2, 0:1]))
            link(dve.tensor_tensor_scan(run[:, order], cut[:, order], data[:, order], whole[:, 2:3], ALU.add, ALU.max))

        @block.tensor
        def _(pe):
            pe.wait_ge(ends_ready, 1)
            pe.transpose(ps[0:1, 0, 0:P], whole[:, 0:1], env["ident"][:])
            pe.transpose(ps[0:1, 1, 0:P], whole[:, 1:2], env["ident"][:]).then_inc(turned, 1)
            pe.wait_ge(carries, 1)
            src = line[:, 2, 0:P] if way == 1 else line[:, 3, H0:P + H0]
            pe.transpose(ps[:, 2, 0:1], src, env["ident"][0:1, 0:1]).then_inc(placed, 1)


BT = 8
NB2 = ET2 // BT
HALVES = 2
OHW = NT * RW
GC = GN // 2


def leaky(dve, out, z):
    return dve.scalar_tensor_tensor(out, z, 0.2, z, ALU.mult, ALU.max)


def finish_attention(nc, env, d, acc, x, x1n):
    with ExitStack() as ctx:
        den = ctx.enter_context(nc.sbuf_tensor(fresh("f_den"), [P, 2, NT, H0], F32))
        w = ctx.enter_context(nc.sbuf_tensor(fresh("f_wo"), [P, KC, D], F32))
        load_all(nc, [(w[:], d["woT"].rearrange("(k p) m -> p k m", p=P))])
        load_nodes(nc, x, d["x"])
        with nc.semaphore("f_chain") as chain_sem, nc.Block() as block:
            @block.vector
            def _(dve):
                link = Chain(dve, chain_sem)
                sums = acc[:, :, D:D + H0]
                link(dve.tensor_scalar(den[:, 0], sums, 0.0, None, ALU.is_equal))
                link(dve.tensor_tensor(den[:, 1], den[:, 0], sums, ALU.add))
                link(dve.reciprocal(den[:, 0], den[:, 1]))
                for h in range(H0):
                    part = acc[:, :, h * HD0:(h + 1) * HD0]
                    ins = dve.tensor_tensor(part, part, den[:, 0, :, h:h + 1].to_broadcast([P, NT, HD0]), ALU.mult)
                link(ins)
        project_tiles(nc, acc[:, :, 0:D], w, env["ident"],
                      lambda dve, out, t: dve.tensor_tensor(tile(x, t), tile(x, t), out[:, 0:D], ALU.add))


def routing_tables(nc, env, d, x1n, h20, dtab):
    with ExitStack() as ctx:
        w = ctx.enter_context(nc.sbuf_tensor(fresh("r_w"), [P, KC, HR16], F32))
        att = ctx.enter_context(nc.sbuf_tensor(fresh("r_att"), [P, 2, HR16], F32))
        prod = ctx.enter_context(nc.sbuf_tensor(fresh("r_prod"), [P, NT, HR16], F32))
        top = ctx.enter_context(nc.sbuf_tensor(fresh("r_top"), [P, 2, HR], F32))
        load_all(nc, [(w[:], d["w_gat"].rearrange("(k p) m -> p k m", p=P)),
                      (att[:, 0, :], d["att_src"].partition_broadcast(P)),
                      (att[:, 1, :], d["att_dst"].partition_broadcast(P))])
        project_tiles(nc, x1n, w, env["ident"],
                      lambda dve, out, t: dve.tensor_copy(tile(h20[:, :, 0:HR16], t), out[:, 0:HR16]))
        with ExitStack() as ctx2:
            chain_sem = ctx2.enter_context(nc.semaphore("r_chain"))
            topped = ctx2.enter_context(nc.semaphore("r_topped"))
            spread = ctx2.enter_context(nc.semaphore("r_spread"))
            tabled = ctx2.enter_context(nc.semaphore("r_tabled"))
            stored = ctx2.enter_context(nc.semaphore("r_stored"))
            block = ctx2.enter_context(nc.Block())

            @block.vector
            def _(dve):
                link = Chain(dve, chain_sem)
                for n, out in enumerate((h20[:, :, HR16:RW], dtab[:, :, 0:HR])):
                    link(dve.tensor_tensor(prod[:], h20[:, :, 0:HR16], att[:, n, :].unsqueeze(1).to_broadcast([P, NT, HR16]), ALU.mult))
                    link(dve.tensor_reduce(out, prod[:].rearrange("p t (h e) -> p t h e", h=HR), AX.X, ALU.add))
                dve.tensor_reduce(top[:, 0, :], h20[:, :, HR16:RW].rearrange("p t h -> p h t"), AX.X, ALU.max).then_inc(topped, 1)
                dve.wait_ge(spread, 1)
                link(dve.tensor_tensor(prod[:, :, 0:HR], dtab[:, :, 0:HR], top[:, 1, :].unsqueeze(1).to_broadcast([P, NT, HR]), ALU.add))
                leaky(dve, dtab[:, :, HR:2 * HR], prod[:, :, 0:HR]).then_inc(tabled, 1)

            @block.gpsimd
            def _(pool):
                pool.wait_ge(topped, 1)
                pool.partition_all_reduce(top[:, 1, :], top[:, 0, :], P, bass.bass_isa.ReduceOp.max).then_inc(spread, 1)

            @block.sync
            def _(sp):
                sp.wait_ge(tabled, 1)
                sp.dma_start(d["h_tab"].rearrange("(t p) w -> p t w", p=P), h20[:]).then_inc(stored, 16)
                sp.dma_start(d["d_tab"].rearrange("(t p) w -> p t w", p=P), dtab[:]).then_inc(stored, 16)
                sp.wait_ge(stored, 32)


def routing_sums(nc, env, d, sums, key):
    SD = -(-ETX // NB2)
    with ExitStack() as ctx:
        def sb(name, shape, dt=F32):
            return ctx.enter_context(nc.sbuf_tensor(fresh(name), shape, dt))

        def sem(name):
            return ctx.enter_context(nc.semaphore(name))
        ends = sb("g_ends", [P, ET2 + HALVES * BT, 2], I32)
        bits = sb("g_bits", [P, 2, ET2], I32)
        lowhigh = sb("g_lowhigh", [P, 2, ET2])
        idx = sb("g_idx", [P, HALVES, BT, 2], I32)
        hrow = sb("g_hrow", [P, HALVES, BT, RW])
        drow = sb("g_drow", [P, HALVES, BT, 2 * HR])
        score = sb("g_score", [P, HALVES, BT, HR])
        value = sb("g_value", [P, HALVES, BT, RW])
        low = sb("g_low", [P, HALVES, BT, P])
        high = sb("g_high", [P, HALVES, BT, NT])
        spread = sb("g_spread", [P, 4, NT, RW])
        zero = sb("g_zero", [P, OHW // 2])
        srcs = sb("g_srcs", [P, 2, NB2 * SD])
        noise = sb("g_noise", [P, NT])
        d_low = sb("g_d_low", [P, 2, SD, P], BF16)
        d_high = sb("g_d_high", [P, 2, SD, NT], BF16)
        d_zero = sb("g_d_zero", [P, P], BF16)
        pd = ctx.enter_context(nc.psum_tensor(fresh("g_pd"), [P, 512], F32))
        marked, counted = sem("g_marked"), sem("g_counted")
        ps = ctx.enter_context(nc.psum_tensor(fresh("g_ps"), [P, 2, 512], F32))
        loaded, prepared, chain_sem, zeroed = sem("g_loaded"), sem("g_prepared"), sem("g_chain"), sem("g_zeroed")
        idx_ready, rows_used, shifted, exped = sem("g_idx"), sem("g_used"), sem("g_shifted"), sem("g_exped")
        landed = [sem(f"g_landed{n}") for n in range(HALVES)]
        spread_ready, multiplied, done = sem("g_spread"), sem("g_mult"), sem("g_done")
        block = ctx.enter_context(nc.Block())

        @block.sync
        def _(sp):
            sp.dma_start(ends[:], d["ends2"]).then_inc(loaded, 16)
            sp.dma_start(noise[:], d["noise_cols"]).then_inc(loaded, 16)

        @block.gpsimd
        def _(pool):
            with pool.Fori(0, NB2 // HALVES) as i:
                for n in range(HALVES):
                    k = i * HALVES + n
                    pool.wait_ge(idx_ready, k + 1)
                    pool.wait_ge(rows_used, k + 1)
                    pool.nop(nofuse=True)
                    for u in range(BT):
                        gather_rows(pool, d["h_tab"], hrow[:, n, u, :], idx[:, n, u, 0:1], landed[n])
                        gather_rows(pool, d["d_tab"], drow[:, n, u, :], idx[:, n, u, 1:2], landed[n])

        @block.scalar
        def _(act):
            act.wait_ge(prepared, 1)
            for n in range(HALVES):
                act.copy(idx[:, n], ends[:, n * BT:(n + 1) * BT, :]).then_inc(idx_ready, 1)
            with act.Fori(0, NB2 // HALVES) as i:
                for n in range(HALVES):
                    k = i * HALVES + n
                    act.wait_ge(shifted, k + 1)
                    act.activation(value[:, n, :, HR16:RW], score[:, n], ACT.Exp).then_inc(exped, 1)
                    act.wait_ge(landed[n], (i + 1) * (16 * 2 * BT))
                    act.copy(idx[:, n], ends[:, bass.ds((k + HALVES) * BT, BT), :]).then_inc(idx_ready, 1)

        @block.tensor
        def _(pe):
            pe.wait_ge(zeroed, 2)
            for a in range(2):
                pe.matmul(ps[:, a, 0:OHW // 2], zero[:, 0:P], zero[:], start=True, stop=False)
            pe.matmul(pd[:, 0:NT], d_zero[:], d_zero[:, 0:NT], start=True, stop=False)
            with pe.Fori(0, NB2 // HALVES) as i:
                for n in range(HALVES):
                    for u in range(BT):
                        m = (i * HALVES + n) * BT + u
                        pe.wait_ge(spread_ready, m + 1)
                        for a in range(2):
                            ins = pe.matmul(ps[:, a, 0:OHW // 2], low[:, n, u, :],
                                            spread[:, u % 4].rearrange("p b w -> p (b w)")[:, a * (OHW // 2):(a + 1) * (OHW // 2)],
                                            start=False, stop=False)
                        ins.then_inc(multiplied, 1)
                    pe.wait_ge(marked, i * HALVES + n + 1)
                    for u in range(SD):
                        ins = pe.matmul(pd[:, 0:NT], d_low[:, n, u, :], d_high[:, n, u, :], start=False, stop=False)
                    ins.then_inc(counted, 1)
            pe.matmul(pd[:, 0:NT], d_zero[:], d_zero[:, 0:NT], start=False, stop=True)
            for a in range(2):
                ins = pe.matmul(ps[:, a, 0:OHW // 2], zero[:, 0:P], zero[:], start=False, stop=True)
            ins.then_inc(done, 1)

        @block.vector
        def _(dve):
            link = Chain(dve, chain_sem)
            dve.sem_inc(rows_used, HALVES)
            dve.sem_inc(multiplied, BT + 4)
            dve.sem_inc(counted, HALVES)
            dve.memset(zero[:], 0.0).then_inc(zeroed, 1)
            dve.memset(d_zero[:], 0.0).then_inc(zeroed, 1)
            with nc.sbuf_tensor(fresh("g_src_bits"), [P, 2, ETX], I32) as src_bits:
                link(dve.tensor_scalar(src_bits[:, 0, :], env["src"][:], P - 1, None, ALU.bitwise_and))
                link(dve.tensor_scalar(src_bits[:, 1, :], env["src"][:], 7, None, ALU.logical_shift_right))
                link(dve.memset(srcs[:, :, ETX:], float(PAD_DST)))
                link(dve.tensor_copy(srcs[:, :, 0:ETX], src_bits[:]))
            dve.wait_ge(loaded, 32)
            link(dve.tensor_scalar(bits[:, 0, :], ends[:, 0:ET2, 1], P - 1, None, ALU.bitwise_and))
            link(dve.tensor_scalar(bits[:, 1, :], ends[:, 0:ET2, 1], 7, None, ALU.logical_shift_right))
            link(dve.tensor_copy(lowhigh[:], bits[:]))
            link(dve.tensor_scalar(ends[:], ends[:], float(N - 1), None, ALU.min))
            dve.drain().then_inc(prepared, 1)
            with dve.Fori(0, NB2 // HALVES) as i:
                for n in range(HALVES):
                    k = i * HALVES + n
                    t = k * BT
                    dve.wait_ge(landed[n], (i + 1) * (16 * 2 * BT))
                    dve.wait_ge(multiplied, t + 4)
                    dve.tensor_tensor(score[:, n], hrow[:, n, :, HR16:RW], drow[:, n, :, 0:HR], ALU.add).then_inc(chain_sem, 1)
                    dve.wait_ge(chain_sem, k * 2 + link.n + 1)
                    leaky(dve, score[:, n], score[:, n]).then_inc(chain_sem, 1)
                    dve.wait_ge(chain_sem, k * 2 + link.n + 2)
                    dve.tensor_tensor(score[:, n], score[:, n], drow[:, n, :, HR:2 * HR], ALU.subtract).then_inc(shifted, 1)
                    dve.tensor_tensor(low[:, n], env["iota"][:].unsqueeze(1).to_broadcast([P, BT, P]),
                                      bc(lowhigh[:, 0, bass.ds(t, BT)], [P, BT, P]), ALU.is_equal)
                    dve.tensor_tensor(high[:, n], env["iota"][:, 0:NT].unsqueeze(1).to_broadcast([P, BT, NT]),
                                      bc(lowhigh[:, 1, bass.ds(t, BT)], [P, BT, NT]), ALU.is_equal)
                    dve.wait_ge(counted, k + 1)
                    dve.tensor_tensor(d_low[:, n], env["iota"][:].unsqueeze(1).to_broadcast([P, SD, P]),
                                      bc(srcs[:, 0, bass.ds(k * SD, SD)], [P, SD, P]), ALU.is_equal)
                    dve.tensor_tensor(d_high[:, n], env["iota"][:, 0:NT].unsqueeze(1).to_broadcast([P, SD, NT]),
                                      bc(srcs[:, 1, bass.ds(k * SD, SD)], [P, SD, NT]), ALU.is_equal).then_inc(marked, 1)
                    dve.wait_ge(exped, k + 1)
                    dve.tensor_tensor(value[:, n, :, 0:HR16].rearrange("p u (h e) -> p u h e", h=HR),
                                      hrow[:, n, :, 0:HR16].rearrange("p u (h e) -> p u h e", h=HR),
                                      bc(value[:, n, :, HR16:RW], [P, BT, HR, NX]), ALU.mult).then_inc(rows_used, 1)
                    dve.wait_ge(rows_used, k + 1 + HALVES)
                    for u in range(BT):
                        dve.wait_ge(multiplied, t + u + 1 + BT)
                        dve.tensor_tensor(spread[:, u % 4], high[:, n, u, :].unsqueeze(2).to_broadcast([P, NT, RW]),
                                          value[:, n, u, :].unsqueeze(1).to_broadcast([P, NT, RW]), ALU.mult).then_inc(spread_ready, 1)
            dve.wait_ge(done, 1)
            dve.tensor_tensor(key[:], pd[:, 0:NT], noise[:], ALU.add)
            flat = sums[:].rearrange("p b w -> p (b w)")
            for a in range(2):
                dve.tensor_copy(flat[:, a * (OHW // 2):(a + 1) * (OHW // 2)], ps[:, a, 0:OHW // 2])


def routing_gates(nc, env, d, h20, dtab, sums, gates):
    T = [P, NT, HR]
    with ExitStack() as ctx:
        def sb(name, shape, dt=F32):
            return ctx.enter_context(nc.sbuf_tensor(fresh(name), shape, dt))
        z = sb("t_z", [P, NT, HR])
        p = sb("t_p", [P, NT, HR])
        loop = sb("t_loop", [P, NT, HR16])
        agg = sb("t_agg", [P, NT, HR16])
        score = sb("t_score", [P, NT, NX])
        rank = sb("t_rank", [P, NT, NX])
        cmp = sb("t_cmp", [P, NT])
        one = sb("t_one", [P, 2, NT])
        rows = sb("t_rows", [P, 3, HR16])
        load_all(nc, [(rows[:, 0, :], d["b_gat"].partition_broadcast(P)),
                      (rows[:, 1, :], d["ln_gamma"].partition_broadcast(P)),
                      (rows[:, 2, :], d["ln_beta"].partition_broadcast(P))])
        with ExitStack() as ctx2:
            chain_sem = ctx2.enter_context(nc.semaphore("t_chain"))
            ready = ctx2.enter_context(nc.semaphore("t_ready"))
            exped = ctx2.enter_context(nc.semaphore("t_exped"))
            block = ctx2.enter_context(nc.Block())

            @block.vector
            def _(dve):
                link = Chain(dve, chain_sem)
                link(dve.tensor_tensor(z[:], h20[:, :, HR16:RW], dtab[:, :, 0:HR], ALU.add))
                link(leaky(dve, z[:], z[:]))
                dve.tensor_tensor(z[:], z[:], dtab[:, :, HR:2 * HR], ALU.subtract).then_inc(ready, 1)
                dve.wait_ge(exped, 1)
                link(dve.tensor_tensor(loop[:].rearrange("p t (h e) -> p t h e", h=HR),
                                       h20[:, :, 0:HR16].rearrange("p t (h e) -> p t h e", h=HR),
                                       bc(p[:], [P, NT, HR, NX]), ALU.mult))
                link(dve.tensor_tensor(loop[:], loop[:], sums[:, :, 0:HR16], ALU.add))
                link(dve.tensor_tensor(p[:], p[:], sums[:, :, HR16:RW], ALU.add))
                link(dve.tensor_scalar(p[:], p[:], 1e-16, None, ALU.add))
                link(dve.reciprocal(z[:], p[:]))
                link(dve.tensor_tensor(agg[:].rearrange("p t (h e) -> p t h e", h=HR),
                                       loop[:].rearrange("p t (h e) -> p t h e", h=HR),
                                       bc(z[:], [P, NT, HR, NX]), ALU.mult))
                link(dve.tensor_tensor(agg[:], agg[:], rows[:, 0, :].unsqueeze(1).to_broadcast([P, NT, HR16]), ALU.add))

            @block.scalar
            def _(act):
                act.wait_ge(ready, 1)
                act.activation(p[:], z[:], ACT.Exp).then_inc(exped, 1)

        layernorm(nc, agg[:], agg[:], loop[:], rows[:, 1, :], rows[:, 2, :])
        with ExitStack() as ctx2:
            chain_sem = ctx2.enter_context(nc.semaphore("t_chain2"))
            ready = ctx2.enter_context(nc.semaphore("t_ready2"))
            exped = ctx2.enter_context(nc.semaphore("t_exped2"))
            block = ctx2.enter_context(nc.Block())

            @block.vector
            def _(dve):
                link = Chain(dve, chain_sem)
                link(dve.tensor_reduce(score[:], agg[:].rearrange("p t (h e) -> p t e h", h=HR), AX.X, ALU.add))
                link(dve.tensor_scalar(score[:], score[:], 1.0 / HR, None, ALU.mult))
                link(dve.memset(rank[:], 0.0))
                for e in range(NX):
                    for o in range(NX):
                        if o != e:
                            link(dve.tensor_tensor(cmp[:], score[:, :, o], score[:, :, e], ALU.is_ge if o < e else ALU.is_gt))
                            link(dve.tensor_tensor(rank[:, :, e], rank[:, :, e], cmp[:], ALU.add))
                link(dve.tensor_scalar(rank[:], rank[:], 2.0, None, ALU.is_lt))
                link(dve.tensor_reduce(one[:, 0, :], score[:], AX.X, ALU.max))
                dve.tensor_tensor(score[:], score[:], bc(one[:, 0, :], [P, NT, NX]), ALU.subtract).then_inc(ready, 1)
                dve.wait_ge(exped, 1)
                link(dve.tensor_tensor(z[:], z[:], rank[:], ALU.mult))
                link(dve.tensor_reduce(one[:, 0, :], z[:], AX.X, ALU.add))
                link(dve.reciprocal(one[:, 1, :], one[:, 0, :]))
                link(dve.tensor_tensor(gates[:], z[:], bc(one[:, 1, :], [P, NT, NX]), ALU.mult))

            @block.scalar
            def _(act):
                act.wait_ge(ready, 1)
                act.activation(z[:], score[:], ACT.Exp).then_inc(exped, 1)


def expert_ffn(nc, xT, gates, x, w1, b1, w2, b2, experts, shared, func=ACT.Gelu, route=None, stream=None, count=None):
    HC = w2.shape[1] // experts
    layers = 1 if shared else experts
    HS, OS = 2, 4
    with ExitStack() as ctx:
        hT = ctx.enter_context(nc.sbuf_tensor(fresh("ff_hT"), [P, HC, GN], F32))
        biased = ctx.enter_context(nc.sbuf_tensor(fresh("ff_out"), [P, 2, D], F32))
        ph = ctx.enter_context(nc.psum_tensor(fresh("ff_ph"), [P, HS, 512], F32))
        po = ctx.enter_context(nc.psum_tensor(fresh("ff_po"), [P, OS, 512], F32))
        h_made = ctx.enter_context(nc.semaphore("ff_h_made"))
        h_ready = ctx.enter_context(nc.semaphore("ff_h_ready"))
        o_made = ctx.enter_context(nc.semaphore("ff_o_made"))
        o_used = ctx.enter_context(nc.semaphore("ff_o_used"))
        added = ctx.enter_context(nc.semaphore("ff_added"))
        x_loaded = ctx.enter_context(nc.semaphore("ff_x_loaded"))
        x_stored = ctx.enter_context(nc.semaphore("ff_x_stored"))
        r_made = ctx.enter_context(nc.semaphore("ff_r_made"))
        r_shifted = ctx.enter_context(nc.semaphore("ff_r_shifted"))
        r_exped = ctx.enter_context(nc.semaphore("ff_r_exped"))
        r_chain = ctx.enter_context(nc.semaphore("ff_r_chain"))
        if route:
            wg, bg, countdown = route
            pr = ctx.enter_context(nc.psum_tensor(fresh("ff_pr"), [P, 512], F32))
            lg = ctx.enter_context(nc.sbuf_tensor(fresh("ff_lg"), [P, 4, U, NE], F32))
            one = ctx.enter_context(nc.sbuf_tensor(fresh("ff_one"), [P, 3, U], F32))
        smaller = ctx.enter_context(nc.semaphore("ff_smaller"))
        equal = ctx.enter_context(nc.semaphore("ff_equal"))
        if count:
            key, keys, earlier, trash, part = count
        block = ctx.enter_context(nc.Block())
        per = experts // layers
        NH = layers * HC * 2
        NO = experts * U
        assert NH % HS == 0
        before = [m - OS if m >= OS else max(b for b in range(NO) if b % OS == m) - NO for m in range(NO)]

        @block.tensor
        def _(pe):
            with pe.Fori(0, GROUPS) as g:
                for layer in range(layers):
                    for c in range(HC):
                        for half in range(2):
                            n = (layer * HC + c) * 2 + half
                            pe.wait_ge(h_ready, g * NH + n + 1)
                            for k in range(KC):
                                ins = pe.matmul(ph[:, n % HS, 0:GC], w1[:, k, (layer * HC + c) * P:(layer * HC + c + 1) * P],
                                                xT[:, k, bass.ds(g * GN + half * GC, GC)], start=(k == 0), stop=(k == KC - 1))
                            ins.then_inc(h_made, 1)
                    if route:
                        pe.wait_ge(h_ready, g * NH + (layer + 1) * HC * 2 + HS)
                        pe.wait_ge(r_shifted, g + 1)
                        for u in range(U):
                            for c in range(HC):
                                ins = pe.matmul(pr[:, u * NE:(u + 1) * NE], hT[:, c, u * P:(u + 1) * P], wg[:, c, :],
                                                start=(c == 0), stop=(c == HC - 1))
                        ins.then_inc(r_made, 1)
                    for e in range(layer * per, (layer + 1) * per):
                        for u in range(U):
                            m = e * U + u
                            pe.wait_ge(h_ready, g * NH + (layer + 1) * HC * 2 + HS)
                            pe.wait_ge(o_used, g * NO + before[m] + 1 + NO)
                            for c in range(HC):
                                ins = pe.matmul(po[:, m % OS, 0:D], hT[:, c, u * P:(u + 1) * P], w2[:, e * HC + c, :],
                                                start=(c == 0), stop=(c == HC - 1))
                            ins.then_inc(o_made, 1)

        @block.scalar
        def _(act):
            act.sem_inc(h_ready, HS)
            act.sem_inc(o_made, NO)
            act.sem_inc(smaller, 1)

            def count_smaller(t):
                act.wait_ge(smaller, t + 1)
                act.activation(trash[:, 1, :], keys[:], ACT.Sign, bias=key[:, bass.ds(t, 1)], scale=-1.0,
                               accum_out=part[:, 1, bass.ds(t, 1)]).then_inc(smaller, 1)

            with act.Fori(0, GROUPS) as g:
                for layer in range(layers):
                    act.wait_ge(o_made, g * NO + layer * per * U + NO)
                    for c in range(HC):
                        for half in range(2):
                            n = (layer * HC + c) * 2 + half
                            act.wait_ge(h_made, g * NH + n + 1)
                            act.activation(hT[:, c, half * GC:(half + 1) * GC], ph[:, n % HS, 0:GC], func,
                                           bias=b1[:, layer * HC + c:layer * HC + c + 1]).then_inc(h_ready, 1)
                    if count:
                        for u in range(layer * U // layers, (layer + 1) * U // layers):
                            count_smaller(g * U + u)
                    if route:
                        act.wait_ge(r_shifted, g + 2)
                        act.activation(lg[:, 2], lg[:, 1], ACT.Exp).then_inc(r_exped, 1)

        @block.vector
        def _(dve):
            dve.sem_inc(o_used, NO)
            dve.sem_inc(added, 2)
            dve.sem_inc(r_shifted, 1)
            dve.sem_inc(equal, 1)

            def count_equal(t):
                dve.wait_ge(equal, t + 1)
                dve.scalar_tensor_tensor(trash[:, 0, :], keys[:], key[:, bass.ds(t, 1)], earlier[:, bass.ds(NP - t * P, NP)],
                                         ALU.is_equal, ALU.mult, accum_out=part[:, 0, bass.ds(t, 1)]).then_inc(equal, 1)

            with dve.Fori(0, GROUPS) as g:
                if route:
                    full = [P, U, NE]
                    steps = Steps(dve, r_chain, g, 7)
                    dve.wait_ge(r_made, g + 1)
                    steps(dve.tensor_tensor(lg[:, 0], pr[:, 0:U * NE].rearrange("p (u e) -> p u e", e=NE),
                                            bg.unsqueeze(1).to_broadcast(full), ALU.add))
                    steps(dve.tensor_reduce(one[:, 0, :], lg[:, 0], AX.X, ALU.max))
                    dve.tensor_tensor(lg[:, 1], lg[:, 0], bc(one[:, 0, :], full), ALU.subtract).then_inc(r_shifted, 1)
                    dve.wait_ge(r_exped, g * 2 + 1)
                    steps(dve.tensor_reduce(one[:, 1, :], lg[:, 2], AX.X, ALU.add))
                    steps(dve.scalar_tensor_tensor(lg[:, 0].rearrange("p u e -> p (u e)"), lg[:, 1].rearrange("p u e -> p (u e)"), 0.0,
                                                   countdown, ALU.is_equal, ALU.mult))
                    steps(dve.tensor_reduce(one[:, 0, :], lg[:, 0], AX.X, ALU.max))
                    steps(dve.reciprocal(one[:, 2, :], one[:, 1, :]))
                    steps(dve.tensor_tensor(lg[:, 3], lg[:, 0], bc(one[:, 0, :], full), ALU.is_equal))
                    dve.tensor_tensor(gates[:, bass.ds(g * U, U), :], lg[:, 3], bc(one[:, 2, :], full), ALU.mult).then_inc(r_exped, 1)
                    dve.wait_ge(r_exped, g * 2 + 2)
                if stream:
                    dve.wait_ge(x_loaded, g * 16 + 16)
                for e in range(experts):
                    for u in range(U):
                        m = e * U + u
                        t = g * U + u
                        xt = x[:, u, :] if stream else tile(x, t)
                        dve.wait_ge(o_made, g * NO + m + 1 + NO)
                        dve.wait_ge(added, g * NO + m + 1 + (NO % 2 if m == 0 else 0))
                        dve.tensor_tensor(biased[:, m % 2, :], po[:, m % OS, 0:D], b2[:, e, :], ALU.add).then_inc(o_used, 1)
                        dve.wait_ge(o_used, g * NO + m + 1 + NO)
                        dve.scalar_tensor_tensor(xt, biased[:, m % 2, :], tile(gates[:, :, e:e + 1], t), xt,
                                                 ALU.mult, ALU.add).then_inc(added, 1)
                        if count and m % experts == experts - 1:
                            count_equal(g * U + m // experts)

        if stream:
            @block.sync
            def _(sp):
                with sp.Fori(0, GROUPS) as g:
                    sp.dma_start(x[:], rows_of(stream[0])[:, bass.ds(g * U, U), :]).then_inc(x_loaded, 16)
                    sp.wait_ge(added, g * NO + NO + 2)
                    sp.nop(nofuse=True)
                    sp.dma_start(rows_of(stream[1])[:, bass.ds(g * U, U), :], x[:]).then_inc(x_stored, 16)
                    sp.wait_ge(x_stored, g * 16 + 16)
                    sp.nop(nofuse=True)


def rank_tables(nc, env, d, key, keys, earlier):
    with ExitStack() as ctx:
        def sem(name):
            return ctx.enter_context(nc.semaphore(name))
        col = ctx.enter_context(nc.sbuf_tensor(fresh("k_col"), [P, 1], F32))
        stored, loaded, col_ready, chain_sem = sem("k_stored"), sem("k_loaded"), sem("k_col"), sem("k_chain")
        block = ctx.enter_context(nc.Block())

        @block.sync
        def _(sp):
            sp.dma_start(d["key_line"].rearrange("(t p) -> p t", p=P), key[:], allow_slow_non_contiguous=True).then_inc(stored, 16)
            sp.wait_ge(stored, 16)
            sp.dma_start(keys[:], d["key_line"].partition_broadcast(P)).then_inc(loaded, 16)
            sp.wait_ge(loaded, 16)

        @block.gpsimd
        def _(pool):
            pool.iota(col[:], pattern=[[0, 1]], base=0, channel_multiplier=1,
                      allow_small_or_imprecise_dtypes=True).then_inc(col_ready, 1)

        @block.vector
        def _(dve):
            link = Chain(dve, chain_sem)
            link(dve.memset(earlier[:, 0:NP], 0.5))
            link(dve.memset(earlier[:, NP:2 * NP], -0.5))
            dve.wait_ge(col_ready, 1)
            link(dve.tensor_scalar(earlier[:, NP:NP + P], env["iota"][:], col[:], -0.5, ALU.is_lt, ALU.add))


def ranks(nc, part, rank):
    with nc.semaphore("k_rank") as chain_sem, nc.Block() as block:
        @block.vector
        def _(dve):
            link = Chain(dve, chain_sem)
            link(dve.tensor_scalar(part[:, 1, :], part[:, 1, :], float(NP), 0.5, ALU.add, ALU.mult))
            link(dve.tensor_tensor(part[:, 0, :], part[:, 0, :], part[:, 1, :], ALU.add))
            link(dve.tensor_copy(rank[:], part[:, 0, :]))


def move_rows(nc, env, rank, table, buf, gather):
    with ExitStack() as ctx:
        slot = ctx.enter_context(nc.sbuf_tensor(fresh("v_slot"), [P, U, D], F32))
        idx = ctx.enter_context(nc.sbuf_tensor(fresh("v_idx"), [P, U], I32))
        idx_ready = ctx.enter_context(nc.semaphore("v_idx"))
        slot_ready = ctx.enter_context(nc.semaphore("v_slot"))
        group_moved = ctx.enter_context(nc.semaphore("v_group"))
        moved = [ctx.enter_context(nc.semaphore(f"v_moved{u}")) for u in range(U)]
        block = ctx.enter_context(nc.Block())

        @block.vector
        def _(dve):
            if gather:
                dve.sem_inc(slot_ready, U)
            else:
                dve.sem_inc(group_moved, 1)
            with dve.Fori(0, GROUPS) as g:
                if gather:
                    dve.wait_ge(slot_ready, g * U + U)
                    dve.tensor_copy(idx[:], rank[:, bass.ds(g * U, U)]).then_inc(idx_ready, 1)
                    for u in range(U):
                        dve.wait_ge(moved[u], g * 16 + 16)
                        dve.tensor_copy(tile(buf, g * U + u), slot[:, u, :]).then_inc(slot_ready, 1)
                else:
                    dve.wait_ge(group_moved, g + 1)
                    dve.tensor_copy(idx[:], rank[:, bass.ds(g * U, U)]).then_inc(idx_ready, 1)
                    for u in range(U):
                        dve.tensor_copy(slot[:, u, :], tile(buf, g * U + u)).then_inc(slot_ready, 1)

        @block.gpsimd
        def _(pool):
            with pool.Fori(0, GROUPS) as g:
                pool.wait_ge(idx_ready, g + 1)
                pool.nop(nofuse=True)
                for u in range(U):
                    if gather:
                        gather_rows(pool, table, slot[:, u, :], idx[:, u:u + 1], moved[u])
                    else:
                        pool.wait_ge(slot_ready, g * U + u + 1)
                        pool.nop(nofuse=True)
                        pool.indirect_dma_start(table, bass.IndirectOffsetOnAxis(ap=idx[:, u:u + 1], axis=0),
                                                slot[:, u, :], None).then_inc(moved[u], 16)
                if not gather:
                    for u in range(U):
                        pool.wait_ge(moved[u], g * 16 + 16)
                    pool.sem_inc(group_moved, 1)


def attention_tables(nc, env, d, x2n, rows, tgt):
    with ExitStack() as ctx:
        w = ctx.enter_context(nc.sbuf_tensor(fresh("o_w"), [P, KC, D], F32))
        att = ctx.enter_context(nc.sbuf_tensor(fresh("o_att"), [P, 2, D], F32))
        top = ctx.enter_context(nc.sbuf_tensor(fresh("o_top"), [P, 2, H1], F32))
        z = ctx.enter_context(nc.sbuf_tensor(fresh("o_z"), [P, NT, H1], F32))
        load_all(nc, [(w[:], d["gat_wT"].rearrange("(k p) m -> p k m", p=P)),
                      (att[:, 0, :], d["gat_a_src"].partition_broadcast(P)),
                      (att[:, 1, :], d["gat_a_tgt"].partition_broadcast(P))])
        project_tiles(nc, x2n, w, env["ident"],
                      lambda dve, out, t: dve.tensor_copy(tile(rows[:, :, 0:D], t), out[:, 0:D]))
        chain_sem = ctx.enter_context(nc.semaphore("o_chain"))
        topped = ctx.enter_context(nc.semaphore("o_topped"))
        spread = ctx.enter_context(nc.semaphore("o_spread"))
        stored = ctx.enter_context(nc.semaphore("o_stored"))
        block = ctx.enter_context(nc.Block())

        @block.vector
        def _(dve):
            link = Chain(dve, chain_sem)
            for n, out in enumerate((rows[:, :, D:PW], tgt[:, :, 0:H1])):
                link(dve.tensor_tensor(x2n[:], rows[:, :, 0:D], att[:, n, :].unsqueeze(1).to_broadcast([P, NT, D]), ALU.mult))
                link(dve.tensor_reduce(out, x2n[:].rearrange("p t (h c) -> p t h c", h=H1), AX.X, ALU.add))
            dve.tensor_reduce(top[:, 0, :], rows[:, :, D:PW].rearrange("p t h -> p h t"), AX.X, ALU.max).then_inc(topped, 1)
            link(dve.memset(tgt[:, :, 2 * H1:TW], 1.0))
            dve.wait_ge(spread, 1)
            link(dve.tensor_tensor(z[:], tgt[:, :, 0:H1], top[:, 1, :].unsqueeze(1).to_broadcast([P, NT, H1]), ALU.add))
            link(leaky(dve, tgt[:, :, H1:2 * H1], z[:]))

        @block.gpsimd
        def _(pool):
            pool.wait_ge(topped, 1)
            pool.partition_all_reduce(top[:, 1, :], top[:, 0, :], P, bass.bass_isa.ReduceOp.max).then_inc(spread, 1)

        @block.sync
        def _(sp):
            sp.wait_ge(topped, 1)
            sp.dma_start(rows_of(d["proj_tab"]), rows[:]).then_inc(stored, 16)
            sp.wait_ge(stored, 16)


def second_attention(nc, env, d, tgt, acc, top):
    G, SLOTS, PS = 4, 4, 4
    NG = STEPS // G
    TURNS = NG // SLOTS
    CA = 1 + SLOTS * G
    with ExitStack() as ctx:
        def sb(name, shape, dt=F32):
            return ctx.enter_context(nc.sbuf_tensor(fresh(name), shape, dt))

        def sem(name):
            return ctx.enter_context(nc.semaphore(name))

        def banks(name, n):
            return ctx.enter_context(nc.psum_tensor(fresh(name), [P, n, 512], F32))
        idx = sb("h_idx", [P, SLOTS, G], I32)
        rows = sb("h_rows", [P, SLOTS, G, PW])
        msg = sb("h_msg", [P, SLOTS, G, PW])
        oh = sb("h_oh", [P, SLOTS, G, P])
        ohT = sb("h_ohT", [P, SLOTS, G, P])
        side = sb("h_side", [P, SLOTS, G, TW])
        z = sb("h_z", [P, SLOTS, G, H1])
        e = sb("h_e", [P, SLOTS, G, H1])
        shift = sb("h_shift", [P, SLOTS, G, H1])
        valid = sb("h_valid", [P, SLOTS, G])
        cand = sb("h_cand", [P, SLOTS, G, H1])
        best = sb("h_best", [P, SLOTS, G, H1])
        pT, pS, pa = banks("h_pT", 2), banks("h_pS", 2), banks("h_pa", PS)
        idx_ready, oh_ready, turned, ohT_ready = sem("h_idx"), sem("h_oh"), sem("h_turned"), sem("h_ohT")
        sides_made, side_ready, scored, exped = sem("h_sides_made"), sem("h_side"), sem("h_scored"), sem("h_exped")
        msg_ready, made, added, bested, chain_sem = (
            sem("h_msg"), sem("h_made"), sem("h_added"), sem("h_bested"), sem("h_chain"))
        landed = [sem(f"h_landed{n}") for n in range(SLOTS)]
        block = ctx.enter_context(nc.Block())

        @block.gpsimd
        def _(pool):
            def fetch(k, n):
                pool.wait_ge(idx_ready, k + 1)
                pool.wait_ge(msg_ready, k + 1)
                pool.nop(nofuse=True)
                for u in range(G):
                    gather_rows(pool, d["proj_tab"], rows[:, n, u, :], idx[:, n, u:u + 1], landed[n])

            with pool.Fori(0, TURNS) as i:
                for n in range(SLOTS):
                    fetch(i * SLOTS + n, n)
            for n in range(2):
                fetch(NG + n, n)

        @block.scalar
        def _(act):
            def turn_copy(k, n):
                act.wait_ge(turned, k + 1)
                act.wait_ge(sides_made, k + 1)
                act.copy(ohT[:, n % SLOTS], pT[:, n % 2, 0:G * P].rearrange("p (u e) -> p u e", u=G)).then_inc(ohT_ready, 1)

            def side_copy(k, n):
                act.wait_ge(sides_made, k + 1 + SLOTS)
                act.copy(side[:, n % SLOTS], pS[:, n % 2, 0:G * TW].rearrange("p (u w) -> p u w", u=G)).then_inc(side_ready, 1)

            def exps(k, n):
                act.wait_ge(scored, k * 3 + 3)
                act.wait_ge(made, k * G + G)
                act.activation(msg[:, n % SLOTS, :, D:PW], shift[:, n % SLOTS], ACT.Exp).then_inc(exped, 1)

            def indices(k, n, rounds, b):
                act.wait_ge(landed[n % SLOTS], rounds * (16 * G))
                for u in range(G):
                    t = tile_of(nc, k * G + u, b[u])
                    ins = act.copy(idx[:, n % SLOTS, u:u + 1], env["src"][:, bass.ds(t, 1)])
                ins.then_inc(idx_ready, 1)

            act.copy(idx[:].rearrange("p k u -> p (k u)"), env["src"][:, 0:SLOTS * G]).then_inc(idx_ready, SLOTS)
            b = blocks_of(nc, act, env, SLOTS * G, 2 * G)
            for k in range(3):
                turn_copy(k, k)
                side_copy(k, k)
                if k < 2:
                    exps(k, k)
                    indices(k + SLOTS, k, 1, b[k * G:])
            with act.Fori(0, TURNS) as i:
                b = blocks_of(nc, act, env, (i * SLOTS + 6) * G, SLOTS * G)
                for n in range(SLOTS):
                    j = i * SLOTS + n
                    turn_copy(j + 3, n + 3)
                    exps(j + 2, n + 2)
                    act.wait_ge(bested, i + (2 if n == SLOTS - 1 else 1))
                    side_copy(j + 3, n + 3)
                    indices(j + 6, n + 2, i + 1 + (n + 2) // SLOTS, b[n * G:])

        @block.tensor
        def _(pe):
            def turn(k, n):
                pe.wait_ge(oh_ready, k + 1)
                pe.wait_ge(ohT_ready, k + 1)
                for u in range(G):
                    ins = pe.transpose(pT[:, n % 2, u * P:(u + 1) * P], oh[:, n % SLOTS, u, :], env["ident"][:])
                ins.then_inc(turned, 1)

            def dst_sides(k, n, b):
                pe.wait_ge(ohT_ready, k + 1 + 2)
                pe.wait_ge(side_ready, k + 1)
                for u in range(G):
                    ins = pe.matmul(pS[:, n % 2, u * TW:(u + 1) * TW], ohT[:, n % SLOTS, u, :], tile(tgt, b[u]), start=True, stop=True)
                ins.then_inc(sides_made, 1)

            def sums(k, n):
                pe.wait_ge(msg_ready, k + 1 + SLOTS)
                for u in range(G):
                    pe.wait_ge(added, k * G + u + 1 + CA - PS)
                    pe.matmul(pa[:, u, 0:PW], oh[:, n % SLOTS, u, :], msg[:, n % SLOTS, u, :],
                              start=True, stop=True).then_inc(made, 1)

            pe.sem_inc(sides_made, SLOTS)
            pe.sem_inc(made, SLOTS * G)
            b = blocks_of(nc, pe, env, 0, 3 * G)
            for k in range(3):
                turn(k, k)
                dst_sides(k, k, b[k * G:])
            sums(0, 0)
            with pe.Fori(0, TURNS) as i:
                for n in range(SLOTS):
                    j = i * SLOTS + n
                    turn(j + 3, n + 3)
                    if n == 0:
                        b = blocks_of(nc, pe, env, (i * SLOTS + 3) * G, SLOTS * G)
                    sums(j + 1, n + 1)
                    dst_sides(j + 3, n + 3, b[n * G:])

        @block.vector
        def _(dve):
            def mark(k, n, u, t):
                if u == 0:
                    dve.wait_ge(made, k * G + G)
                ins = one_hot(dve, env, oh[:, n % SLOTS, u, :], k * G + u, t[u])
                if u == G - 1:
                    ins.then_inc(oh_ready, 1)

            def sum_sides(k, n, rounds):
                n = n % SLOTS
                dve.wait_ge(landed[n], rounds * (16 * G))
                dve.wait_ge(side_ready, k + 1 + 2)
                dve.tensor_tensor(z[:, n], rows[:, n, :, D:PW], side[:, n, :, 0:H1], ALU.add).then_inc(scored, 1)

            def bend(k, n):
                dve.wait_ge(scored, k * 3 + 1)
                leaky(dve, e[:, n % SLOTS], z[:, n % SLOTS]).then_inc(scored, 1)

            def shifts(k, n):
                n = n % SLOTS
                dve.wait_ge(scored, k * 3 + 2)
                dve.tensor_tensor(shift[:, n], e[:, n], side[:, n, :, H1:2 * H1], ALU.subtract).then_inc(scored, 1)

            def best_valid(groups):
                dve.tensor_scalar(valid[:, 0:groups], side[:, 0:groups, :, 2 * H1], -1.0, -NEG, ALU.add, ALU.mult).then_inc(chain_sem, 1)

            def best_cand(turn, groups):
                dve.wait_ge(chain_sem, turn * 2 + 1)
                dve.tensor_tensor(cand[:, 0:groups], e[:, 0:groups], bc(valid[:, 0:groups], [P, groups, G, H1]), ALU.add).then_inc(chain_sem, 1)

            def best_max(turn, groups):
                dve.wait_ge(chain_sem, turn * 2 + 2)
                dve.tensor_tensor(best[:, 0:groups], best[:, 0:groups], cand[:, 0:groups], ALU.max).then_inc(bested, 1)

            def weigh(k, n):
                n = n % SLOTS
                dve.wait_ge(exped, k + 1)
                dve.tensor_tensor(msg[:, n, :, 0:D].rearrange("p u (h c) -> p u h c", h=H1),
                                  rows[:, n, :, 0:D].rearrange("p u (h c) -> p u h c", h=H1),
                                  bc(msg[:, n, :, D:PW], [P, G, H1, HD1]), ALU.mult).then_inc(msg_ready, 1)

            def add(k, n, u, b):
                b = nc.s_assert_within(b[u], 0, NT - 1, skip_runtime_bounds_check_because="a block of nodes")
                count = k * G + u + CA
                dve.wait_ge(made, count)
                dve.wait_ge(added, count)
                dve.tensor_tensor(tile(acc, b), tile(acc, b), pa[:, u, 0:PW], ALU.add).then_inc(added, 1)

            dve.sem_inc(msg_ready, SLOTS)
            dve.sem_inc(ohT_ready, 2)
            dve.sem_inc(side_ready, 2)
            for k in range(BLEAD):
                for u in range(G):
                    mark(k, k, u, [k * G + v for v in range(G)])
            dve.memset(acc[:], 0.0).then_inc(added, 1)
            dve.memset(best[:], NEG).then_inc(added, CA - 1)
            dve.wait_ge(added, CA)
            for k in range(2):
                sum_sides(k, k, 1)
                bend(k, k)
                shifts(k, k)
            weigh(0, 0)
            best_valid(2)
            best_cand(0, 2)
            best_max(0, 2)
            with dve.Fori(0, TURNS) as i:
                for n in range(SLOTS):
                    j = i * SLOTS + n
                    weigh(j + 1, n + 1)
                    v = group_of(nc, dve, env["block_fours"], j, ETX - 1, 2 * G)
                    sum_sides(j + 2, n + 2, i + 1 + (n + 2) // SLOTS)
                    t = v[G:]
                    add(j, n, 0, v)
                    bend(j + 2, n + 2)
                    mark(j + BLEAD, n + BLEAD, 0, t)
                    add(j, n, 1, v)
                    shifts(j + 2, n + 2)
                    mark(j + BLEAD, n + BLEAD, 1, t)
                    if n == SLOTS - 1:
                        best_valid(SLOTS)
                    add(j, n, 2, v)
                    if n == SLOTS - 1:
                        best_cand(i + 1, SLOTS)
                    mark(j + BLEAD, n + BLEAD, 2, t)
                    add(j, n, 3, v)
                    if n == SLOTS - 1:
                        dve.wait_ge(bested, i + 1)
                        best_max(i + 1, SLOTS)
                    mark(j + BLEAD, n + BLEAD, 3, t)
            dve.wait_ge(bested, TURNS + 1)
            dve.tensor_reduce(top[:, 0:1], best[:].rearrange("p k u h -> p (k u h)"), AX.X, ALU.max).then_inc(bested, 1)


TC = GN // 2
CHUNKS = NP // TC
LOG_SMALL = 2.0 ** -6


def mamba(nc, env, d, xT):
    with ExitStack() as ctx:
        def sb(name, shape, dt=F32):
            return ctx.enter_context(nc.sbuf_tensor(fresh(name), shape, dt))

        def sem(name):
            return ctx.enter_context(nc.semaphore(name))
        NBC = 3 * 2 * DS
        w_in = sb("b_win", [P, KC, 2 * D])
        w_r = sb("b_wr", [P, KC, DTR])
        w_bc = sb("b_wbc", [P, KC, 3, 2 * DS])
        w_dt = sb("b_wdt", [DTR, D])
        col = sb("b_col", [P, 3, KC])
        conv = sb("b_conv", [P, KC, CONV])
        A = sb("b_A", [P, KC, DS])
        xc = sb("b_xc", [P, KC, TC + CONV - 1])
        cv = sb("b_cv", [P, KC, TC])
        z = sb("b_z", [P, KC, TC])
        low_dt = sb("b_low_dt", [DTR, TC])
        rest = sb("b_rest", [NBC, TC])
        parts = sb("b_parts", [NBC, TC], BF16)
        select = sb("b_select", [NBC, 2 * DS], BF16)
        mag = sb("b_mag", [P, KC, TC])
        u = sb("b_u", [P, KC, TC])
        lg = sb("b_lg", [P, KC, TC])
        small = sb("b_small", [P, KC, TC])
        ser = sb("b_ser", [P, KC, TC])
        dt = sb("b_dt", [P, KC, TC])
        du = sb("b_du", [P, KC, TC])
        dA = sb("b_dA", [P, 2, KC, TC])
        dB = sb("b_dB", [P, 2, KC, TC])
        hs = sb("b_hs", [P, 2, KC, TC])
        Cs = sb("b_Cs", [P, 2, TC])
        hC = sb("b_hC", [P, 2, KC, TC])
        state = sb("b_state", [P, DS, KC])
        y = sb("b_y", [P, KC, TC])
        ps = ctx.enter_context(nc.psum_tensor(fresh("b_ps"), [P, 8, 512], F32))
        loaded, ready, chain_sem = sem("b_loaded"), sem("b_ready"), sem("b_chain")
        in_made, in_read, conved, siluc, dbc_made, dbc_copied, dt_made = (
            sem("b_in_made"), sem("b_in_read"), sem("b_conved"), sem("b_siluc"), sem("b_dbcm"), sem("b_dbcc"), sem("b_dtm"))
        act_dt, split, du_ready, y_done = sem("b_act_dt"), sem("b_split"), sem("b_du"), sem("b_ydone")
        bc_made, c_copied, dA_ready, dB_ready, scanned, hC_ready, y_added = (
            sem("b_bcm"), sem("b_cc"), sem("b_dA"), sem("b_dB"), sem("b_scan"), sem("b_hC"), sem("b_yadd"))
        block = ctx.enter_context(nc.Block())
        LOADS = 11
        DVE_STEPS = 26

        @block.sync
        def _(sp):
            for dst, src in [(w_in[:], d["in_wT"].rearrange("(k p) m -> p k m", p=P)),
                             (w_r[:], d["x_wT"].rearrange("(k p) m -> p k m", p=P)[:, :, 0:DTR])] + [
                             (w_bc[:, :, j, :], d["x_wT"].rearrange("(k p) m -> p k m", p=P)[:, :, DTR:]) for j in range(3)] + [
                             (w_dt[:], d["dt_wT"]), (conv[:], d["conv_w"].rearrange("(k p) m -> p k m", p=P)),
                             (A[:], d["A_log"].rearrange("(k p) m -> p k m", p=P)),
                             (col[:, 0, :], d["conv_b"]),
                             (col[:, 1, :], d["dt_b"]),
                             (col[:, 2, :], d["D_param"])]:
                sp.dma_start(dst, src).then_inc(loaded, 16)

        @block.tensor
        def _(pe):
            pe.wait_ge(loaded, 16 * LOADS)
            with pe.Fori(0, CHUNKS) as g:
                pe.wait_ge(y_done, g + 1)
                for m in range(4):
                    for k in range(KC):
                        ins = pe.matmul(ps[:, m, 0:TC], w_in[:, k, m * P:(m + 1) * P], xT[:, k, bass.ds(g * TC, TC)],
                                        start=(k == 0), stop=(k == KC - 1))
                    if m % 2:
                        ins.then_inc(in_made, 1)
                pe.wait_ge(siluc, g * 2 + 1)
                for k in range(KC):
                    ins = pe.matmul(ps[0:DTR, 7, 0:TC], w_r[:, k, :], cv[:, k, :], start=(k == 0), stop=(k == KC - 1))
                ins.then_inc(dbc_made, 1)
                for k in range(KC):
                    ins = pe.matmul(ps[0:NBC, 4, 0:TC], w_bc[:, k].rearrange("p j m -> p (j m)"), cv[:, k, :],
                                    start=(k == 0), stop=(k == KC - 1))
                ins.then_inc(dbc_made, 1)
                pe.wait_ge(dbc_copied, g * 2 + 1)
                for k in range(KC):
                    ins = pe.matmul(ps[:, 5 + k, 0:TC], w_dt[:, k * P:(k + 1) * P], low_dt[:], start=True, stop=True)
                ins.then_inc(dt_made, 1)

                def add_y(n):
                    pe.wait_ge(hC_ready, g * DS + n + 1 + 2)
                    for k in range(KC):
                        ins = pe.matmul(ps[:, k, 0:TC], env["ident"][:], hC[:, n % 2, k, :],
                                        start=(n == 0), stop=(n == DS - 1))
                    ins.then_inc(y_added, 1)

                for n in range(DS):
                    if n < 2:
                        pe.wait_ge(act_dt, g * 2 + 1)
                        pe.wait_ge(siluc, g * 2 + 2)
                        pe.wait_ge(split, g + 1)
                    pe.wait_ge(dB_ready, g * DS + n + 1)
                    pe.wait_ge(c_copied, g * DS + n + 1)
                    for bank, row in ((2 + n % 2, n), (4 + n % 2, DS + n)):
                        ins = pe.matmul(ps[:, bank, 0:TC], select[:, row:row + 1].to_broadcast([NBC, P]), parts[:],
                                        start=True, stop=True)
                    ins.then_inc(bc_made, 1)
                    if n > 1:
                        add_y(n - 2)
                for n in (DS - 2, DS - 1):
                    add_y(n)

        @block.scalar
        def _(act):
            act.sem_inc(dA_ready, 1)
            act.sem_inc(c_copied, 2)
            act.wait_ge(loaded, 16 * LOADS)
            act.activation(A[:], A[:], ACT.Exp).then_inc(ready, 1)
            act.wait_ge(ready, 1)
            act.mul(A[:], A[:], -1.0).then_inc(ready, 1)
            act.wait_ge(ready, 2)
            with act.Fori(0, CHUNKS) as g:
                act.wait_ge(in_made, g * 2 + 1)
                act.copy(xc[:, :, CONV - 1:], ps[:, 0:2, 0:TC]).then_inc(in_read, 1)
                act.wait_ge(conved, g + 1)
                act.activation(cv[:], cv[:], ACT.Silu).then_inc(siluc, 1)
                act.wait_ge(in_made, g * 2 + 2)
                act.activation(z[:], ps[:, 2:4, 0:TC], ACT.Silu).then_inc(siluc, 1)
                act.wait_ge(dbc_made, g * 2 + 1)
                act.copy(low_dt[:], ps[0:DTR, 7, 0:TC]).then_inc(dbc_copied, 1)
                act.wait_ge(dbc_made, g * 2 + 2)
                act.copy(rest[:], ps[0:NBC, 4, 0:TC]).then_inc(dbc_copied, 1)
                act.wait_ge(dt_made, g + 1)
                for k in range(KC):
                    act.activation(mag[:, k, :], ps[:, 5 + k, 0:TC], ACT.Abs, bias=col[:, 1, k:k + 1])
                for k in range(KC):
                    ins = act.activation(dt[:, k, :], ps[:, 5 + k, 0:TC], ACT.Relu, bias=col[:, 1, k:k + 1])
                ins.then_inc(act_dt, 1)
                act.wait_ge(act_dt, g * 2 + 1)
                act.activation(u[:], mag[:], ACT.Exp, scale=-1.0).then_inc(ready, 1)
                act.wait_ge(ready, g + 3)
                act.activation(lg[:], u[:], ACT.Ln, bias=1.0).then_inc(act_dt, 1)
                act.wait_ge(du_ready, g + 1)
                for n in range(DS):
                    act.wait_ge(scanned, g * DS + n + 1)
                    for k in range(KC):
                        ins = act.activation(dA[:, n % 2, k, :], dt[:, k, :], ACT.Exp, scale=A[:, k, n:n + 1])
                    ins.then_inc(dA_ready, 1)
                    act.wait_ge(bc_made, g * DS + n + 1)
                    act.wait_ge(hC_ready, g * DS + n + 1)
                    act.copy(Cs[:, n % 2, :], ps[:, 4 + n % 2, 0:TC]).then_inc(c_copied, 1)

        @block.gpsimd
        def _(pool):
            pool.sem_inc(y_added, 2)
            pool.sem_inc(hC_ready, 2)
            with pool.Fori(0, CHUNKS) as g:
                for n in range(DS):
                    m = g * DS + n
                    pool.wait_ge(scanned, m + 1 + 2)
                    pool.wait_ge(c_copied, m + 1 + 2)
                    pool.wait_ge(y_added, m + 1)
                    for k in range(KC):
                        ins = pool.tensor_tensor(hC[:, n % 2, k, :], hs[:, n % 2, k, :], Cs[:, n % 2, :], ALU.mult)
                    ins.then_inc(hC_ready, 1)

        @block.vector
        def _(dve):
            dve.sem_inc(y_done, 1)
            dve.sem_inc(dB_ready, 2)
            dve.sem_inc(scanned, 2)
            link = Chain(dve, chain_sem)
            link(dve.memset(state[:], 0.0))
            link(dve.memset(xc[:, :, 0:CONV - 1], 0.0))
            for j in range(3):
                rows = slice(j * 2 * DS, (j + 1) * 2 * DS)
                link(dve.tensor_copy(select[rows, :], env["ident"][rows, rows]))
            dve.wait_ge(loaded, 16 * LOADS)
            with dve.Fori(0, CHUNKS) as g:
                steps = Steps(dve, chain_sem, g, DVE_STEPS)
                steps.n = link.n
                dve.wait_ge(in_read, g + 1)
                for k in range(KC):
                    steps(dve.tensor_scalar(cv[:, k, :], xc[:, k, 0:TC], conv[:, k, 0:1], col[:, 0, k:k + 1], ALU.mult, ALU.add))
                    for j in range(1, CONV):
                        steps(dve.scalar_tensor_tensor(cv[:, k, :], xc[:, k, j:j + TC], conv[:, k, j:j + 1], cv[:, k, :], ALU.mult, ALU.add))
                dve.tensor_copy(small[:, :, 0:CONV - 1], xc[:, :, TC:TC + CONV - 1]).then_inc(conved, 1)
                dve.wait_ge(conved, g + 1)
                steps(dve.tensor_copy(xc[:, :, 0:CONV - 1], small[:, :, 0:CONV - 1]))
                dve.wait_ge(dbc_copied, g * 2 + 2)
                steps(dve.tensor_copy(parts[:], rest[:]))
                for rows in (slice(0, 4 * DS), slice(0, 2 * DS)):
                    steps(dve.tensor_tensor(rest[rows, :], rest[rows, :], parts[rows, :], ALU.subtract))
                    ins = dve.tensor_copy(parts[rows, :], rest[rows, :])
                    if rows.stop == 4 * DS:
                        steps(ins)
                ins.then_inc(split, 1)
                dve.wait_ge(act_dt, g * 2 + 2)
                steps(dve.tensor_scalar(small[:], u[:], LOG_SMALL, None, ALU.is_lt))
                steps(dve.tensor_scalar(ser[:], u[:], -0.25, 1.0 / 3.0, ALU.mult, ALU.add))
                steps(dve.tensor_tensor(ser[:], ser[:], u[:], ALU.mult))
                steps(dve.scalar_tensor_tensor(ser[:], ser[:], -0.5, u[:], ALU.add, ALU.mult))
                steps(dve.scalar_tensor_tensor(ser[:], ser[:], 1.0, u[:], ALU.add, ALU.mult))
                steps(dve.tensor_tensor(ser[:], ser[:], lg[:], ALU.subtract))
                steps(dve.tensor_tensor(ser[:], ser[:], small[:], ALU.mult))
                steps(dve.tensor_tensor(ser[:], ser[:], lg[:], ALU.add))
                steps(dve.tensor_tensor(dt[:], dt[:], ser[:], ALU.add))
                steps(dve.tensor_tensor(du[:], dt[:], cv[:], ALU.mult))
                dve.sem_inc(du_ready, 1)

                for n in range(DS):
                    m = g * DS + n
                    dve.wait_ge(bc_made, m + 1)
                    dve.tensor_tensor(dB[:, n % 2], du[:], ps[:, 2 + n % 2, 0:TC].unsqueeze(1).to_broadcast([P, KC, TC]),
                                      ALU.mult).then_inc(dB_ready, 1)
                    dve.wait_ge(dB_ready, m + 1 + 2)
                    dve.wait_ge(dA_ready, m + 2)
                    dve.wait_ge(hC_ready, m + 1)
                    for k in range(KC):
                        ins = dve.tensor_tensor_scan(hs[:, n % 2, k, :], dA[:, n % 2, k, :], dB[:, n % 2, k, :],
                                                     state[:, n, k:k + 1], ALU.mult, ALU.add)
                    ins.then_inc(scanned, 1)
                    dve.wait_ge(scanned, m + 1 + 2)
                    dve.tensor_copy(state[:, n, :], hs[:, n % 2, :, TC - 1])
                dve.wait_ge(y_added, g * DS + DS + 2)
                for k in range(KC):
                    steps(dve.scalar_tensor_tensor(y[:, k, :], cv[:, k, :], col[:, 2, k:k + 1], ps[:, k, 0:TC], ALU.mult, ALU.add))
                steps(dve.tensor_tensor(xT[:, :, bass.ds(g * TC, TC)], y[:], z[:], ALU.mult))
                assert steps.n == link.n + DVE_STEPS, steps.n - link.n
                dve.sem_inc(y_done, 1)


def local_and_global(nc, env, d, acc, x, other, top):
    with ExitStack() as ctx:
        rows = ctx.enter_context(nc.sbuf_tensor(fresh("l_rows"), [P, 5, D], F32))
        eps = ctx.enter_context(nc.sbuf_tensor(fresh("l_eps"), [P, NT, H1], F32))
        bound = ctx.enter_context(nc.sbuf_tensor(fresh("l_bound"), [P, NT, H1], F32))
        best = ctx.enter_context(nc.sbuf_tensor(fresh("l_best"), [P, 1], F32))
        load_all(nc, [(rows[:, n, :], d[name].partition_broadcast(P)) for n, name in
                      enumerate(["gat_b", "ln_local_g", "ln_local_b", "ln_global_g", "ln_global_b"])] +
                 [(bound[:], d["bound_tab"].rearrange("(t p) w -> p t w", p=P))])
        with ExitStack() as ctx2:
            chain_sem = ctx2.enter_context(nc.semaphore("l_chain"))
            spread = ctx2.enter_context(nc.semaphore("l_spread"))
            shifted = ctx2.enter_context(nc.semaphore("l_shifted"))
            exped = ctx2.enter_context(nc.semaphore("l_exped"))
            block = ctx2.enter_context(nc.Block())

            @block.gpsimd
            def _(pool):
                pool.partition_all_reduce(best[:], top[:, 0:1], P, bass.bass_isa.ReduceOp.max).then_inc(spread, 1)

            @block.vector
            def _(dve):
                link = Chain(dve, chain_sem)
                dve.wait_ge(spread, 1)
                dve.tensor_scalar(eps[:], bound[:], best[:], -1.0, ALU.subtract, ALU.mult).then_inc(shifted, 1)
                dve.wait_ge(exped, 1)
                link(dve.scalar_tensor_tensor(eps[:], eps[:], 1e-16, acc[:, :, D:PW], ALU.mult, ALU.add))
                link(dve.reciprocal(bound[:], eps[:]))
                for h in range(H1):
                    part = acc[:, :, h * HD1:(h + 1) * HD1]
                    ins = dve.tensor_tensor(part, part, bound[:, :, h:h + 1].to_broadcast([P, NT, HD1]), ALU.mult)
                link(ins)
                hl = acc[:, :, 0:D]
                link(dve.tensor_tensor(hl, hl, x[:], ALU.add))
                link(dve.tensor_tensor(hl, hl, rows[:, 0, :].unsqueeze(1).to_broadcast([P, NT, D]), ALU.add))
                dve.tensor_scalar(other[:], hl, 0.0, None, ALU.min).then_inc(shifted, 1)
                dve.wait_ge(exped, 2)
                link(dve.scalar_tensor_tensor(hl, hl, 0.0, other[:], ALU.max, ALU.add))
                link(dve.tensor_scalar(hl, hl, -1.0, None, ALU.add))

            @block.scalar
            def _(act):
                act.wait_ge(shifted, 1)
                act.activation(eps[:], eps[:], ACT.Exp).then_inc(exped, 1)
                act.wait_ge(shifted, 2)
                act.activation(other[:], other[:], ACT.Exp).then_inc(exped, 1)
        layernorm(nc, acc[:, :, 0:D], acc[:, :, 0:D], other[:], rows[:, 1, :], rows[:, 2, :])
        move_rows(nc, env, env["rank"], d["y_tab"], other, True)
        with nc.semaphore("l_add") as added, nc.Block() as block:
            @block.vector
            def _(dve):
                dve.tensor_tensor(other[:], other[:], x[:], ALU.add).then_inc(added, 1)
                dve.wait_ge(added, 1)
        layernorm(nc, other[:], other[:], x[:], rows[:, 3, :], rows[:, 4, :])


def gate_and_mix(nc, env, d, acc, gate, other):
    with ExitStack() as ctx:
        w = ctx.enter_context(nc.sbuf_tensor(fresh("i_w"), [P, 2, KC, D], F32))
        load_all(nc, [(w[:, n], d[name].rearrange("(k p) m -> p k m", p=P)) for n, name in enumerate(("wlT", "wgT"))])
        project_tiles(nc, acc[:, :, 0:D], w[:, 0], env["ident"],
                      lambda dve, out, t: dve.tensor_copy(tile(gate, t), out[:, 0:D]))
        project_tiles(nc, other, w[:, 1], env["ident"],
                      lambda dve, out, t: dve.tensor_tensor(tile(gate, t), tile(gate, t), out[:, 0:D], ALU.add))
        with ExitStack() as ctx2:
            chain_sem = ctx2.enter_context(nc.semaphore("i_chain"))
            opened = ctx2.enter_context(nc.semaphore("i_opened"))
            block = ctx2.enter_context(nc.Block())

            @block.scalar
            def _(act):
                act.activation(gate[:], gate[:], ACT.Sigmoid).then_inc(opened, 1)

            @block.vector
            def _(dve):
                link = Chain(dve, chain_sem)
                hl = acc[:, :, 0:D]
                link(dve.tensor_tensor(hl, hl, other[:], ALU.subtract))
                dve.wait_ge(opened, 1)
                link(dve.tensor_tensor(hl, hl, gate[:], ALU.mult))
                link(dve.tensor_tensor(other[:], other[:], hl, ALU.add))




INTERNAL = [("q_tab", [NP, D], F32), ("k_tab", [NP, D], F32), ("v_tab", [NP, D], F32),
            ("h_tab", [NP, RW], F32), ("d_tab", [NP, 2 * HR], F32), ("x1_tab", [NP, D], F32), ("x1n_tab", [NP, D], F32), ("x2_tab", [NP, D], F32),
            ("x2n_tab", [NP, D], F32), ("proj_tab", [NP, PW], F32), ("bound_tab", [NP, H1], F32), ("key_line", [NP], F32),
            ("xs_tab", [NP, D], F32), ("y_tab", [NP, D], F32), ("agg_tab", [NP, PW], F32), ("x3_tab", [NP, D], F32)]


def flat_nodes(acc):
    return acc[:].rearrange("p t w -> p (t w)")[:, 0:NT * D].rearrange("p (t w) -> p t w", w=D)


def fill(nc, buf, value):
    with nc.semaphore("fill") as filled, nc.Block() as block:
        @block.vector
        def _(dve):
            dve.memset(buf[:], value).then_inc(filled, 1)
            dve.wait_ge(filled, 1)


def reset_semaphores(nc):
    free = sorted(nc.free_semaphores)
    with nc.Block() as block:
        @block.gpsimd
        def _(pool):
            start = free[0]
            for n, sem in enumerate(free):
                if n + 1 == len(free) or free[n + 1] != sem + 1:
                    pool.dma_reset(range(start, sem + 1))
                    pool.sem_clear(range(start, sem + 1))
                    start = free[n + 1] if n + 1 < len(free) else sem


def edge_tables(nc, env, d, keep, stack):
    for name, shape, dt in [("src", [P, ETX], I32), ("dst", [P, ETX], F32), ("base", [P, SL], F32), ("steps", [P, 2 * SL], I32)]:
        env[name] = keep(fresh(name), shape, dt, stack)
    env["step_b"], env["tile_pairs"], env["block_pairs"], env["block_fours"] = (
        env["steps"][0:1, 0:SL], env["steps"][32:33, :], env["steps"][64:65, :], env["steps"][96:97, :])
    walk(nc, env, d)
    reset_semaphores(nc)


def program(nc, d):
    NAMES.clear()
    for name, shape, dt in INTERNAL:
        d[name] = nc.dram_tensor(name, shape, dt, kind="Internal").ap()
    with ExitStack() as ctx:
        def keep(name, shape, dt=F32, stack=ctx):
            return stack.enter_context(nc.sbuf_tensor(name, shape, dt))
        ident = keep("ident", [P, P])
        iota = keep("iota", [P, P])
        env = {"ident": ident, "iota": iota}
        constants(nc, ident, iota)
        phase_qkv(nc, env, d)
        reset_semaphores(nc)
        gates = keep("gates", [P, NT, NE])
        ones = keep("ones", [P, NT, 1])
        top = keep("top", [P, 1])
        env["rank"] = keep("rank", [P, NT], I32)
        key = keep("key", [P, NT])
        edges = ExitStack()
        edge_tables(nc, env, d, keep, edges)
        with ExitStack() as first:
            h20 = keep("h20", [P, NT, RW], stack=first)
            dtab = keep("dtab", [P, NT, 2 * HR], stack=first)
            routing = ExitStack()
            with nc.sbuf_tensor("logits", [P, LW + 2 * H0], F32) as logits:
                load_all(nc, [(logits[:, 0:LW], d["bias_cols"].rearrange("p t h -> p (t h)"))])
                with nc.sbuf_tensor("q", [P, NT, D], F32) as q:
                    load_all(nc, [(q[:], rows_of(d["q_tab"]))])
                    edge_logits(nc, env, d, logits, q)
                segment_exp(nc, env, d, logits)
                acc = first.enter_context(nc.sbuf_tensor("acc", [P, NT, D + H0], F32, side="right"))
                edge_sums(nc, env, d, logits, acc)
            x = keep("x1", [P, NT, D], stack=routing)
            x1n = keep("x1n", [P, NT, D], stack=routing)
            reset_semaphores(nc)
            finish_attention(nc, env, d, acc, x, x1n)
            layernorm(nc, x[:], x1n[:], flat_nodes(acc))
            store_nodes(nc, [(d["x1_tab"], x), (d["x1n_tab"], x1n)])
            routing_tables(nc, env, d, x1n, h20, dtab)
            routing.close()
            sums = keep("sums", [P, NT, RW], stack=first)
            routing_sums(nc, env, d, sums, key)
            routing_gates(nc, env, d, h20, dtab, sums, gates[:, :, 0:NX])
        reset_semaphores(nc)
        edges.close()
        with ExitStack() as ffn:
            xT = keep("x1nT", [P, KC, NP], stack=ffn)
            with nc.sbuf_tensor("x1n_again", [P, NT, D], F32, side="right") as x1n:
                load_all(nc, [(x1n[:], rows_of(d["x1n_tab"]))])
                project_tiles(nc, x1n, None, ident, None, xT=xT)
            w1 = keep("f0_w1", [P, KC, NX * FH], stack=ffn)
            b1 = keep("f0_b1", [P, NX * FH // P], stack=ffn)
            w2 = keep("f0_w2", [P, NX * FH // P, D], stack=ffn)
            b2 = keep("f0_b2", [P, NX, D], stack=ffn)
            load_all(nc, [(w1[:], d["w1_0"].rearrange("(k p) m -> p k m", p=P)), (b1[:], d["b1_0"]),
                          (w2[:], d["w2_0"].rearrange("(c p) m -> p c m", p=P)),
                          (b2[:].rearrange("p e m -> p (e m)"), d["b2_0"].partition_broadcast(P))])
            x = keep("x1_group", [P, U, D], stack=ffn)
            keys = keep("k_keys", [P, NP], stack=ffn)
            earlier = keep("k_earlier", [P, 2 * NP], BF16, stack=ffn)
            trash = keep("k_trash", [P, 2, NP], BF16, stack=ffn)
            part = keep("k_part", [P, 2, NT], stack=ffn)
            rank_tables(nc, env, d, key, keys, earlier)
            expert_ffn(nc, xT, gates, x, w1, b1, w2, b2, NX, False, stream=(d["x1_tab"], d["x2_tab"]),
                       count=(key, keys, earlier, trash, part))
            ranks(nc, part, env["rank"])
        edges = ExitStack()
        edge_tables(nc, env, d, keep, edges)
        reset_semaphores(nc)
        with ExitStack() as second:
            reset_semaphores(nc)
            tgt = keep("tgt", [P, NT, TW], stack=second)
            with nc.sbuf_tensor("x2", [P, NT, D], F32) as x, nc.sbuf_tensor("x2n", [P, NT, D], F32) as x2n:
                load_all(nc, [(x[:], rows_of(d["x2_tab"]))])
                with nc.sbuf_tensor("x2sq", [P, NT, D], F32) as squares:
                    layernorm(nc, x[:], x2n[:], squares[:])
                store_nodes(nc, [(d["x2n_tab"], x2n)])
                move_rows(nc, env, env["rank"], d["xs_tab"], x2n, False)
                with nc.sbuf_tensor("proj", [P, NT, PW], F32) as proj:
                    attention_tables(nc, env, d, x2n, proj, tgt)
            reset_semaphores(nc)
            store_nodes(nc, [(d["bound_tab"], tgt[:, :, H1:2 * H1])])
            acc = keep("acc1", [P, NT, PW], stack=second)
            second_attention(nc, env, d, tgt, acc, top)
            store_nodes(nc, [(d["agg_tab"], acc)])
        edges.close()
        reset_semaphores(nc)
        with ExitStack() as scan:
            xT = keep("xsT", [P, KC, NP], stack=scan)
            with nc.sbuf_tensor("xs", [P, NT, D], F32) as xs:
                load_all(nc, [(xs[:], rows_of(d["xs_tab"]))])
                project_tiles(nc, xs, None, ident, None, xT=xT)
            reset_semaphores(nc)
            mamba(nc, env, d, xT)
            w = keep("out_w", [P, KC, D], stack=scan)
            y = keep("y", [P, NT, D], stack=scan)
            load_all(nc, [(w[:], d["out_wT"].rearrange("(k p) m -> p k m", p=P))])
            project_tiles(nc, None, w, ident, lambda dve, out, t: dve.tensor_copy(tile(y, t), out[:, 0:D]), turned_src=xT)
            store_nodes(nc, [(d["y_tab"], y)])
        reset_semaphores(nc)
        with ExitStack() as last:
            a = keep("buf_a", [P, NT, PW], stack=last)
            b = keep("buf_b", [P, NT, D], stack=last)
            c = keep("buf_c", [P, NT, D], stack=last)
            b_turned = b[:].rearrange("p t d -> p (t d)").rearrange("p (k n) -> p k n", k=KC)
            load_all(nc, [(a[:], rows_of(d["agg_tab"])), (b[:], rows_of(d["x2n_tab"]))])
            local_and_global(nc, env, d, a, b, c, top)
            reset_semaphores(nc)
            gate_and_mix(nc, env, d, a, b, c)
            with ExitStack() as ffn:
                w1 = keep("f1_w1", [P, KC, 2 * D], stack=ffn)
                b1 = keep("f1_b1", [P, 2 * D // P], stack=ffn)
                w2 = keep("f1_w2", [P, 2 * D // P, D], stack=ffn)
                b2 = keep("f1_b2", [P, 1, D], stack=ffn)
                load_all(nc, [(w1[:], d["ff1_T"].rearrange("(k p) m -> p k m", p=P)), (b1[:], d["ff1_b"]),
                              (w2[:], d["ff2_T"].rearrange("(c p) m -> p c m", p=P)),
                              (b2[:, 0, :], d["ff2_b"].partition_broadcast(P))])
                fill(nc, ones, 1.0)
                project_tiles(nc, c, None, ident, None, xT=b_turned)
                expert_ffn(nc, b_turned, ones, c, w1, b1, w2, b2, 1, True, func=ACT.Relu)
            reset_semaphores(nc)
            rows = keep("ln2_rows", [P, 2, D], stack=last)
            load_all(nc, [(rows[:, n, :], d[name].partition_broadcast(P)) for n, name in enumerate(("ln2_g", "ln2_b"))])
            layernorm(nc, c[:], c[:], b[:], rows[:, 0, :], rows[:, 1, :])
            load_all(nc, [(b[:], rows_of(d["x2_tab"]))])
            with nc.semaphore("x3_add") as added, nc.Block() as block:
                @block.vector
                def _(dve):
                    dve.tensor_tensor(c[:], c[:], b[:], ALU.add).then_inc(added, 1)
                    dve.wait_ge(added, 1)
            store_nodes(nc, [(d["x3_tab"], c)])
        with ExitStack() as last:
            xT = keep("x3T", [P, KC, NP], stack=last)
            with nc.sbuf_tensor("x3", [P, NT, D], F32) as x, nc.sbuf_tensor("x3n", [P, NT, D], F32) as x3n:
                load_all(nc, [(x[:], rows_of(d["x3_tab"]))])
                layernorm(nc, x[:], x3n[:], xT[:].rearrange("p k n -> p (k n)").rearrange("p (t w) -> p t w", w=D))
                project_tiles(nc, x3n, None, ident, None, xT=xT)
            reset_semaphores(nc)
            w1 = keep("f2_w1", [P, KC, HID], stack=last)
            b1 = keep("f2_b1", [P, HID // P], stack=last)
            wg = keep("f2_wg", [P, HID // P, NE], stack=last)
            bg = keep("f2_bg", [P, NE], stack=last)
            b2 = keep("f2_b2", [P, NE, D], stack=last)
            countdown = keep("f2_count", [P, U * NE], stack=last)
            load_all(nc, [(w1[:], d["w1_1"].rearrange("(k p) m -> p k m", p=P)), (b1[:], d["b1_1"]),
                          (wg[:], d["wg_1"].rearrange("(c p) m -> p c m", p=P)), (bg[:], d["bg_1"].partition_broadcast(P)),
                          (b2[:].rearrange("p e m -> p (e m)"), d["bd_1"].partition_broadcast(P))])
            with nc.semaphore("countdown") as made, nc.Block() as block:
                @block.gpsimd
                def _(pool):
                    pool.iota(countdown[:], pattern=[[0, U], [-1, NE]], base=NE, channel_multiplier=0,
                              allow_small_or_imprecise_dtypes=True).then_inc(made, 1)
                    pool.wait_ge(made, 1)
            w2 = keep("f2_wd", [P, NE * HID // P, D], stack=last)
            load_all(nc, [(w2[:], d["wd_1"].rearrange("(c p) m -> p c m", p=P))])
            x = keep("x3_group", [P, U, D], stack=last)
            expert_ffn(nc, xT, gates, x, w1, b1, w2, b2, NE, True, route=(wg[:], bg[:], countdown[:]),
                       stream=(d["x3_tab"], d["out"]))


def edge_columns(a, pad, tiles=ETX):
    full = np.full((tiles * P,) + a.shape[1:], pad, a.dtype)
    full[:E] = a
    return np.ascontiguousarray(np.swapaxes(full.reshape((tiles, P) + a.shape[1:]), 0, 1))


def routing_columns(e):
    full = np.zeros((2, ET2 + HALVES * BT, P), e.dtype)
    full[:, :ET2] = e.reshape(2, ET2, P)
    return np.ascontiguousarray(full.transpose(2, 1, 0))


def node_columns(a, pad):
    full = np.full(NP, pad, a.dtype)
    full[:N] = a
    return np.ascontiguousarray(full.reshape(NT, P).T)


def T(a):
    return np.ascontiguousarray(a.T)


def layout(i):
    i = {k: np.asarray(v) for k, v in i.items()}
    dst = i["dst"]
    linear = np.full(ET * P + 2, PAD_DST, dst.dtype)
    linear[0] = PAD_DST
    linear[1:E + 1] = dst
    return {
        "x": i["x"],
        "wqkvT": np.ascontiguousarray(np.concatenate([i["L0_gnn_Wq"].T, i["L0_gnn_Wk"].T, i["L0_gnn_Wv"].T], 1)),
        "woT": np.ascontiguousarray(i["L0_gnn_Wo"].T),
        "tile_last": edge_columns(dst, PAD_DST)[P - 1].copy(),
        "src_cols": edge_columns(i["src"], NP - 1),
        "dst_cols": edge_columns(dst, PAD_DST),
        "bias_cols": edge_columns(i["edge_attr_8"], 0, ET),
        "dst_line": linear,
        "ends2": routing_columns(i["L0_ffn_edge_index"]),
        "w_gat": i["L0_ffn_W_gat"],
        "att_src": i["L0_ffn_att_src"].reshape(-1),
        "att_dst": i["L0_ffn_att_dst"].reshape(-1),
        "b_gat": i["L0_ffn_b_gat"],
        "ln_gamma": i["L0_ffn_ln_gamma"],
        "ln_beta": i["L0_ffn_ln_beta"],
        "w1_0": np.ascontiguousarray(i["L0_ffn_W1"].transpose(1, 0, 2).reshape(D, NX * FH)),
        "b1_0": np.ascontiguousarray(i["L0_ffn_b1"].reshape(NX * FH // P, P).T),
        "w2_0": i["L0_ffn_W2"].reshape(NX * FH, D),
        "b2_0": i["L0_ffn_b2"].reshape(-1),
        "noise_cols": node_columns(i["node_vec"], 3e38),
        "gat_wT": T(i["L1_gnn_gat_w"]),
        "gat_a_src": i["L1_gnn_gat_a_src"].reshape(-1),
        "gat_a_tgt": i["L1_gnn_gat_a_tgt"].reshape(-1),
        "gat_b": i["L1_gnn_gat_b"],
        "ln_local_g": i["L1_gnn_ln_local_g"],
        "ln_local_b": i["L1_gnn_ln_local_b"],
        "ln_global_g": i["L1_gnn_ln_global_g"],
        "ln_global_b": i["L1_gnn_ln_global_b"],
        "ln2_g": i["L1_gnn_ln2_g"],
        "ln2_b": i["L1_gnn_ln2_b"],
        "in_wT": T(i["L1_gnn_in_proj_w"]),
        "x_wT": T(i["L1_gnn_x_proj_w"]),
        "dt_wT": T(i["L1_gnn_dt_proj_w"]),
        "out_wT": T(i["L1_gnn_out_proj_w"]),
        "conv_w": i["L1_gnn_conv_w"],
        "conv_b": T(i["L1_gnn_conv_b"].reshape(KC, P)),
        "dt_b": T(i["L1_gnn_dt_proj_b"].reshape(KC, P)),
        "A_log": i["L1_gnn_A_log"],
        "D_param": T(i["L1_gnn_D_param"].reshape(KC, P)),
        "wlT": T(i["L1_gnn_wl"]),
        "wgT": T(i["L1_gnn_wg"]),
        "ff1_T": T(i["L1_gnn_ff1_w"]),
        "ff1_b": T(i["L1_gnn_ff1_b"].reshape(-1, P)),
        "ff2_T": T(i["L1_gnn_ff2_w"]),
        "ff2_b": i["L1_gnn_ff2_b"],
        "w1_1": i["L1_ffn_W1"],
        "b1_1": T(i["L1_ffn_b1"].reshape(-1, P)),
        "wg_1": i["L1_ffn_Wg"],
        "bg_1": i["L1_ffn_bg"],
        "wd_1": i["L1_ffn_Wd"].reshape(NE * HID, D),
        "bd_1": i["L1_ffn_bd"].reshape(-1),
    }


OUT_SHAPE = (NP, D)


def kernel(**inputs):
    import concourse.bacc as _bacc
    from concourse.bass_utils import run_bass_kernel_spmd as _run

    nc = _bacc.Bacc("TRN2", target_bir_lowering=False, num_devices=1)
    arrays = layout(inputs)
    d = {n: nc.dram_tensor(n, a.shape, mybir.dt.from_np(a.dtype), kind="ExternalInput").ap()
         for n, a in arrays.items()}
    d["out"] = nc.dram_tensor("out", OUT_SHAPE, F32, kind="ExternalOutput").ap()
    program(nc, d)
    r = _run(nc, [arrays], core_ids=[0])
    return r.results[0]["out"][:N]
```
